# Optimizing a Trainium2 kernel written in Bass

```python
import numpy as np
import jax
import jax.numpy as jnp

def _softmax(x, axis=-1):
    return jax.nn.softmax(x, axis=axis)

def _gelu(x):
    return jax.nn.gelu(x, approximate=True)

def _silu(x):
    return jax.nn.silu(x)

def _sigmoid(x):
    return jax.nn.sigmoid(x)

def _layernorm(x, axis=-1, eps=1e-05):
    m = jnp.mean(x, axis=axis, keepdims=True)
    v = jnp.var(x, axis=axis, keepdims=True)
    return (x - m) / jnp.sqrt(v + eps)

def _scatter_add(tgt, idx, src, axis=0):
    return tgt.at[idx].add(src)

def _segment_sum(src, seg, n):
    return jax.ops.segment_sum(src, seg, n)
kernel_name = 'mk_prb_d4_jaxref_r8_e5c495'

def setup_inputs(seed: int=0):
    np.random.seed(seed)
    _w = jnp.asarray

    def _L0_attn_setup():
        import jax, jax.numpy as jnp
        import numpy as np
        B, N, D = (8, 128, 512)
        H = 8
        HEAD_DIM = D // H
        E = HEAD_DIM // H
        key = jax.random.key(seed)
        ks = jax.random.split(key, 7)
        s = 0.02
        return {'x': jax.random.normal(ks[0], (B, N, D), dtype=jnp.float32), 'Wqk_w': jax.random.normal(ks[1], (2 * HEAD_DIM, D), dtype=jnp.float32) * s, 'Wqk_b': jnp.zeros((2 * HEAD_DIM,), dtype=jnp.float32), 'Wv_w': jax.random.normal(ks[2], (HEAD_DIM, D), dtype=jnp.float32) * s, 'Wv_b': jnp.zeros((HEAD_DIM,), dtype=jnp.float32), 'Wo_w': jax.random.normal(ks[3], (D, HEAD_DIM), dtype=jnp.float32) * s, 'Wo_b': jnp.zeros((D,), dtype=jnp.float32)}
    _L0_attn_in = _L0_attn_setup()

    def _L0_ffn_setup():
        import jax, jax.numpy as jnp
        import numpy as np
        LORA_RANK = 16
        LORA_ALPHA = 16
        LORA_SCALE = LORA_ALPHA / LORA_RANK
        key = jax.random.key(seed)
        k1, k2, k3, k4, k5 = jax.random.split(key, 5)
        B, S, D_IN, D_OUT, N_LORA, R = (8, 256, 512, 512, 3, LORA_RANK)
        std = 1.0 / np.sqrt(D_IN)
        x = jax.random.normal(k1, (B, S, D_IN), dtype=jnp.float32)
        weight = jax.random.truncated_normal(k2, -3.0, 3.0, (D_OUT, D_IN), dtype=jnp.float32) * std
        bias = jax.random.normal(k3, (D_OUT,), dtype=jnp.float32) * 0.01
        lora_A = jax.random.normal(k4, (N_LORA, R, D_IN), dtype=jnp.float32) * std
        lora_B = jax.random.normal(k5, (N_LORA, D_OUT, R), dtype=jnp.float32) * 0.02
        lora_start_indices = jnp.arange(4, dtype=jnp.int64) * 2
        return {'x': x, 'weight': weight, 'bias': bias, 'lora_A': lora_A, 'lora_B': lora_B, 'lora_start_indices': lora_start_indices}
    _L0_ffn_in = _L0_ffn_setup()

    def _L1_attn_setup():
        import jax, jax.numpy as jnp
        import numpy as np
        import math
        B, S, D = (1, 256, 512)
        H, KV, HD = (32, 8, 128)
        GROUPS = H // KV
        SYS_LEN, IMG_LEN = (35, 72)
        ENH, SUP = (1.5, 0.5)
        ROPE_BASE = 10000.0

        def _rope_cos_sin(seq_len, dtype):
            inv_freq = 1.0 / ROPE_BASE ** (jnp.arange(0, HD, 2, dtype=jnp.float32) / HD)
            pos = jnp.arange(seq_len, dtype=jnp.float32)
            freqs = pos[:, None] * inv_freq[None, :]
            emb = jnp.concatenate([freqs, freqs], axis=-1)
            return (jnp.cos(emb).astype(dtype), jnp.sin(emb).astype(dtype))

        def _rotate_half(x):
            x1, x2 = (x[..., :HD // 2], x[..., HD // 2:])
            return jnp.concatenate([-x2, x1], axis=-1)
        key = jax.random.key(seed)
        ks = jax.random.split(key, 5)
        scale = 0.02
        return {'hidden_states': jax.random.normal(ks[0], (B, S, D), dtype=jnp.float32), 'wq': jax.random.normal(ks[1], (H * HD, D), dtype=jnp.float32) * scale, 'wk': jax.random.normal(ks[2], (KV * HD, D), dtype=jnp.float32) * scale, 'wv': jax.random.normal(ks[3], (KV * HD, D), dtype=jnp.float32) * scale, 'wo': jax.random.normal(ks[4], (D, H * HD), dtype=jnp.float32) * scale}
    _L1_attn_in = _L1_attn_setup()

    def _L1_ffn_setup():
        import jax, jax.numpy as jnp
        import numpy as np
        DIM = 512
        INTER = 128
        E = 16
        GROUPS = 4
        LIM = 2
        K = 2
        SHARED_INTER = 2 * INTER
        SCALE = 1.0
        key = jax.random.key(seed)
        ks = jax.random.split(key, 16)

        def n(k, shape, s=0.02):
            return jax.random.normal(k, shape, jnp.float32) * s
        return {'x': jax.random.normal(ks[0], (1, 256, DIM), jnp.float32), 'router_w': n(ks[1], (DIM, E)), 'router_b': n(ks[2], (E,)), 'router_bias': n(ks[3], (E,), 1.0), 'ew1': n(ks[4], (E, DIM, INTER)), 'eb1': n(ks[5], (E, INTER)), 'ew2': n(ks[6], (E, DIM, INTER)), 'eb2': n(ks[7], (E, INTER)), 'ew3': n(ks[8], (E, INTER, DIM)), 'eb3': n(ks[9], (E, DIM)), 'sw1': n(ks[10], (DIM, SHARED_INTER)), 'sb1': n(ks[11], (SHARED_INTER,)), 'sw2': n(ks[12], (DIM, SHARED_INTER)), 'sb2': n(ks[13], (SHARED_INTER,)), 'sw3': n(ks[14], (SHARED_INTER, DIM)), 'sb3': n(ks[15], (DIM,))}
    _L1_ffn_in = _L1_ffn_setup()

    def _L2_attn_setup():
        import math
        import jax, jax.numpy as jnp
        import numpy as np
        B, T, E = (2, 256, 512)
        H, HKV = (32, 8)
        DH = E // H
        G = H // HKV
        ROPE_THETA = 500000.0
        ROPE_FACTOR = 32.0
        HI_FREQ_FACTOR = 4.0
        LO_FREQ_FACTOR = 1.0
        ORIG_CTX = 1024

        def _rope_cos_sin(t_len):
            inv_freq = 1.0 / ROPE_THETA ** (jnp.arange(0, DH, 2, dtype=jnp.float32) / DH)
            wavelen = 2.0 * math.pi / inv_freq
            cut_lo = ORIG_CTX / HI_FREQ_FACTOR
            cut_hi = ORIG_CTX / LO_FREQ_FACTOR
            inv_freq = jnp.where(wavelen > cut_hi, inv_freq / ROPE_FACTOR, inv_freq)
            smooth = (ORIG_CTX / wavelen - LO_FREQ_FACTOR) / (HI_FREQ_FACTOR - LO_FREQ_FACTOR)
            smoothed = (1.0 - smooth) * inv_freq / ROPE_FACTOR + smooth * inv_freq
            is_medium = ~(wavelen < cut_hi) & ~(wavelen > cut_lo)
            inv_freq = jnp.where(is_medium, smoothed, inv_freq)
            pos = jnp.arange(t_len, dtype=jnp.float32)
            freqs = pos[:, None] * inv_freq[None, :]
            emb = jnp.concatenate([freqs, freqs], axis=-1)
            return (jnp.cos(emb), jnp.sin(emb))

        def _rotate_half(x):
            x1, x2 = jnp.split(x, 2, axis=-1)
            return jnp.concatenate([-x2, x1], axis=-1)
        key = jax.random.key(seed)
        kx, kq, kk, kv, ko = jax.random.split(key, 5)
        w = lambda k, shape: jax.random.normal(k, shape, jnp.float32) * 0.02
        return {'x': jax.random.normal(kx, (B, T, E), jnp.float32), 'Wq': w(kq, (E, E)), 'Wk': w(kk, (HKV * DH, E)), 'Wv': w(kv, (HKV * DH, E)), 'Wo': w(ko, (E, E))}
    _L2_attn_in = _L2_attn_setup()

    def _L2_ffn_setup():
        import jax, jax.numpy as jnp
        import numpy as np
        HID, BOT, RDIM, NSLOT, K, VB = (512, 64, 48, 128, 8, 32)
        TAU_LOW, TAU_HIGH, EARLY_EXIT = (0.5, 2.0, 0.05)

        def _uncertainty(h, Wu1, bu1, Wu2, bu2):
            var = jnp.var(h, axis=-1)
            log_var = jnp.log1p(var)
            norm_var = log_var / (jnp.mean(log_var) + 1e-06)
            learned = (jax.nn.gelu(h @ Wu1.T + bu1) @ Wu2.T + bu2)[..., 0]
            return jnp.clip(norm_var * 0.5 + jax.nn.sigmoid(learned) * 2.5, 0.0, 5.0)
        key = jax.random.key(seed)
        ks = jax.random.split(key, 12)
        B, S = (2, 256)
        return {'hidden_states': jax.random.normal(ks[0], (B, S, HID), dtype=jnp.float32), 'Wq': jax.random.normal(ks[1], (BOT, HID), dtype=jnp.float32) / np.sqrt(HID), 'Wr': jax.random.normal(ks[2], (RDIM, BOT), dtype=jnp.float32) / np.sqrt(BOT), 'aux_keys': jax.random.normal(ks[3], (NSLOT, BOT), dtype=jnp.float32) * 0.01, 'aux_values': jax.random.normal(ks[4], (NSLOT, HID), dtype=jnp.float32) * 0.02, 'Wvd': jax.random.normal(ks[5], (VB, HID), dtype=jnp.float32) * 0.1 / np.sqrt(HID), 'Wvu': jax.random.normal(ks[6], (HID, VB), dtype=jnp.float32) * 0.1 / np.sqrt(VB), 'Wu1': jax.random.normal(ks[7], (HID // 4, HID), dtype=jnp.float32) / np.sqrt(HID), 'bu1': jnp.zeros((HID // 4,), dtype=jnp.float32), 'Wu2': jax.random.normal(ks[8], (1, HID // 4), dtype=jnp.float32) * 0.01, 'bu2': jnp.zeros((1,), dtype=jnp.float32), 'gate_w1': jnp.float32(0.5), 'gate_bias': jnp.float32(-1.0), 'log_rel': jnp.zeros((NSLOT,), dtype=jnp.float32)}
    _L2_ffn_in = _L2_ffn_setup()

    def _L3_attn_setup():
        import jax, jax.numpy as jnp
        import numpy as np
        H, KV, HD, HID = (32, 8, 128, 512)
        THETA, FACTOR, HI_FF, LO_FF, ORIG_MAX = (500000.0, 8.0, 4.0, 1.0, 1024)

        def _llama3_inv_freq():
            inv = 1.0 / THETA ** (np.arange(0, HD, 2, dtype=np.float64) / HD)
            wavelen = 2.0 * np.pi / inv
            low_wl = ORIG_MAX / LO_FF
            high_wl = ORIG_MAX / HI_FF
            smooth = (ORIG_MAX / wavelen - LO_FF) / (HI_FF - LO_FF)
            scaled = np.where(wavelen > low_wl, inv / FACTOR, inv)
            mid = (wavelen <= low_wl) & (wavelen >= high_wl)
            scaled = np.where(mid, (1 - smooth) * inv / FACTOR + smooth * inv, scaled)
            return scaled.astype(np.float32)

        def _rope_cos_sin(T):
            inv = _llama3_inv_freq()
            pos = np.arange(T, dtype=np.float32)
            freqs = pos[:, None] * inv[None, :]
            emb = np.concatenate([freqs, freqs], axis=-1)
            return (jnp.asarray(np.cos(emb)), jnp.asarray(np.sin(emb)))

        def _rotate_half(x):
            x1, x2 = jnp.split(x, 2, axis=-1)
            return jnp.concatenate([-x2, x1], axis=-1)
        key = jax.random.key(seed)
        ks = jax.random.split(key, 5)
        s = 1.0 / np.sqrt(HID)
        return {'x': jax.random.normal(ks[0], (1, 256, HID), jnp.float32), 'wq': jax.random.normal(ks[1], (HID, H * HD), jnp.float32) * s, 'wk': jax.random.normal(ks[2], (HID, KV * HD), jnp.float32) * s, 'wv': jax.random.normal(ks[3], (HID, KV * HD), jnp.float32) * s, 'wo': jax.random.normal(ks[4], (H * HD, HID), jnp.float32) * s}
    _L3_attn_in = _L3_attn_setup()

    def _L3_ffn_setup():
        import jax, jax.numpy as jnp
        import numpy as np
        HID, BOT, RDIM, NSLOT, K, VB = (512, 64, 48, 128, 8, 32)
        TAU_LOW, TAU_HIGH, EARLY_EXIT = (0.5, 2.0, 0.05)

        def _uncertainty(h, Wu1, bu1, Wu2, bu2):
            var = jnp.var(h, axis=-1)
            log_var = jnp.log1p(var)
            norm_var = log_var / (jnp.mean(log_var) + 1e-06)
            learned = (jax.nn.gelu(h @ Wu1.T + bu1) @ Wu2.T + bu2)[..., 0]
            return jnp.clip(norm_var * 0.5 + jax.nn.sigmoid(learned) * 2.5, 0.0, 5.0)
        key = jax.random.key(seed)
        ks = jax.random.split(key, 12)
        B, S = (2, 256)
        return {'hidden_states': jax.random.normal(ks[0], (B, S, HID), dtype=jnp.float32), 'Wq': jax.random.normal(ks[1], (BOT, HID), dtype=jnp.float32) / np.sqrt(HID), 'Wr': jax.random.normal(ks[2], (RDIM, BOT), dtype=jnp.float32) / np.sqrt(BOT), 'aux_keys': jax.random.normal(ks[3], (NSLOT, BOT), dtype=jnp.float32) * 0.01, 'aux_values': jax.random.normal(ks[4], (NSLOT, HID), dtype=jnp.float32) * 0.02, 'Wvd': jax.random.normal(ks[5], (VB, HID), dtype=jnp.float32) * 0.1 / np.sqrt(HID), 'Wvu': jax.random.normal(ks[6], (HID, VB), dtype=jnp.float32) * 0.1 / np.sqrt(VB), 'Wu1': jax.random.normal(ks[7], (HID // 4, HID), dtype=jnp.float32) / np.sqrt(HID), 'bu1': jnp.zeros((HID // 4,), dtype=jnp.float32), 'Wu2': jax.random.normal(ks[8], (1, HID // 4), dtype=jnp.float32) * 0.01, 'bu2': jnp.zeros((1,), dtype=jnp.float32), 'gate_w1': jnp.float32(0.5), 'gate_bias': jnp.float32(-1.0), 'log_rel': jnp.zeros((NSLOT,), dtype=jnp.float32)}
    _L3_ffn_in = _L3_ffn_setup()
    _d = {'L0_attn_x': _L0_attn_in['x'], 'L0_attn_Wqk_w': _L0_attn_in['Wqk_w'], 'L0_attn_Wqk_b': _L0_attn_in['Wqk_b'], 'L0_attn_Wv_w': _L0_attn_in['Wv_w'], 'L0_attn_Wv_b': _L0_attn_in['Wv_b'], 'L0_attn_Wo_w': _L0_attn_in['Wo_w'], 'L0_attn_Wo_b': _L0_attn_in['Wo_b'], 'L0_ffn_weight': _L0_ffn_in['weight'], 'L0_ffn_bias': _L0_ffn_in['bias'], 'L0_ffn_lora_A': _L0_ffn_in['lora_A'], 'L0_ffn_lora_B': _L0_ffn_in['lora_B'], 'L0_ffn_lora_start_indices': _L0_ffn_in['lora_start_indices'], 'L1_attn_wq': _L1_attn_in['wq'], 'L1_attn_wk': _L1_attn_in['wk'], 'L1_attn_wv': _L1_attn_in['wv'], 'L1_attn_wo': _L1_attn_in['wo'], 'L1_ffn_router_w': _L1_ffn_in['router_w'], 'L1_ffn_router_b': _L1_ffn_in['router_b'], 'L1_ffn_router_bias': _L1_ffn_in['router_bias'], 'L1_ffn_ew1': _L1_ffn_in['ew1'], 'L1_ffn_eb1': _L1_ffn_in['eb1'], 'L1_ffn_ew2': _L1_ffn_in['ew2'], 'L1_ffn_eb2': _L1_ffn_in['eb2'], 'L1_ffn_ew3': _L1_ffn_in['ew3'], 'L1_ffn_eb3': _L1_ffn_in['eb3'], 'L1_ffn_sw1': _L1_ffn_in['sw1'], 'L1_ffn_sb1': _L1_ffn_in['sb1'], 'L1_ffn_sw2': _L1_ffn_in['sw2'], 'L1_ffn_sb2': _L1_ffn_in['sb2'], 'L1_ffn_sw3': _L1_ffn_in['sw3'], 'L1_ffn_sb3': _L1_ffn_in['sb3'], 'L2_attn_Wq': _L2_attn_in['Wq'], 'L2_attn_Wk': _L2_attn_in['Wk'], 'L2_attn_Wv': _L2_attn_in['Wv'], 'L2_attn_Wo': _L2_attn_in['Wo'], 'L2_ffn_Wq': _L2_ffn_in['Wq'], 'L2_ffn_Wr': _L2_ffn_in['Wr'], 'L2_ffn_aux_keys': _L2_ffn_in['aux_keys'], 'L2_ffn_aux_values': _L2_ffn_in['aux_values'], 'L2_ffn_Wvd': _L2_ffn_in['Wvd'], 'L2_ffn_Wvu': _L2_ffn_in['Wvu'], 'L2_ffn_Wu1': _L2_ffn_in['Wu1'], 'L2_ffn_bu1': _L2_ffn_in['bu1'], 'L2_ffn_Wu2': _L2_ffn_in['Wu2'], 'L2_ffn_bu2': _L2_ffn_in['bu2'], 'L2_ffn_gate_w1': _L2_ffn_in['gate_w1'], 'L2_ffn_gate_bias': _L2_ffn_in['gate_bias'], 'L2_ffn_log_rel': _L2_ffn_in['log_rel'], 'L3_attn_wq': _L3_attn_in['wq'], 'L3_attn_wk': _L3_attn_in['wk'], 'L3_attn_wv': _L3_attn_in['wv'], 'L3_attn_wo': _L3_attn_in['wo'], 'L3_ffn_Wq': _L3_ffn_in['Wq'], 'L3_ffn_Wr': _L3_ffn_in['Wr'], 'L3_ffn_aux_keys': _L3_ffn_in['aux_keys'], 'L3_ffn_aux_values': _L3_ffn_in['aux_values'], 'L3_ffn_Wvd': _L3_ffn_in['Wvd'], 'L3_ffn_Wvu': _L3_ffn_in['Wvu'], 'L3_ffn_Wu1': _L3_ffn_in['Wu1'], 'L3_ffn_bu1': _L3_ffn_in['bu1'], 'L3_ffn_Wu2': _L3_ffn_in['Wu2'], 'L3_ffn_bu2': _L3_ffn_in['bu2'], 'L3_ffn_gate_w1': _L3_ffn_in['gate_w1'], 'L3_ffn_gate_bias': _L3_ffn_in['gate_bias'], 'L3_ffn_log_rel': _L3_ffn_in['log_rel']}
    _x0 = _d['L0_attn_x']
    _d['L0_attn_x'] = jax.random.normal(jax.random.fold_in(jax.random.key(seed), 1), (2, 512, 512), dtype=_x0.dtype)
    del _x0
    return _d

def reference(L0_attn_x, L0_attn_Wqk_w, L0_attn_Wqk_b, L0_attn_Wv_w, L0_attn_Wv_b, L0_attn_Wo_w, L0_attn_Wo_b, L0_ffn_weight, L0_ffn_bias, L0_ffn_lora_A, L0_ffn_lora_B, L0_ffn_lora_start_indices, L1_attn_wq, L1_attn_wk, L1_attn_wv, L1_attn_wo, L1_ffn_router_w, L1_ffn_router_b, L1_ffn_router_bias, L1_ffn_ew1, L1_ffn_eb1, L1_ffn_ew2, L1_ffn_eb2, L1_ffn_ew3, L1_ffn_eb3, L1_ffn_sw1, L1_ffn_sb1, L1_ffn_sw2, L1_ffn_sb2, L1_ffn_sw3, L1_ffn_sb3, L2_attn_Wq, L2_attn_Wk, L2_attn_Wv, L2_attn_Wo, L2_ffn_Wq, L2_ffn_Wr, L2_ffn_aux_keys, L2_ffn_aux_values, L2_ffn_Wvd, L2_ffn_Wvu, L2_ffn_Wu1, L2_ffn_bu1, L2_ffn_Wu2, L2_ffn_bu2, L2_ffn_gate_w1, L2_ffn_gate_bias, L2_ffn_log_rel, L3_attn_wq, L3_attn_wk, L3_attn_wv, L3_attn_wo, L3_ffn_Wq, L3_ffn_Wr, L3_ffn_aux_keys, L3_ffn_aux_values, L3_ffn_Wvd, L3_ffn_Wvu, L3_ffn_Wu1, L3_ffn_bu1, L3_ffn_Wu2, L3_ffn_bu2, L3_ffn_gate_w1, L3_ffn_gate_bias, L3_ffn_log_rel):

    def _L0_attn_ref(x, Wqk_w, Wqk_b, Wv_w, Wv_b, Wo_w, Wo_b):
        import jax, jax.numpy as jnp
        import numpy as np
        B, N, D = (8, 128, 512)
        H = 8
        HEAD_DIM = D // H
        E = HEAD_DIM // H
        b, n, _ = x.shape
        qk = (x @ Wqk_w.T + Wqk_b).reshape(b, n, H, E, 2)
        q = jnp.transpose(qk[..., 0], (0, 2, 1, 3))
        k = jnp.transpose(qk[..., 1], (0, 2, 1, 3))
        v = (x @ Wv_w.T + Wv_b).reshape(b, n, H, E)
        v = jnp.transpose(v, (0, 2, 1, 3))
        scores = jnp.einsum('bhqd,bhkd->bhqk', q, k)
        attn = jax.nn.softmax(scores, axis=-1) / jnp.asarray(HEAD_DIM ** 0.5, x.dtype)
        out = jnp.einsum('bhsl,bhlv->bhsv', attn, v)
        out = jnp.transpose(out, (0, 2, 1, 3)).reshape(b, n, H * E)
        return out @ Wo_w.T + Wo_b

    def _L0_ffn_ref(x, weight, bias, lora_A, lora_B, lora_start_indices):
        import jax, jax.numpy as jnp
        import numpy as np
        LORA_RANK = 16
        LORA_ALPHA = 16
        LORA_SCALE = LORA_ALPHA / LORA_RANK
        y = jnp.einsum('bsd,od->bso', x, weight) + bias
        B = x.shape[0]
        seg = jnp.searchsorted(lora_start_indices, jnp.arange(B), side='right') - 1
        adapter_idx = jnp.clip(seg - 1, 0, lora_A.shape[0] - 1)
        A = lora_A[adapter_idx]
        Bw = lora_B[adapter_idx]
        lo = jnp.einsum('bsr,bor->bso', jnp.einsum('bsd,brd->bsr', x, A), Bw) * LORA_SCALE
        use_lora = (seg > 0)[:, None, None]
        return y + jnp.where(use_lora, lo, jnp.zeros((), dtype=y.dtype))

    def _L1_attn_ref(hidden_states, wq, wk, wv, wo):
        import jax, jax.numpy as jnp
        import numpy as np
        import math
        B, S, D = (1, 256, 512)
        H, KV, HD = (32, 8, 128)
        GROUPS = H // KV
        SYS_LEN, IMG_LEN = (35, 72)
        ENH, SUP = (1.5, 0.5)
        ROPE_BASE = 10000.0

        def _rope_cos_sin(seq_len, dtype):
            inv_freq = 1.0 / ROPE_BASE ** (jnp.arange(0, HD, 2, dtype=jnp.float32) / HD)
            pos = jnp.arange(seq_len, dtype=jnp.float32)
            freqs = pos[:, None] * inv_freq[None, :]
            emb = jnp.concatenate([freqs, freqs], axis=-1)
            return (jnp.cos(emb).astype(dtype), jnp.sin(emb).astype(dtype))

        def _rotate_half(x):
            x1, x2 = (x[..., :HD // 2], x[..., HD // 2:])
            return jnp.concatenate([-x2, x1], axis=-1)
        bsz, q_len, _ = hidden_states.shape
        dt = hidden_states.dtype
        q = (hidden_states @ wq.T).reshape(bsz, q_len, H, HD).transpose(0, 2, 1, 3)
        k = (hidden_states @ wk.T).reshape(bsz, q_len, KV, HD).transpose(0, 2, 1, 3)
        v = (hidden_states @ wv.T).reshape(bsz, q_len, KV, HD).transpose(0, 2, 1, 3)
        cos, sin = _rope_cos_sin(q_len, dt)
        q = q * cos + _rotate_half(q) * sin
        k = k * cos + _rotate_half(k) * sin
        k = jnp.repeat(k, GROUPS, axis=1)
        v = jnp.repeat(v, GROUPS, axis=1)
        scores = jnp.einsum('bhqd,bhkd->bhqk', q, k) / math.sqrt(HD)
        kpos = jnp.arange(q_len)
        key_scale = jnp.where(kpos < SYS_LEN, SUP, jnp.where(kpos < SYS_LEN + IMG_LEN, ENH, 1.0)).astype(dt)
        qpos = jnp.arange(q_len)
        row_sel = (qpos >= SYS_LEN + IMG_LEN)[:, None]
        scale = jnp.where(row_sel, key_scale[None, :], jnp.ones((), dt))
        scores = scores * scale
        causal = jnp.where(qpos[:, None] >= kpos[None, :], 0.0, jnp.finfo(jnp.float32).min)
        scores = scores + causal.astype(dt)
        probs = jax.nn.softmax(scores.astype(jnp.float32), axis=-1).astype(dt)
        attn = jnp.einsum('bhqk,bhkd->bhqd', probs, v)
        attn = attn.transpose(0, 2, 1, 3).reshape(bsz, q_len, H * HD)
        return attn @ wo.T

    def _L1_ffn_ref(x, router_w, router_b, router_bias, ew1, eb1, ew2, eb2, ew3, eb3, sw1, sb1, sw2, sb2, sw3, sb3):
        import jax, jax.numpy as jnp
        import numpy as np
        DIM = 512
        INTER = 128
        E = 16
        GROUPS = 4
        LIM = 2
        K = 2
        SHARED_INTER = 2 * INTER
        SCALE = 1.0
        shape = x.shape
        xt = x.reshape(-1, DIM)
        T = xt.shape[0]
        logits = xt @ router_w + router_b
        scores = jax.nn.softmax(logits.astype(jnp.float32), axis=-1) + router_bias
        g = scores.reshape(T, GROUPS, E // GROUPS)
        _, gidx = jax.lax.top_k(g.max(axis=-1), LIM)
        keep = jnp.zeros((T, GROUPS), bool).at[jnp.arange(T)[:, None], gidx].set(True)
        masked = jnp.where(keep[:, :, None], g, -jnp.inf).reshape(T, E)
        _, idx = jax.lax.top_k(masked, K)
        vals = (jnp.take_along_axis(scores, idx, axis=1) * SCALE).astype(x.dtype)
        gate = jnp.zeros((T, E), x.dtype).at[jnp.arange(T)[:, None], idx].add(vals)

        def step(y, p):
            w1, b1, w2, b2, w3, b3, ge = p
            h = jax.nn.silu(xt @ w1 + b1) * (xt @ w2 + b2)
            return (y + ge[:, None] * (h @ w3 + b3), None)
        y, _ = jax.lax.scan(step, jnp.zeros_like(xt), (ew1, eb1, ew2, eb2, ew3, eb3, gate.T))
        z = jax.nn.silu(xt @ sw1 + sb1) * (xt @ sw2 + sb2) @ sw3 + sb3
        return (y + z).reshape(shape)

    def _L2_attn_ref(x, Wq, Wk, Wv, Wo):
        import math
        import jax, jax.numpy as jnp
        import numpy as np
        B, T, E = (2, 256, 512)
        H, HKV = (32, 8)
        DH = E // H
        G = H // HKV
        ROPE_THETA = 500000.0
        ROPE_FACTOR = 32.0
        HI_FREQ_FACTOR = 4.0
        LO_FREQ_FACTOR = 1.0
        ORIG_CTX = 1024

        def _rope_cos_sin(t_len):
            inv_freq = 1.0 / ROPE_THETA ** (jnp.arange(0, DH, 2, dtype=jnp.float32) / DH)
            wavelen = 2.0 * math.pi / inv_freq
            cut_lo = ORIG_CTX / HI_FREQ_FACTOR
            cut_hi = ORIG_CTX / LO_FREQ_FACTOR
            inv_freq = jnp.where(wavelen > cut_hi, inv_freq / ROPE_FACTOR, inv_freq)
            smooth = (ORIG_CTX / wavelen - LO_FREQ_FACTOR) / (HI_FREQ_FACTOR - LO_FREQ_FACTOR)
            smoothed = (1.0 - smooth) * inv_freq / ROPE_FACTOR + smooth * inv_freq
            is_medium = ~(wavelen < cut_hi) & ~(wavelen > cut_lo)
            inv_freq = jnp.where(is_medium, smoothed, inv_freq)
            pos = jnp.arange(t_len, dtype=jnp.float32)
            freqs = pos[:, None] * inv_freq[None, :]
            emb = jnp.concatenate([freqs, freqs], axis=-1)
            return (jnp.cos(emb), jnp.sin(emb))

        def _rotate_half(x):
            x1, x2 = jnp.split(x, 2, axis=-1)
            return jnp.concatenate([-x2, x1], axis=-1)
        b, t, _ = x.shape
        q = (x @ Wq.T).reshape(b, t, H, DH).transpose(0, 2, 1, 3)
        k = (x @ Wk.T).reshape(b, t, HKV, DH).transpose(0, 2, 1, 3)
        v = (x @ Wv.T).reshape(b, t, HKV, DH).transpose(0, 2, 1, 3)
        cos, sin = _rope_cos_sin(t)
        cos = cos.astype(x.dtype)[None, None]
        sin = sin.astype(x.dtype)[None, None]
        q = q * cos + _rotate_half(q) * sin
        k = k * cos + _rotate_half(k) * sin
        qg = q.reshape(b, HKV, G, t, DH)
        scores = jnp.einsum('bhgtd,bhkd->bhgtk', qg.astype(jnp.float32), k.astype(jnp.float32)) / math.sqrt(DH)
        causal = jnp.tril(jnp.ones((t, t), dtype=bool))
        scores = jnp.where(causal[None, None, None], scores, jnp.finfo(jnp.float32).min)
        attn = jax.nn.softmax(scores, axis=-1).astype(x.dtype)
        ctx = jnp.einsum('bhgtk,bhkd->bhgtd', attn, v)
        out = ctx.reshape(b, H, t, DH).transpose(0, 2, 1, 3).reshape(b, t, E)
        return out @ Wo.T

    def _L2_ffn_ref(hidden_states, Wq, Wr, aux_keys, aux_values, Wvd, Wvu, Wu1, bu1, Wu2, bu2, gate_w1, gate_bias, log_rel):
        import jax, jax.numpy as jnp
        import numpy as np
        HID, BOT, RDIM, NSLOT, K, VB = (512, 64, 48, 128, 8, 32)
        TAU_LOW, TAU_HIGH, EARLY_EXIT = (0.5, 2.0, 0.05)

        def _uncertainty(h, Wu1, bu1, Wu2, bu2):
            var = jnp.var(h, axis=-1)
            log_var = jnp.log1p(var)
            norm_var = log_var / (jnp.mean(log_var) + 1e-06)
            learned = (jax.nn.gelu(h @ Wu1.T + bu1) @ Wu2.T + bu2)[..., 0]
            return jnp.clip(norm_var * 0.5 + jax.nn.sigmoid(learned) * 2.5, 0.0, 5.0)
        query = hidden_states @ Wq.T
        rq = query @ Wr.T
        rk = aux_keys @ Wr.T
        router_scores = jnp.einsum('bsr,nr->bsn', rq, rk) / np.sqrt(RDIM) + log_rel
        top_scores, top_idx = jax.lax.top_k(router_scores, K)
        sel_keys = aux_keys[top_idx]
        attn = jnp.einsum('bsd,bskd->bsk', query, sel_keys) / np.sqrt(BOT) + log_rel[top_idx]
        w = jax.nn.softmax(attn, axis=-1)
        sel_vals = aux_values[top_idx]
        aux_out = jnp.einsum('bsk,bskh->bsh', w, sel_vals)
        aux_out = aux_out @ Wvd.T @ Wvu.T
        u = _uncertainty(hidden_states, Wu1, bu1, Wu2, bu2)
        u_norm = jnp.clip((u - TAU_LOW) / (TAU_HIGH - TAU_LOW), 0.0, 1.0)
        gate = jax.nn.sigmoid(gate_w1 * u_norm + gate_bias)
        gate = jnp.where(gate < EARLY_EXIT, 0.0, gate)
        return hidden_states + gate[..., None] * aux_out

    def _L3_attn_ref(x, wq, wk, wv, wo):
        import jax, jax.numpy as jnp
        import numpy as np
        H, KV, HD, HID = (32, 8, 128, 512)
        THETA, FACTOR, HI_FF, LO_FF, ORIG_MAX = (500000.0, 8.0, 4.0, 1.0, 1024)

        def _llama3_inv_freq():
            inv = 1.0 / THETA ** (np.arange(0, HD, 2, dtype=np.float64) / HD)
            wavelen = 2.0 * np.pi / inv
            low_wl = ORIG_MAX / LO_FF
            high_wl = ORIG_MAX / HI_FF
            smooth = (ORIG_MAX / wavelen - LO_FF) / (HI_FF - LO_FF)
            scaled = np.where(wavelen > low_wl, inv / FACTOR, inv)
            mid = (wavelen <= low_wl) & (wavelen >= high_wl)
            scaled = np.where(mid, (1 - smooth) * inv / FACTOR + smooth * inv, scaled)
            return scaled.astype(np.float32)

        def _rope_cos_sin(T):
            inv = _llama3_inv_freq()
            pos = np.arange(T, dtype=np.float32)
            freqs = pos[:, None] * inv[None, :]
            emb = np.concatenate([freqs, freqs], axis=-1)
            return (jnp.asarray(np.cos(emb)), jnp.asarray(np.sin(emb)))

        def _rotate_half(x):
            x1, x2 = jnp.split(x, 2, axis=-1)
            return jnp.concatenate([-x2, x1], axis=-1)
        B, T, _ = x.shape
        q = (x @ wq).reshape(B, T, H, HD).transpose(0, 2, 1, 3)
        k = (x @ wk).reshape(B, T, KV, HD).transpose(0, 2, 1, 3)
        v = (x @ wv).reshape(B, T, KV, HD).transpose(0, 2, 1, 3)
        cos, sin = _rope_cos_sin(T)
        q = q * cos + _rotate_half(q) * sin
        k = k * cos + _rotate_half(k) * sin
        rep = H // KV
        k = jnp.repeat(k, rep, axis=1)
        v = jnp.repeat(v, rep, axis=1)
        scores = jnp.einsum('bhtd,bhsd->bhts', q, k) * (1.0 / np.sqrt(HD))
        mask = jnp.tril(jnp.ones((T, T), dtype=bool))
        scores = jnp.where(mask, scores, -jnp.inf)
        att = jax.nn.softmax(scores, axis=-1)
        out = jnp.einsum('bhts,bhsd->bhtd', att, v)
        out = out.transpose(0, 2, 1, 3).reshape(B, T, H * HD)
        return out @ wo

    def _L3_ffn_ref(hidden_states, Wq, Wr, aux_keys, aux_values, Wvd, Wvu, Wu1, bu1, Wu2, bu2, gate_w1, gate_bias, log_rel):
        import jax, jax.numpy as jnp
        import numpy as np
        HID, BOT, RDIM, NSLOT, K, VB = (512, 64, 48, 128, 8, 32)
        TAU_LOW, TAU_HIGH, EARLY_EXIT = (0.5, 2.0, 0.05)

        def _uncertainty(h, Wu1, bu1, Wu2, bu2):
            var = jnp.var(h, axis=-1)
            log_var = jnp.log1p(var)
            norm_var = log_var / (jnp.mean(log_var) + 1e-06)
            learned = (jax.nn.gelu(h @ Wu1.T + bu1) @ Wu2.T + bu2)[..., 0]
            return jnp.clip(norm_var * 0.5 + jax.nn.sigmoid(learned) * 2.5, 0.0, 5.0)
        query = hidden_states @ Wq.T
        rq = query @ Wr.T
        rk = aux_keys @ Wr.T
        router_scores = jnp.einsum('bsr,nr->bsn', rq, rk) / np.sqrt(RDIM) + log_rel
        top_scores, top_idx = jax.lax.top_k(router_scores, K)
        sel_keys = aux_keys[top_idx]
        attn = jnp.einsum('bsd,bskd->bsk', query, sel_keys) / np.sqrt(BOT) + log_rel[top_idx]
        w = jax.nn.softmax(attn, axis=-1)
        sel_vals = aux_values[top_idx]
        aux_out = jnp.einsum('bsk,bskh->bsh', w, sel_vals)
        aux_out = aux_out @ Wvd.T @ Wvu.T
        u = _uncertainty(hidden_states, Wu1, bu1, Wu2, bu2)
        u_norm = jnp.clip((u - TAU_LOW) / (TAU_HIGH - TAU_LOW), 0.0, 1.0)
        gate = jax.nn.sigmoid(gate_w1 * u_norm + gate_bias)
        gate = jnp.where(gate < EARLY_EXIT, 0.0, gate)
        return hidden_states + gate[..., None] * aux_out
    x = L0_attn_x
    xn = _layernorm(x, axis=-1)
    x = x + _L0_attn_ref(xn, L0_attn_Wqk_w, L0_attn_Wqk_b, L0_attn_Wv_w, L0_attn_Wv_b, L0_attn_Wo_w, L0_attn_Wo_b) + _L0_ffn_ref(xn, L0_ffn_weight, L0_ffn_bias, L0_ffn_lora_A, L0_ffn_lora_B, L0_ffn_lora_start_indices)
    xn = _layernorm(x, axis=-1)
    x = x + _L1_attn_ref(xn, L1_attn_wq, L1_attn_wk, L1_attn_wv, L1_attn_wo) + _L1_ffn_ref(xn, L1_ffn_router_w, L1_ffn_router_b, L1_ffn_router_bias, L1_ffn_ew1, L1_ffn_eb1, L1_ffn_ew2, L1_ffn_eb2, L1_ffn_ew3, L1_ffn_eb3, L1_ffn_sw1, L1_ffn_sb1, L1_ffn_sw2, L1_ffn_sb2, L1_ffn_sw3, L1_ffn_sb3)
    xn = _layernorm(x, axis=-1)
    x = x + _L2_attn_ref(xn, L2_attn_Wq, L2_attn_Wk, L2_attn_Wv, L2_attn_Wo) + _L2_ffn_ref(xn, L2_ffn_Wq, L2_ffn_Wr, L2_ffn_aux_keys, L2_ffn_aux_values, L2_ffn_Wvd, L2_ffn_Wvu, L2_ffn_Wu1, L2_ffn_bu1, L2_ffn_Wu2, L2_ffn_bu2, L2_ffn_gate_w1, L2_ffn_gate_bias, L2_ffn_log_rel)
    xn = _layernorm(x, axis=-1)
    x = x + _L3_attn_ref(xn, L3_attn_wq, L3_attn_wk, L3_attn_wv, L3_attn_wo) + _L3_ffn_ref(xn, L3_ffn_Wq, L3_ffn_Wr, L3_ffn_aux_keys, L3_ffn_aux_values, L3_ffn_Wvd, L3_ffn_Wvu, L3_ffn_Wu1, L3_ffn_bu1, L3_ffn_Wu2, L3_ffn_bu2, L3_ffn_gate_w1, L3_ffn_gate_bias, L3_ffn_log_rel)
    return x

_drawn_inputs = setup_inputs


def setup_inputs(seed=0):
    import zlib

    import numpy as np

    out = dict(_drawn_inputs(seed))
    spreads = {'L0_attn_Wqk_b': (0.0, 0.8),
     'L0_attn_Wv_b': (0.0, 0.8),
     'L0_attn_Wo_b': (0.0, 0.1),
     'L2_ffn_bu1': (0.0, 2.0),
     'L2_ffn_log_rel': (0.0, 2.0),
     'L3_ffn_bu1': (0.0, 2.0),
     'L3_ffn_log_rel': (0.0, 2.0)}
    factors = {'L0_attn_Wqk_w': 8.0,
     'L0_attn_Wv_w': 8.0,
     'L0_attn_Wo_w': 8.0,
     'L0_ffn_bias': 6.231,
     'L1_attn_wq': 5.826,
     'L1_attn_wk': 5.836,
     'L1_ffn_router_w': 8.0,
     'L1_ffn_router_b': 37.916,
     'L1_ffn_eb1': 8.0,
     'L1_ffn_eb2': 8.0,
     'L1_ffn_sb1': 8.0,
     'L1_ffn_sb2': 8.0,
     'L1_ffn_sb3': 3.507,
     'L2_attn_Wq': 8.0,
     'L2_attn_Wk': 8.0,
     'L2_attn_Wv': 3.264,
     'L2_attn_Wo': 3.282,
     'L2_ffn_Wq': 64.0,
     'L2_ffn_Wr': 64.0,
     'L2_ffn_aux_keys': 64.0,
     'L2_ffn_aux_values': 64.0,
     'L2_ffn_Wvd': 64.0,
     'L2_ffn_Wvu': 64.0,
     'L2_ffn_Wu1': 64.0,
     'L2_ffn_Wu2': 64.0,
     'L3_ffn_Wq': 64.0,
     'L3_ffn_Wr': 64.0,
     'L3_ffn_aux_keys': 64.0,
     'L3_ffn_aux_values': 64.0,
     'L3_ffn_Wvd': 64.0,
     'L3_ffn_Wvu': 64.0,
     'L3_ffn_Wu1': 64.0,
     'L3_ffn_Wu2': 64.0}
    for name, (base, spread) in spreads.items():
        noise = np.random.default_rng([zlib.crc32(name.encode()), seed]).standard_normal(out[name].shape)
        drawn = base * np.exp(spread * noise) if base else spread * noise
        out[name] = jnp.asarray(drawn.astype(out[name].dtype))
    for name, factor in factors.items():
        out[name] = (out[name] * factor).astype(out[name].dtype)
    return out
```

```python
from contextlib import ExitStack

import numpy as np
import concourse.bass as bass
from concourse import mybir

F32 = mybir.dt.float32
F32R = mybir.dt.float32r
BF16 = mybir.dt.bfloat16
I32 = mybir.dt.int32
ACT = mybir.ActivationFunctionType
ALU = mybir.AluOpType
AX = mybir.AxisListType.X

P = 128
D = 512
KT = D // P
BATCH, SEQ = 2, 512
QT = SEQ // P
TT = BATCH * QT
TOK = BATCH * SEQ
EPS = 1e-5
MASKED = -1e30

HD, HEADS, GROUPS = 128, 32, 8
HPG = HEADS // GROUPS
SYS_LEN, IMG_LEN, SUP, ENH = 35, 72, 0.5, 1.5

EXPERTS, INTER, MGROUPS = 16, 128, 4
SLABS = EXPERTS + 2

BOT, RDIM, NSLOT, TOPK, VB = 64, 48, 128, 8, 32


class Count:

    def __init__(self, sem):
        self.sem, self.base, self.per = sem, 0, 0

    def start(self, per):
        first = self.per == 0
        assert first or self.per == per
        self.per = per
        return first


class Shared:
    pass


def make_shared(nc, ctx):
    k = Shared()
    k.nc = nc

    def sb(name, shape, dt=F32, stack=ctx):
        return stack.enter_context(nc.sbuf_tensor(name, shape, dt))

    k.sb = sb
    k.sems = {}

    def sem(name):
        if name not in k.sems:
            k.sems[name] = Count(ctx.enter_context(nc.semaphore(name)))
        return k.sems[name]

    k.sem = sem
    k.ctx = ctx
    k.x = sb("x", [P, TT, D])
    k.xTh = sb("xTh", [P, KT, TOK], F32R)
    k.xTl = sb("xTl", [P, KT, TOK], F32R)
    k.ident = sb("ident", [P, P])
    k.identb = sb("identb", [P, P], BF16)
    k.maskb = sb("maskb", [P, P], BF16)
    k.xvar = sb("xvar", [P, TT])
    k.bank = [ctx.enter_context(nc.psum_tensor(f"bank{n}", [P, 512], F32)) for n in range(8)]
    return k


def matmul3(nc, out, ah, al, bh, bl, first, last):
    nc.tensor.matmul(out, ah, bh, start=first, stop=False)
    nc.tensor.matmul(out, ah, bl, start=False, stop=False)
    return nc.tensor.matmul(out, al, bh, start=False, stop=last)


def load_constants(k, d):
    nc = k.nc
    with ExitStack() as st:
        cst = k.sb("cst", [P, 2, P], F32, st)
        c_in, c_cast, x_in = k.sem("c_in"), k.sem("c_cast"), k.sem("x_in")
        block = st.enter_context(nc.Block())

        @block.sync
        def _(sp):
            sp.dma_start(cst[:, :, :], d["consts"]).then_inc(c_in.sem, 16)
            sp.dma_start(k.x[:, :, :], d["x"].rearrange("(t p) n -> p t n", p=P)).then_inc(x_in.sem, 16)

        @block.vector
        def _(dve):
            dve.wait_ge(c_in.sem, 16)
            nc.vector.tensor_copy(k.ident[:, :], cst[:, 0, :])
            nc.vector.tensor_copy(k.identb[:, :], cst[:, 0, :])
            nc.vector.tensor_copy(k.maskb[:, :], cst[:, 1, :]).then_inc(c_cast.sem, 1)
            dve.wait_ge(x_in.sem, 16)


def layer_norm(k, n, add_normed):
    nc = k.nc
    with ExitStack() as st:
        xn = k.sb(f"xn{n}", [P, TT, D], F32, st)
        stats = k.sb(f"stats{n}", [P, TT, 6], F32, st)
        mv = k.sb(f"mv{n}", [P, TT, 2], F32, st)
        stats2 = k.sb(f"stats2{n}", [P, TT, 6], F32, st)
        mv2 = k.sb(f"mv2{n}", [P, TT, 2], F32, st)
        veps = k.sb(f"veps{n}", [P, TT], F32, st)
        sd = k.sb(f"sd{n}", [P, TT], F32, st)
        rstd = k.sb(f"rstd{n}", [P, TT], F32, st)
        chain, sq, normed, turned, hi, lo = (k.sem("ln_" + s) for s in "chain sqrt normed turned hi lo".split())
        c0, s0, n0, t0, h0, l0 = (s.base for s in (chain, sq, normed, turned, hi, lo))
        banks = k.bank[0:4]
        block = st.enter_context(nc.Block())
        steps = [0]

        @block.vector
        def _(dve):
            def link(ins):
                steps[0] += 1
                ins.then_inc(chain.sem, 1)
                dve.wait_ge(chain.sem, c0 + steps[0])

            for t in range(TT):
                ins = nc.vector.bn_stats(stats[:, t, :], k.x[:, t, :])
            link(ins)
            for t in range(TT):
                ins = nc.vector.bn_aggr(mv[:, t, :], stats[:, t, :])
            link(ins)
            nc.vector.tensor_scalar(veps[:, :], mv[:, :, 1], EPS, None, ALU.add).then_inc(chain.sem, 1)
            steps[0] += 1
            dve.wait_ge(sq.sem, s0 + 1)
            link(nc.vector.reciprocal(rstd[:, :], sd[:, :]))

            def low_part(t):
                dve.wait_ge(hi.sem, h0 + t + 1)
                nc.vector.tensor_tensor(
                    k.xTl[:, :, t * P:(t + 1) * P], banks[t % 4][:, :].rearrange("p (a q) -> p a q", a=KT),
                    k.xTh[:, :, t * P:(t + 1) * P].bitcast(F32), ALU.subtract).then_inc(lo.sem, 1)

            for t in range(TT):
                nc.vector.tensor_scalar(xn[:, t, :], k.x[:, t, :], mv[:, t, 0:1], rstd[:, t:t + 1],
                                        ALU.subtract, ALU.mult).then_inc(normed.sem, 1)
                if t >= 1:
                    low_part(t - 1)
            low_part(TT - 1)
            if add_normed:
                dve.wait_ge(normed.sem, n0 + TT)
                for t in range(TT):
                    ins = nc.vector.bn_stats(stats2[:, t, :], xn[:, t, :])
                link(ins)
                for t in range(TT):
                    ins = nc.vector.bn_aggr(mv2[:, t, :], stats2[:, t, :])
                link(ins)
                nc.vector.tensor_copy(k.xvar[:, :], mv2[:, :, 1])

        @block.scalar
        def _(act):
            act.wait_ge(chain.sem, c0 + 3)
            nc.scalar.activation(sd[:, :], veps[:, :], ACT.Sqrt).then_inc(sq.sem, 1)
            for t in range(TT):
                act.wait_ge(turned.sem, t0 + t + 1)
                nc.scalar.activation(k.xTh[:, :, t * P:(t + 1) * P],
                                     banks[t % 4][:, :].rearrange("p (a q) -> p a q", a=KT), ACT.Copy).then_inc(hi.sem, 1)

        @block.tensor
        def _(pe):
            for t in range(TT):
                pe.wait_ge(normed.sem, n0 + t + 1)
                if t >= 4:
                    pe.wait_ge(lo.sem, l0 + t - 3)
                for a in range(KT):
                    ins = nc.tensor.transpose(banks[t % 4][:, a * P:(a + 1) * P], xn[:, t, a * P:(a + 1) * P], k.ident[:, :])
                ins.then_inc(turned.sem, 1)

        @block.gpsimd
        def _(pool):
            if add_normed:
                for t in range(TT):
                    pool.wait_ge(normed.sem, n0 + t + 1)
                    nc.gpsimd.tensor_tensor(k.x[:, t, :], k.x[:, t, :], xn[:, t, :], ALU.add)

        chain.base += steps[0]
        sq.base += 1
        for s in (normed, turned, hi, lo):
            s.base += TT


def wide_attention(k, d, name, tile0_scale):
    nc = k.nc
    UNITS = BATCH * HPG
    ACC, SM, TR = 20, 4 * UNITS, 4 * UNITS
    W_SEQ = ["wk", "wq0", "wq1", "wv", "wq2", "wq3", "wo0", "wo1", "wo2", "wo3"]
    w_at = {w: n for n, w in enumerate(W_SEQ)}
    acc_seq = ["K0", "K1", "Q0", "Q1", "V0", "V1"] + [f"Q{u}" for u in range(2, 8)] + [f"W{t}" for t in range(TT)]
    assert len(acc_seq) == ACC
    acc_at = {a: n for n, a in enumerate(acc_seq)}
    row_off = [P * i * (i + 1) // 2 for i in range(QT + 1)]
    ORDER = [3, 2, 1, 0]

    with ExitStack() as st:
        def sb(nm, shape, dt=F32):
            return k.sb(name + nm, shape, dt, st)

        wq_st = sb("wq_st", [P, 2, KT, HD])
        wo_st = sb("wo_st", [P, 2, D])
        wk_st = sb("wk_st", [P, KT, HD])
        wv_st = sb("wv_st", [P, KT, HD])
        wqh, wql = sb("wqh", [P, HPG, KT, HD], F32R), sb("wql", [P, HPG, KT, HD], F32R)
        woh, wol = sb("woh", [P, HPG, D], F32R), sb("wol", [P, HPG, D], F32R)
        wkh, wkl = sb("wkh", [P, KT, HD], F32R), sb("wkl", [P, KT, HD], F32R)
        wvh, wvl = sb("wvh", [P, KT, HD], F32R), sb("wvl", [P, KT, HD], F32R)
        kh, kl = sb("kh", [P, BATCH, SEQ], F32R), sb("kl", [P, BATCH, SEQ], F32R)
        vh, vl = sb("vh", [P, TT, HD], F32R), sb("vl", [P, TT, HD], F32R)
        rope_a, rope_b, rope_s = sb("rope_a", [P, SEQ]), sb("rope_b", [P, SEQ]), sb("rope_s", [P, SEQ])
        qh, ql = sb("qh", [P, 3, SEQ], F32R), sb("ql", [P, 3, SEQ], F32R)
        probs = sb("probs", [P, 2, row_off[QT]])
        pth, ptl = sb("pth", [P, 2, SEQ], F32R), sb("ptl", [P, 2, SEQ], F32R)
        oth, otl = sb("oth", [P, UNITS, SEQ], F32R), sb("otl", [P, UNITS, SEQ], F32R)
        tables = sb("tables", [P, 4, SEQ])
        t0s = sb("t0s", [P, P]) if tile0_scale else None
        negmax, rowsum, rinv = sb("negmax", [P, UNITS, QT]), sb("rowsum", [P, UNITS, QT]), sb("rinv", [P, UNITS, QT])

        acc, sbank, tbank, obank = k.bank[0:2], k.bank[2:5], k.bank[5:7], k.bank[7]

        pers = dict(acc_mm=ACC, s_mm=SM, t_mm=TR, pv_mm=TR,
                    acc_out=ACC, maxed=SM, rinv_ok=UNITS, pt_lo=TR, o_lo=UNITS,
                    exp_ok=SM, pt_hi=TR, o_hi=UNITS, qk_hi=10, v_hi=2, w_hi=10,
                    qk_sum=10, qk_lo=10, norm_ok=SM, w_lo=10)
        s = {n: k.sem("wa_" + n) for n in pers}
        due = {n: s[n].start(pers[n]) for n in pers}
        d_in = {n: k.sem("wa_in_" + n) for n in ("wq0", "wq1", "wo0", "wo1", "wk", "wv", "tab")}
        d_base = {n: d_in[n].base for n in d_in}
        swaps = k.sem("wa_tab_seen")
        base = {n: s[n].base for n in pers}

        def credit(eng, *names):
            for n in names:
                if due[n]:
                    eng.sem_inc(s[n].sem, pers[n])

        def waits(eng, g):
            def w(n, count):
                eng.wait_ge(s[n].sem, base[n] + pers[n] + g * pers[n] + count)
            return w

        block = st.enter_context(nc.Block())

        @block.sync
        def _(sp):
            sp.dma_start(tables[:, :, :], d[name + "tables"]).then_inc(d_in["tab"].sem, 16)
            if tile0_scale:
                sp.dma_start(t0s[:, :], d[name + "t0s"]).then_inc(d_in["tab"].sem, 16)
            with sp.Fori(0, GROUPS) as g:
                w = waits(sp, g)

                def load(buf, src, sem):
                    sp.dma_start(buf, src).then_inc(d_in[sem].sem, 16)

                def wq(h):
                    w("w_lo", w_at[f"wq{h - 2}"] + 1 if h >= 2 else w_at[f"wq{h + 2}"] + 1 - 10)
                    load(wq_st[:, h % 2, :, :], d[name + "wq"][bass.ds(g * HPG + h, 1)].rearrange("a p k n -> p (a k) n"), f"wq{h % 2}")

                def wo(h):
                    w("w_lo", w_at[f"wo{h - 2}"] + 1 if h >= 2 else w_at[f"wo{h + 2}"] + 1 - 10)
                    load(wo_st[:, h % 2, :], d[name + "wo"][bass.ds(g * HPG + h, 1)].rearrange("a p n -> p (a n)"), f"wo{h % 2}")

                w("w_lo", w_at["wk"] + 1 - 10)
                load(wk_st[:, :, :], d[name + "wk"][bass.ds(g, 1)].rearrange("a p k n -> p (a k) n"), "wk")
                wq(0)
                wq(1)
                w("w_lo", w_at["wv"] + 1 - 10)
                load(wv_st[:, :, :], d[name + "wv"][bass.ds(g, 1)].rearrange("a p k n -> p (a k) n"), "wv")
                wq(2)
                wq(3)
                for h in range(HPG):
                    wo(h)

        def weight_parts(wname):
            h = int(wname[2]) if len(wname) == 3 else 0
            if wname.startswith("wq"):
                return wq_st[:, h % 2, :, :], wqh[:, h, :, :], wql[:, h, :, :], f"wq{h % 2}", 2, h // 2 + 1
            if wname.startswith("wo"):
                return wo_st[:, h % 2, :], woh[:, h, :], wol[:, h, :], f"wo{h % 2}", 2, h // 2 + 1
            if wname == "wk":
                return wk_st[:, :, :], wkh[:, :, :], wkl[:, :, :], "wk", 1, 1
            return wv_st[:, :, :], wvh[:, :, :], wvl[:, :, :], "wv", 1, 1

        def qk_parts(a):
            n = int(a[1:])
            if a[0] == "K":
                return kh[:, n, :], kl[:, n, :]
            return qh[:, n % 3, :], ql[:, n % 3, :]

        qk_seq = ["K0", "K1"] + [f"Q{u}" for u in range(UNITS)]
        qk_at = {a: n for n, a in enumerate(qk_seq)}

        @block.tensor
        def _(pe):
            credit(pe, "acc_mm", "s_mm", "t_mm", "pv_mm")
            with pe.Fori(0, GROUPS) as g:
                w = waits(pe, g)

                def acc_bank(a):
                    w("acc_out", acc_at[a] - 1)
                    return acc[acc_at[a] % 2]

                def project_qk(a, wh, wl, b, wname):
                    bank = acc_bank(a)
                    w("w_lo", w_at[wname] + 1)
                    for t in range(KT):
                        ins = matmul3(nc, bank[:, :], wh[:, t, :], wl[:, t, :], k.xTh[:, t, b * SEQ:(b + 1) * SEQ],
                                      k.xTl[:, t, b * SEQ:(b + 1) * SEQ], t == 0, t == KT - 1)
                    ins.then_inc(s["acc_mm"].sem, 1)

                def project_q(u):
                    h = u % HPG
                    project_qk(f"Q{u}", wqh[:, h, :, :], wql[:, h, :, :], u // HPG, f"wq{h}")

                def project_v(half):
                    bank = acc_bank(f"V{half}")
                    w("w_lo", w_at["wv"] + 1)
                    for t in range(QT):
                        tok = slice((half * QT + t) * P, (half * QT + t + 1) * P)
                        for a in range(KT):
                            ins = matmul3(nc, bank[:, t * HD:(t + 1) * HD], k.xTh[:, a, tok], k.xTl[:, a, tok],
                                          wvh[:, a, :], wvl[:, a, :], a == 0, a == KT - 1)
                    ins.then_inc(s["acc_mm"].sem, 1)

                def scores(u, n):
                    i, m, b = ORDER[n], 4 * u + n, u // HPG
                    w("exp_ok", m - 2 if m >= 3 else 0)
                    w("qk_lo", qk_at[f"Q{u}"] + 1)
                    keys = (i + 1) * P
                    out = sbank[m % 3][:, 0:keys]
                    rows = slice(i * P, (i + 1) * P)
                    matmul3(nc, out, qh[:, u % 3, rows], ql[:, u % 3, rows], kh[:, b, 0:keys], kl[:, b, 0:keys], True, False)
                    nc.tensor.matmul(sbank[m % 3][:, i * P:keys], k.identb[:, :], k.maskb[:, :],
                                     start=False, stop=True).then_inc(s["s_mm"].sem, 1)

                def turn_probs(u, j):
                    n = 4 * u + j
                    w("pt_lo", n - 1)
                    if j == 0:
                        w("norm_ok", 4 * u + 4)
                    for i in range(j, QT):
                        ins = nc.tensor.transpose(tbank[n % 2][:, i * P:(i + 1) * P],
                                                  probs[:, u % 2, row_off[i] + j * P:row_off[i] + (j + 1) * P], k.ident[:, :])
                    ins.then_inc(s["t_mm"].sem, 1)

                def values(u, j):
                    n, vt = 4 * u + j, (u // HPG) * QT + j
                    if j == 0:
                        w("o_lo", u)
                        w("acc_out", acc_at[f"V{u // HPG}"] + 1)
                    w("pt_lo", n + 1)
                    cols = slice(j * P, SEQ)
                    matmul3(nc, obank[:, cols], vh[:, vt, :], vl[:, vt, :], pth[:, n % 2, cols], ptl[:, n % 2, cols],
                            j == 0, j == QT - 1).then_inc(s["pv_mm"].sem, 1)

                def unit_out(u):
                    turn_probs(u, 0)
                    turn_probs(u, 1)
                    values(u, 0)
                    turn_probs(u, 2)
                    values(u, 1)
                    turn_probs(u, 3)
                    values(u, 2)
                    values(u, 3)

                def project_out(t):
                    bank, b = acc_bank(f"W{t}"), t // QT
                    rows = slice((t % QT) * P, (t % QT + 1) * P)
                    for h in range(HPG):
                        u = b * HPG + h
                        w("o_lo", u + 1)
                        w("w_lo", w_at[f"wo{h}"] + 1)
                        ins = matmul3(nc, bank[:, :], oth[:, u, rows], otl[:, u, rows], woh[:, h, :], wol[:, h, :],
                                      h == 0, h == HPG - 1)
                    ins.then_inc(s["acc_mm"].sem, 1)

                project_qk("K0", wkh, wkl, 0, "wk")
                project_qk("K1", wkh, wkl, 1, "wk")
                project_q(0)
                project_q(1)
                project_v(0)
                project_v(1)
                for u in range(UNITS + 1):
                    if u < UNITS:
                        scores(u, 0)
                        scores(u, 1)
                        scores(u, 2)
                    if u + 2 < UNITS:
                        project_q(u + 2)
                    if u < UNITS:
                        scores(u, 3)
                    if u >= 5:
                        project_out(u - 5)
                    if u >= 1:
                        unit_out(u - 1)
                for t in range(QT, TT):
                    project_out(t)

        @block.vector
        def _(dve):
            credit(dve, "acc_out", "maxed", "rinv_ok", "pt_lo", "o_lo")
            dve.wait_ge(d_in["tab"].sem, d_base["tab"] + (32 if tile0_scale else 16))
            with dve.Fori(0, GROUPS) as g:
                w = waits(dve, g)

                def rope(a):
                    bank, c = acc[acc_at[a] % 2], 2 if a[0] == "K" else 0
                    w("acc_mm", acc_at[a] + 1)
                    w("qk_sum", qk_at[a])
                    H = HD // 2
                    nc.vector.tensor_tensor(rope_a[:, :], bank[:, :], tables[:, c, :], ALU.mult)
                    nc.vector.tensor_tensor(rope_b[0:H, :], bank[H:HD, :], tables[H:HD, c + 1, :], ALU.mult)
                    nc.vector.tensor_tensor(rope_b[H:HD, :], bank[0:H, :], tables[0:H, c + 1, :],
                                            ALU.mult).then_inc(s["acc_out"].sem, 1)

                def v_low(half):
                    bank = acc[acc_at[f"V{half}"] % 2]
                    w("v_hi", half + 1)
                    tiles = slice(half * QT, (half + 1) * QT)
                    nc.vector.tensor_tensor(vl[:, tiles, :], bank[:, :].rearrange("p (t n) -> p t n", t=QT),
                                            vh[:, tiles, :].bitcast(F32), ALU.subtract).then_inc(s["acc_out"].sem, 1)

                def row_max(u, n):
                    i, m = ORDER[n], 4 * u + n
                    w("s_mm", m + 1)
                    sc = sbank[m % 3][:, 0:(i + 1) * P]
                    if i == 0 and tile0_scale:
                        nc.vector.tensor_tensor(sc, sc, t0s[:, :], ALU.mult).then_inc(swaps.sem, 1)
                        dve.wait_ge(swaps.sem, swaps.base + g * UNITS + u + 1)
                    nc.vector.tensor_reduce(negmax[:, u, i:i + 1], sc, AX, ALU.max, negate=True).then_inc(s["maxed"].sem, 1)

                def probs_low(u, j):
                    n = 4 * u + j
                    w("pt_hi", n + 1)
                    cols = slice(j * P, SEQ)
                    nc.vector.tensor_tensor(ptl[:, n % 2, cols], tbank[n % 2][:, cols], pth[:, n % 2, cols].bitcast(F32),
                                            ALU.subtract).then_inc(s["pt_lo"].sem, 1)

                def out_low(u):
                    w("o_hi", u + 1)
                    nc.vector.tensor_tensor(otl[:, u, :], obank[:, :], oth[:, u, :].bitcast(F32),
                                            ALU.subtract).then_inc(s["o_lo"].sem, 1)

                def add_out(t):
                    w("acc_mm", acc_at[f"W{t}"] + 1)
                    nc.vector.tensor_tensor(k.x[:, t, :], acc[acc_at[f"W{t}"] % 2][:, :], k.x[:, t, :],
                                            ALU.add).then_inc(s["acc_out"].sem, 1)

                for a in ("K0", "K1", "Q0", "Q1"):
                    rope(a)
                v_low(0)
                v_low(1)
                for u in range(UNITS + 1):
                    if u < UNITS:
                        row_max(u, 0)
                        row_max(u, 1)
                        row_max(u, 2)
                    if u + 2 < UNITS:
                        rope(f"Q{u + 2}")
                    if u < UNITS:
                        row_max(u, 3)
                    if u >= 5:
                        add_out(u - 5)
                    if u >= 1:
                        for j in range(QT):
                            probs_low(u - 1, j)
                        out_low(u - 1)
                    if u < UNITS:
                        w("exp_ok", 4 * u + 4)
                        nc.vector.reciprocal(rinv[:, u, :], rowsum[:, u, :]).then_inc(s["rinv_ok"].sem, 1)
                for t in range(QT, TT):
                    add_out(t)

        @block.scalar
        def _(act):
            credit(act, "exp_ok", "pt_hi", "o_hi", "qk_hi", "v_hi", "w_hi")
            with act.Fori(0, GROUPS) as g:
                w = waits(act, g)

                def weight_high(wname):
                    src, hi, _, sem, per, at = weight_parts(wname)
                    act.wait_ge(d_in[sem].sem, d_base[sem] + g * 16 * per + 16 * at)
                    if wname == "wk":
                        w("acc_mm", acc_at["K1"] + 1 - ACC)
                    elif wname == "wv":
                        w("acc_mm", acc_at["V1"] + 1 - ACC)
                    elif wname[1] == "q":
                        w("acc_mm", acc_at[f"Q{int(wname[2]) + HPG}"] + 1 - ACC)
                    else:
                        w("acc_mm", 0)
                    w("w_lo", w_at[wname] - 10 + 1)
                    nc.scalar.activation(hi, src, ACT.Copy).then_inc(s["w_hi"].sem, 1)

                def qk_high(a):
                    w("qk_sum", qk_at[a] + 1)
                    w("s_mm", 4 * (int(a[1:]) - 2) if a[0] == "Q" and int(a[1:]) >= 3 else 0)
                    nc.scalar.activation(qk_parts(a)[0], rope_s[:, :], ACT.Copy).then_inc(s["qk_hi"].sem, 1)

                def v_high(half):
                    w("acc_mm", acc_at[f"V{half}"] + 1)
                    w("pv_mm", 0)
                    tiles = slice(half * QT, (half + 1) * QT)
                    nc.scalar.activation(vh[:, tiles, :], acc[acc_at[f"V{half}"] % 2][:, :].rearrange("p (t n) -> p t n", t=QT),
                                         ACT.Copy).then_inc(s["v_hi"].sem, 1)

                def exps(u, n):
                    i, m = ORDER[n], 4 * u + n
                    w("maxed", m + 1)
                    if n == 0:
                        w("t_mm", 4 * (u - 1))
                        w("rinv_ok", u - 1)
                    nc.scalar.activation(probs[:, u % 2, row_off[i]:row_off[i + 1]], sbank[m % 3][:, 0:(i + 1) * P], ACT.Exp,
                                         bias=negmax[:, u, i:i + 1], accum_out=rowsum[:, u, i:i + 1]).then_inc(s["exp_ok"].sem, 1)

                def probs_high(u, j):
                    n = 4 * u + j
                    w("t_mm", n + 1)
                    w("pv_mm", n - 1)
                    cols = slice(j * P, SEQ)
                    nc.scalar.activation(pth[:, n % 2, cols], tbank[n % 2][:, cols], ACT.Copy).then_inc(s["pt_hi"].sem, 1)

                def out_high(u):
                    w("pv_mm", 4 * u + 4)
                    w("acc_mm", -QT if u < HPG else 0)
                    nc.scalar.activation(oth[:, u, :], obank[:, :], ACT.Copy).then_inc(s["o_hi"].sem, 1)

                for wname in W_SEQ[:5]:
                    weight_high(wname)
                for a in ("K0", "K1", "Q0", "Q1"):
                    qk_high(a)
                v_high(0)
                v_high(1)
                for u in range(UNITS + 1):
                    if u < UNITS:
                        exps(u, 0)
                        exps(u, 1)
                        exps(u, 2)
                    if u == 0:
                        weight_high("wq3")
                    if u + 2 < UNITS:
                        qk_high(f"Q{u + 2}")
                    if u < UNITS:
                        exps(u, 3)
                    if u >= 1:
                        for j in range(QT):
                            probs_high(u - 1, j)
                        out_high(u - 1)
                    if 0 <= u < HPG:
                        weight_high(f"wo{u}")

        @block.gpsimd
        def _(pool):
            credit(pool, "qk_sum", "qk_lo", "norm_ok", "w_lo")
            with pool.Fori(0, GROUPS) as g:
                w = waits(pool, g)

                def weight_low(wname):
                    src, hi, lo, _, _, _ = weight_parts(wname)
                    w("w_hi", w_at[wname] + 1)
                    nc.gpsimd.tensor_tensor(lo, src, hi.bitcast(F32), ALU.subtract).then_inc(s["w_lo"].sem, 1)

                def rotate(a):
                    n = qk_at[a]
                    w("acc_out", acc_at[a] + 1)
                    w("qk_lo", n)
                    nc.gpsimd.tensor_tensor(rope_s[:, :], rope_a[:, :], rope_b[:, :], ALU.add).then_inc(s["qk_sum"].sem, 1)
                    w("qk_hi", n + 1)
                    w("qk_sum", n + 1)
                    hi, lo = qk_parts(a)
                    nc.gpsimd.tensor_tensor(lo, rope_s[:, :], hi.bitcast(F32), ALU.subtract).then_inc(s["qk_lo"].sem, 1)

                def normalise(u, n):
                    i = ORDER[n]
                    w("rinv_ok", u + 1)
                    tile = probs[:, u % 2, row_off[i]:row_off[i + 1]]
                    nc.gpsimd.tensor_tensor(tile, tile, rinv[:, u, i:i + 1].broadcast_to([P, (i + 1) * P]), ALU.mult).then_inc(s["norm_ok"].sem, 1)

                for wname in W_SEQ[:5]:
                    weight_low(wname)
                for a in ("K0", "K1", "Q0", "Q1"):
                    rotate(a)
                for u in range(UNITS):
                    if u == 0:
                        weight_low("wq3")
                    if u + 2 < UNITS:
                        rotate(f"Q{u + 2}")
                    for n in range(QT):
                        normalise(u, n)
                    if u < HPG:
                        weight_low(f"wo{u}")

        for n in pers:
            s[n].base += pers[n] * GROUPS
        for n, loads in (("wq0", 2), ("wq1", 2), ("wo0", 2), ("wo1", 2), ("wk", 1), ("wv", 1)):
            d_in[n].base += 16 * loads * GROUPS
        d_in["tab"].base += 32 if tile0_scale else 16
        if tile0_scale:
            swaps.base += GROUPS * UNITS


def experts(k, d):
    nc = k.nc
    E, G, EG = EXPERTS, MGROUPS, EXPERTS // MGROUPS
    with ExitStack() as st:
        def sb(nm, shape, dt=F32):
            return k.sb("mo_" + nm, shape, dt, st)

        rw, rwh, rwl = sb("rw", [P, KT, E]), sb("rwh", [P, KT, E], F32R), sb("rwl", [P, KT, E], F32R)
        rows = sb("rows", [P, 2, E])
        tri_g, tri_e = sb("tri_g", [P, G, G]), sb("tri_e", [P, E, E])
        z = sb("z", [P, TT, E])
        sc = sb("sc", [P, TT, E])
        mx, sm, ri = sb("mx", [P, TT]), sb("sm", [P, TT]), sb("ri", [P, TT])
        gm = sb("gm", [P, TT, G])
        cg, cg2 = sb("cg", [P, TT * G, G]), sb("cg2", [P, TT * G, G])
        rg, keep, pen = sb("rg", [P, TT, G]), sb("keep", [P, TT, G]), sb("pen", [P, TT, G])
        ce, ce2 = sb("ce", [P, TT * E, E]), sb("ce2", [P, TT * E, E])
        re_ = sb("re", [P, TT, E])
        gates = sb("gates", [P, TT, SLABS])
        gates_e = sb("gates_e", [P, SLABS, TT])
        gate = sb("gate", [P, TT])
        gT = sb("gT", [E + 1, TT, P])
        b3 = sb("b3", [E + 1, D])
        w1s, w2s, w3s = sb("w1s", [P, KT, INTER]), sb("w2s", [P, KT, INTER]), sb("w3s", [P, D])
        w1h, w1l = sb("w1h", [P, KT, INTER], F32R), sb("w1l", [P, KT, INTER], F32R)
        w2h, w2l = sb("w2h", [P, KT, INTER], F32R), sb("w2l", [P, KT, INTER], F32R)
        w3h, w3l = sb("w3h", [P, D], F32R), sb("w3l", [P, D], F32R)
        b12s, b12 = sb("b12s", [P, 2]), sb("b12", [P, 2, 2])
        act1 = sb("act1", [P, 2, SEQ])
        hf = sb("hf", [P, 2, SEQ])
        hh, hl = sb("hh", [P, 2, SEQ], F32R), sb("hl", [P, 2, SEQ], F32R)

        chain, r_in, r_split, r_mm, r_exp, g_mm, g_cp, b_mm, b_add = (
            k.sem("mo_" + n) for n in "chain r_in r_split r_mm r_exp g_mm g_cp b_mm b_add".split())
        pers = dict(up_mm=4, out_mm=TT, silu=2, h=2, x_add=TT, gate=1, h_hi=2, h_lo=2, w_hi=3, w_lo=3, b_cp=1)
        s = {n: k.sem("mo_" + n) for n in pers}
        for n in pers:
            s[n].start(pers[n])
        w_in = {n: k.sem("mo_in_" + n) for n in ("w1", "w2", "w3")}
        up = k.bank[0:4]
        ob = k.bank[4:8]
        block = st.enter_context(nc.Block())

        def waits(eng, e):
            def w(n, count):
                eng.wait_ge(s[n].sem, pers[n] * (e + 1) + count)
            return w

        @block.sync
        def _(sp):
            sp.dma_start(rw[:, :, :], d["router_w"]).then_inc(r_in.sem, 16)
            sp.dma_start(rows[:, :, :], d["router_rows"].partition_broadcast(P)).then_inc(r_in.sem, 16)
            sp.dma_start(tri_g[:, :, :], d["tri_g"].partition_broadcast(P)).then_inc(r_in.sem, 16)
            sp.dma_start(tri_e[:, :, :], d["tri_e"].partition_broadcast(P)).then_inc(r_in.sem, 16)
            sp.dma_start(b3[:, :], d["b3"]).then_inc(r_in.sem, 16)
            with sp.Fori(0, SLABS) as e:
                w = waits(sp, e)
                w("w_lo", -2)
                w("b_cp", 0)
                sp.dma_start(w1s[:, :, :], d["ew1"][bass.ds(e, 1)].rearrange("a p k n -> p (a k) n")).then_inc(w_in["w1"].sem, 16)
                sp.dma_start(b12s[:, :], d["eb12"][bass.ds(e, 1)].rearrange("a p n -> p (a n)")).then_inc(w_in["w1"].sem, 16)
                w("w_lo", -1)
                sp.dma_start(w2s[:, :, :], d["ew2"][bass.ds(e, 1)].rearrange("a p k n -> p (a k) n")).then_inc(w_in["w2"].sem, 16)
                w("w_lo", 0)
                sp.dma_start(w3s[:, :], d["ew3"][bass.ds(e, 1)].rearrange("a p n -> p (a n)")).then_inc(w_in["w3"].sem, 16)

        @block.tensor
        def _(pe):
            pe.wait_ge(r_split.sem, 2)
            for t in range(TT):
                for a in range(KT):
                    ins = matmul3(nc, ob[0][:, t * E:(t + 1) * E], k.xTh[:, a, t * P:(t + 1) * P], k.xTl[:, a, t * P:(t + 1) * P],
                                  rwh[:, a, :], rwl[:, a, :], a == 0, a == KT - 1)
            ins.then_inc(r_mm.sem, 1)
            pe.sem_inc(s["up_mm"].sem, 4)
            pe.sem_inc(s["out_mm"].sem, TT)
            with pe.Fori(0, SLABS) as e:
                w = waits(pe, e)
                for half in range(BATCH):
                    tok = slice(half * SEQ, (half + 1) * SEQ)
                    for n, (wh, wl) in enumerate(((w1h, w1l), (w2h, w2l))):
                        w("h", half - 1)
                        w("w_lo", n + 1)
                        for a in range(KT):
                            ins = matmul3(nc, up[2 * half + n][:, :], wh[:, a, :], wl[:, a, :], k.xTh[:, a, tok],
                                          k.xTl[:, a, tok], a == 0, a == KT - 1)
                        ins.then_inc(s["up_mm"].sem, 1)
                w("w_lo", 3)
                for t in range(TT):
                    w("h_lo", t // QT + 1)
                    w("x_add", t - 3)
                    tok = slice((t % QT) * P, (t % QT + 1) * P)
                    matmul3(nc, ob[t % 4][:, :], hh[:, t // QT, tok], hl[:, t // QT, tok], w3h[:, :], w3l[:, :],
                            True, True).then_inc(s["out_mm"].sem, 1)
            for t in range(TT):
                pe.wait_ge(g_cp.sem, t)
                if t == 0:
                    pe.wait_ge(s["h"].sem, 2 * (SLABS + 1))
                    pe.wait_ge(chain.sem, 1)
                nc.tensor.transpose(up[0][0:E + 1, 0:P], gates[:, t, 0:E + 1], k.ident[:, :]).then_inc(g_mm.sem, 1)
            pe.wait_ge(s["x_add"].sem, TT * (SLABS + 1))
            pe.wait_ge(g_cp.sem, TT)
            for t in range(TT):
                if t >= 4:
                    pe.wait_ge(b_add.sem, t - 3)
                nc.tensor.matmul(ob[t % 4][:, :], gT[:, t, :], b3[:, :], start=True, stop=True).then_inc(b_mm.sem, 1)

        steps = [0]

        @block.vector
        def _(dve):
            def link(ins):
                steps[0] += 1
                ins.then_inc(chain.sem, 1)
                dve.wait_ge(chain.sem, steps[0])

            def over(ap, n):
                return ap.unsqueeze(2).broadcast_to([P, ap.shape[1], n])

            flat = lambda t: t[:, :, :].rearrange("p a b -> p (a b)")
            dve.wait_ge(r_in.sem, 80)
            nc.vector.tensor_copy(rwh[:, :, :], rw[:, :, :]).then_inc(r_split.sem, 1)
            dve.wait_ge(r_split.sem, 1)
            nc.vector.tensor_tensor(rwl[:, :, :], rw[:, :, :], rwh[:, :, :].bitcast(F32), ALU.subtract).then_inc(r_split.sem, 1)
            dve.wait_ge(r_mm.sem, 1)
            link(nc.vector.tensor_tensor(z[:, :, :], ob[0][:, 0:TT * E].rearrange("p (t e) -> p t e", t=TT),
                                         rows[:, 0:1, :].broadcast_to([P, TT, E]), ALU.add))
            link(nc.vector.tensor_reduce(mx[:, :], z[:, :, :], AX, ALU.max))
            link(nc.vector.tensor_tensor(z[:, :, :], z[:, :, :], over(mx[:, :], E), ALU.subtract))
            dve.wait_ge(r_exp.sem, 1)
            link(nc.vector.tensor_reduce(sm[:, :], sc[:, :, :], AX, ALU.add))
            link(nc.vector.reciprocal(ri[:, :], sm[:, :]))
            link(nc.vector.tensor_tensor(sc[:, :, :], sc[:, :, :], over(ri[:, :], E), ALU.mult))
            link(nc.vector.tensor_tensor(sc[:, :, :], sc[:, :, :], rows[:, 1:2, :].broadcast_to([P, TT, E]), ALU.add))
            link(nc.vector.tensor_reduce(gm[:, :, :], sc[:, :, :].rearrange("p t (g n) -> p t g n", g=G), AX, ALU.max))

            def choose(vals, n, cmp, cmp2, tri, rank, chosen, limit):
                mine = vals[:, :, :].rearrange("p t n -> p (t n)").unsqueeze(2).broadcast_to([P, TT * n, n])
                for t in range(TT):
                    theirs = vals[:, t:t + 1, :].broadcast_to([P, n, n])
                    own = mine[:, t * n:(t + 1) * n, :]
                    nc.vector.tensor_tensor(cmp[:, t * n:(t + 1) * n, :], theirs, own, ALU.is_gt)
                    ins = nc.vector.tensor_tensor(cmp2[:, t * n:(t + 1) * n, :], theirs, own, ALU.is_equal)
                link(ins)
                for t in range(TT):
                    ins = nc.vector.tensor_tensor(cmp2[:, t * n:(t + 1) * n, :], cmp2[:, t * n:(t + 1) * n, :], tri[:, :, :], ALU.mult)
                link(ins)
                link(nc.vector.tensor_tensor(cmp[:, :, :], cmp[:, :, :], cmp2[:, :, :], ALU.add))
                link(nc.vector.tensor_reduce(rank[:, :, :].rearrange("p t n -> p (t n)"), cmp[:, :, :], AX, ALU.add))
                link(nc.vector.tensor_scalar(chosen[:, :, :], rank[:, :, :], float(limit), None, ALU.is_lt))

            choose(gm, G, cg, cg2, tri_g, rg, keep, 2)
            link(nc.vector.tensor_scalar(pen[:, :, :], keep[:, :, :], -MASKED, MASKED, ALU.mult, ALU.add))
            link(nc.vector.tensor_tensor(z[:, :, :].rearrange("p t (g n) -> p (t g) n", g=G),
                                         sc[:, :, :].rearrange("p t (g n) -> p (t g) n", g=G), over(flat(keep), EG), ALU.mult))
            link(nc.vector.tensor_tensor(z[:, :, :].rearrange("p t (g n) -> p (t g) n", g=G),
                                         z[:, :, :].rearrange("p t (g n) -> p (t g) n", g=G), over(flat(pen), EG), ALU.add))
            choose(z, E, ce, ce2, tri_e, re_, re_, 2)
            nc.vector.memset(gates[:, :, E:SLABS], 1.0)
            link(nc.vector.tensor_tensor(gates[:, :, 0:E], sc[:, :, :], re_[:, :, :], ALU.mult))
            link(nc.vector.tensor_copy(gates_e[:, :, :], gates[:, :, :].rearrange("p t e -> p e t")))

            for n in ("h", "x_add", "gate"):
                dve.sem_inc(s[n].sem, pers[n])
            with dve.Fori(0, SLABS) as e:
                w = waits(dve, e)
                w("x_add", 0)
                nc.vector.tensor_copy(gate[:, :], gates_e[:, bass.ds(e, 1), :].rearrange("p a t -> p (a t)")).then_inc(s["gate"].sem, 1)
                for half in range(BATCH):
                    w("silu", half + 1)
                    w("up_mm", 2 * half + 2)
                    w("h_lo", half - 1)
                    nc.vector.scalar_tensor_tensor(out=hf[:, half, :], in0=up[2 * half + 1][:, :], scalar=b12[:, 1, 0:1],
                                                   in1=act1[:, half, :], op0=ALU.add, op1=ALU.mult).then_inc(s["h"].sem, 1)
                w("gate", 1)
                for t in range(TT):
                    w("out_mm", t + 1)
                    nc.vector.scalar_tensor_tensor(out=k.x[:, t, :], in0=ob[t % 4][:, :], scalar=gate[:, t:t + 1],
                                                   in1=k.x[:, t, :], op0=ALU.mult, op1=ALU.add).then_inc(s["x_add"].sem, 1)
            for t in range(TT):
                dve.wait_ge(g_mm.sem, t + 1)
                nc.vector.tensor_copy(gT[:, t, :], up[0][0:E + 1, 0:P]).then_inc(g_cp.sem, 1)
            for t in range(TT):
                dve.wait_ge(b_mm.sem, t + 1)
                nc.vector.tensor_tensor(k.x[:, t, :], ob[t % 4][:, :], k.x[:, t, :], ALU.add).then_inc(b_add.sem, 1)

        @block.scalar
        def _(act):
            act.wait_ge(chain.sem, 3)
            nc.scalar.activation(sc[:, :, :], z[:, :, :], ACT.Exp).then_inc(r_exp.sem, 1)
            for n in ("silu", "h_hi", "w_hi", "b_cp"):
                act.sem_inc(s[n].sem, pers[n])
            with act.Fori(0, SLABS) as e:
                w = waits(act, e)

                def weight_high(n, src, hi):
                    act.wait_ge(w_in[f"w{n + 1}"].sem, (32 if n == 0 else 16) * (e + 1))
                    w("up_mm", (-1, 0)[n]) if n < 2 else w("out_mm", 0)
                    w("w_lo", n + 1 - 3)
                    nc.scalar.activation(hi, src, ACT.Copy).then_inc(s["w_hi"].sem, 1)

                weight_high(0, w1s[:, :, :], w1h[:, :, :])
                w("h", 0)
                nc.scalar.activation(b12[:, :, 0], b12s[:, :], ACT.Copy).then_inc(s["b_cp"].sem, 1)
                weight_high(1, w2s[:, :, :], w2h[:, :, :])
                w("b_cp", 1)
                for half in range(BATCH):
                    w("up_mm", 2 * half + 1)
                    w("h", half - 1)
                    nc.scalar.activation(act1[:, half, :], up[2 * half][:, :], ACT.Silu, bias=b12[:, 0, 0:1]).then_inc(s["silu"].sem, 1)
                    if half == 0:
                        weight_high(2, w3s[:, :], w3h[:, :])
                for half in range(BATCH):
                    w("h", half + 1)
                    w("out_mm", -4 if half == 0 else 0)
                    nc.scalar.activation(hh[:, half, :], hf[:, half, :], ACT.Copy).then_inc(s["h_hi"].sem, 1)

        @block.gpsimd
        def _(pool):
            for n in ("h_lo", "w_lo"):
                pool.sem_inc(s[n].sem, pers[n])
            with pool.Fori(0, SLABS) as e:
                w = waits(pool, e)

                def weight_low(n, src, hi, lo):
                    w("w_hi", n + 1)
                    nc.gpsimd.tensor_tensor(lo, src, hi.bitcast(F32), ALU.subtract).then_inc(s["w_lo"].sem, 1)

                weight_low(0, w1s[:, :, :], w1h[:, :, :], w1l[:, :, :])
                weight_low(1, w2s[:, :, :], w2h[:, :, :], w2l[:, :, :])
                weight_low(2, w3s[:, :], w3h[:, :], w3l[:, :])
                for half in range(BATCH):
                    w("h_hi", half + 1)
                    nc.gpsimd.tensor_tensor(hl[:, half, :], hf[:, half, :], hh[:, half, :].bitcast(F32), ALU.subtract).then_inc(s["h_lo"].sem, 1)


def narrow_attention(k, name, turns, dh, causal, qr, kr, vr, outs, shared_kv, divisor):
    nc = k.nc
    UNITS, TILES = 8, 2
    PRE = 2 * TILES
    TR = PRE + 4 * UNITS
    SM = 4 * UNITS
    keys = [(i + 1) * P if causal else SEQ for i in range(QT)]
    first = [j if causal else 0 for j in range(QT)]
    row_off = [sum(keys[:i]) for i in range(QT + 1)]
    col_off = [sum((QT - first[m]) * P for m in range(j)) for j in range(QT + 1)]
    ORDER = [3, 2, 1, 0]
    with ExitStack() as st:
        def sb(nm, shape, dt=F32):
            return k.sb(name + nm, shape, dt, st)

        qst, kst = sb("qst", [P, TILES, QT, 4, 32]), sb("kst", [P, TILES, QT, 4, 32])
        vst = sb("vst", [P, TILES, QT, dh] if shared_kv else [P, QT, UNITS * dh])
        qT, kT = sb("qT", [P, TILES, SEQ]), sb("kT", [P, TILES, SEQ])
        probs, pt = sb("probs", [P, 2, row_off[QT]]), sb("pt", [P, 2, col_off[QT]])
        negmax = sb("negmax", [P, QT, UNITS])
        rowsum, rinv = sb("rowsum", [P, QT, UNITS]), sb("rinv", [P, QT, UNITS])
        sbank, tbank, obank = k.bank[0:3], k.bank[3:6], k.bank[6]
        pers = dict(s_mm=SM, t_mm=TR, pv_mm=UNITS, maxed=SM, t_dve=TR // 2, o_norm=1, rinv_ok=2,
                    exp_ok=SM, t_act=TR // 2, staged=5)
        s = {n: k.sem("na_" + n) for n in pers}
        due = {n: s[n].start(pers[n]) for n in pers}
        base = {n: s[n].base for n in pers}
        zeroed = k.sem("na_zeroed")
        z0 = zeroed.base
        block = st.enter_context(nc.Block())

        def credit(eng, *names):
            for n in names:
                if due[n]:
                    eng.sem_inc(s[n].sem, pers[n])

        def waits(eng, g):
            def w(n, count):
                eng.wait_ge(s[n].sem, base[n] + pers[n] * (g + 1) + count)
            return w

        def copied(w, n):
            w("t_act" if n % 2 == 0 else "t_dve", n // 2 + 1)

        def copy_out(eng_copy, w, n):
            w("t_mm", n + 1)
            if n < PRE:
                w("s_mm", 0)
                dst = (qT, kT)[n % 2][:, n // 2, :]
                return eng_copy(dst, tbank[n % 3][:, :])
            u, j = (n - PRE) // 4, (n - PRE) % 4
            w("pv_mm", u - 1)
            return eng_copy(pt[:, u % 2, col_off[j]:col_off[j + 1]], tbank[n % 3][:, first[j] * P:SEQ])

        @block.gpsimd
        def _(pool):
            nc.gpsimd.memset(qst[:, :, :, :, :], 0.0)
            nc.gpsimd.memset(kst[:, :, :, :, :], 0.0).then_inc(zeroed.sem, 1)
            credit(pool, "staged")
            pool.wait_ge(zeroed.sem, z0 + 1)
            with pool.Fori(0, turns) as g:
                w = waits(pool, g)
                for a in range(TILES):
                    w("t_mm", 2 * a + 2 - TR)
                    nc.gpsimd.tensor_copy(qst[:, a, :, :, 0:dh].rearrange("p t h e -> p (t h) e"),
                                          qr[:, bass.ds(g, 1), a, :, :, :].rearrange("p g t h e -> p (g t h) e")).then_inc(s["staged"].sem, 1)
                    if shared_kv:
                        src = kr[:, bass.ds(g, 1), a, :, :].rearrange("p g t e -> p (g t) e").unsqueeze(2).broadcast_to([P, QT, 4, dh])
                        dst = kst[:, a, :, :, 0:dh]
                    else:
                        src = kr[:, bass.ds(g, 1), a, :, :, :].rearrange("p g t h e -> p (g t h) e")
                        dst = kst[:, a, :, :, 0:dh].rearrange("p t h e -> p (t h) e")
                    nc.gpsimd.tensor_copy(dst, src).then_inc(s["staged"].sem, 1)
                w("pv_mm", 0)
                if shared_kv:
                    nc.gpsimd.tensor_copy(vst[:, :, :, :].rearrange("p a t e -> p (a t e)"),
                                          vr[:, bass.ds(g, 1), :, :, :].rearrange("p g a t e -> p (g a t e)")).then_inc(s["staged"].sem, 1)
                else:
                    nc.gpsimd.tensor_copy(vst[:, :, :].rearrange("p t e -> p (t e)"),
                                          vr[:, bass.ds(g, 1), :, :].rearrange("p g t e -> p (g t e)")).then_inc(s["staged"].sem, 1)

        @block.tensor
        def _(pe):
            credit(pe, "s_mm", "t_mm", "pv_mm")
            with pe.Fori(0, turns) as g:
                w = waits(pe, g)

                def scores(u, n):
                    i, m, a, p0 = ORDER[n], 4 * u + n, u // 4, 32 * (u % 4)
                    w("exp_ok", m - 2 if m >= 3 else 0)
                    if n == 0:
                        copied(w, 2 * a)
                        copied(w, 2 * a + 1)
                    ins = nc.tensor.matmul(sbank[m % 3][:, 0:keys[i]], qT[p0:p0 + dh, a, i * P:(i + 1) * P],
                                           kT[p0:p0 + dh, a, 0:keys[i]], start=True, stop=not causal)
                    if causal:
                        ins = nc.tensor.matmul(sbank[m % 3][:, i * P:keys[i]], k.identb[:, :], k.maskb[:, :],
                                               start=False, stop=True)
                    ins.then_inc(s["s_mm"].sem, 1)

                def turn_probs(u, j):
                    n = PRE + 4 * u + j
                    copied(w, n - 3)
                    if j == 0:
                        w("exp_ok", 4 * u + 4)
                    for i in range(first[j], QT):
                        ins = nc.tensor.transpose(tbank[n % 3][:, i * P:(i + 1) * P],
                                                  probs[:, u % 2, row_off[i] + j * P:row_off[i] + (j + 1) * P], k.ident[:, :])
                    ins.then_inc(s["t_mm"].sem, 1)

                def values(u):
                    copied(w, PRE + 4 * u + 2)
                    copied(w, PRE + 4 * u + 3)
                    if u == 0:
                        w("staged", 5)
                        w("o_norm", 0)
                    for i in range(QT):
                        out = obank[:, (i * UNITS + u) * dh:(i * UNITS + u + 1) * dh]
                        seen = keys[i] // P
                        for j in range(seen):
                            at = col_off[j] + (i - first[j]) * P
                            v = vst[:, u // 4, j, :] if shared_kv else vst[:, j, u * dh:(u + 1) * dh]
                            ins = nc.tensor.matmul(out, pt[:, u % 2, at:at + P], v, start=(j == 0), stop=(j == seen - 1))
                    ins.then_inc(s["pv_mm"].sem, 1)

                for n in range(PRE):
                    src = (qst, kst)[n % 2]
                    copied(w, n - 3)
                    w("staged", n + 1)
                    for t in range(QT):
                        ins = nc.tensor.transpose(tbank[n % 3][:, t * P:(t + 1) * P],
                                                  src[:, n // 2, t, :, :].rearrange("p h e -> p (h e)"), k.ident[:, :])
                    ins.then_inc(s["t_mm"].sem, 1)
                for u in range(UNITS + 2):
                    if u < UNITS:
                        scores(u, 0)
                        scores(u, 1)
                    if 1 <= u <= UNITS:
                        turn_probs(u - 1, 0)
                        turn_probs(u - 1, 1)
                    if u < UNITS:
                        scores(u, 2)
                    if 1 <= u <= UNITS:
                        turn_probs(u - 1, 2)
                        turn_probs(u - 1, 3)
                    if u < UNITS:
                        scores(u, 3)
                    if u >= 2:
                        values(u - 2)

        @block.vector
        def _(dve):
            credit(dve, "maxed", "t_dve", "o_norm", "rinv_ok")
            with dve.Fori(0, turns) as g:
                w = waits(dve, g)

                def row_max(u, n):
                    i, m = ORDER[n], 4 * u + n
                    w("s_mm", m + 1)
                    nc.vector.tensor_reduce(negmax[:, i, u:u + 1], sbank[m % 3][:, 0:keys[i]], AX, ALU.max,
                                            negate=True).then_inc(s["maxed"].sem, 1)

                def copy(n):
                    copy_out(nc.vector.tensor_copy, w, n).then_inc(s["t_dve"].sem, 1)

                copy(1)
                copy(3)
                for u in range(UNITS + 1):
                    if u < UNITS:
                        row_max(u, 0)
                        row_max(u, 1)
                    if u >= 1:
                        copy(PRE + 4 * (u - 1) + 1)
                    if u < UNITS:
                        row_max(u, 2)
                    if u >= 1:
                        copy(PRE + 4 * (u - 1) + 3)
                    if u < UNITS:
                        row_max(u, 3)
                w("exp_ok", SM)
                nc.vector.tensor_scalar(rinv[:, :, :], rowsum[:, :, :], float(divisor), None, ALU.mult).then_inc(s["rinv_ok"].sem, 1)
                w("rinv_ok", 1)
                nc.vector.reciprocal(rinv[:, :, :], rinv[:, :, :]).then_inc(s["rinv_ok"].sem, 1)
                w("pv_mm", UNITS)
                w("rinv_ok", 2)
                nc.vector.tensor_tensor(outs(g), obank[:, 0:QT * UNITS * dh].rearrange("p (m h e) -> p m h e", h=4, e=dh),
                                        rinv[:, :, :].rearrange("p i (b h) -> p (i b) h", h=4).unsqueeze(3).broadcast_to([P, 2 * QT, 4, dh]),
                                        ALU.mult).then_inc(s["o_norm"].sem, 1)

        @block.scalar
        def _(act):
            credit(act, "exp_ok", "t_act")
            with act.Fori(0, turns) as g:
                w = waits(act, g)

                def exps(u, n):
                    i, m = ORDER[n], 4 * u + n
                    w("maxed", m + 1)
                    if n == 0:
                        w("t_mm", 4 * u - 4 if u < 2 else 4 * u)
                        w("o_norm", 0)
                    nc.scalar.activation(probs[:, u % 2, row_off[i]:row_off[i + 1]], sbank[m % 3][:, 0:keys[i]], ACT.Exp,
                                         bias=negmax[:, i, u:u + 1], accum_out=rowsum[:, i, u:u + 1]).then_inc(s["exp_ok"].sem, 1)

                def copy(n):
                    copy_out(lambda o, i: nc.scalar.activation(o, i, ACT.Copy), w, n).then_inc(s["t_act"].sem, 1)

                copy(0)
                copy(2)
                for u in range(UNITS + 1):
                    if u < UNITS:
                        exps(u, 0)
                        exps(u, 1)
                    if u >= 1:
                        copy(PRE + 4 * (u - 1))
                    if u < UNITS:
                        exps(u, 2)
                    if u >= 1:
                        copy(PRE + 4 * (u - 1) + 2)
                    if u < UNITS:
                        exps(u, 3)

        for n in pers:
            s[n].base += pers[n] * turns
        zeroed.base += 1


def narrow_layer0(k, d):
    nc = k.nc
    DH, H, NQKV, RANKS = 8, 8, 192, 48
    with ExitStack() as outer:
        def keep(nm, shape, dt=F32):
            return k.sb("n0" + nm, shape, dt, outer)

        qr, kr = keep("qr", [P, BATCH, 2, QT, 4, DH]), keep("kr", [P, BATCH, 2, QT, 4, DH])
        vr = keep("vr", [P, BATCH, QT, H * DH])
        outs = keep("outs", [P, BATCH, QT * H, DH])
        wo = keep("wo", [H * DH, D])
        with ExitStack() as st:
            def sb(nm, shape, dt=F32):
                return k.sb("n0" + nm, shape, dt, st)

            wa, wah, wal = sb("wa", [P, KT, NQKV]), sb("wah", [P, KT, NQKV], F32R), sb("wal", [P, KT, NQKV], F32R)
            wf, wfh, wfl = sb("wf", [P, KT, D]), sb("wfh", [P, KT, D], F32R), sb("wfl", [P, KT, D], F32R)
            la, lah, lal = sb("la", [P, KT, P]), sb("lah", [P, KT, P], F32R), sb("lal", [P, KT, P], F32R)
            lb = sb("lb", [66, D])
            uT = sb("uT", [66, TOK])
            qkvb = sb("qkvb", [P, NQKV])
            starts, startsf, cmp = sb("starts", [P, 4], I32), sb("startsf", [P, 4]), sb("cmp", [P, BATCH, 4])
            cnt, kcol, amask = sb("cnt", [P, BATCH]), sb("kcol", [P, 1]), sb("amask", [P, BATCH])
            a_in, f_in, c_in, hi, lo, chain, q_mm, q_out, u_mm, u_out, y_mm, y_out, ones = (
                k.sem("n0_" + n) for n in "a_in f_in c_in hi lo chain q_mm q_out u_mm u_out y_mm y_add ones".split())
            parts = ((wa, wah, wal), (la, lah, lal), (wf, wfh, wfl))
            block = st.enter_context(nc.Block())

            @block.sync
            def _(sp):
                sp.dma_start(wa[:, :, :], d["L0_wqkv"]).then_inc(a_in.sem, 16)
                sp.dma_start(la[:, :, :], d["L0_la"]).then_inc(f_in.sem, 16)
                sp.dma_start(wf[:, :, :], d["L0_wf"]).then_inc(f_in.sem, 16)
                sp.dma_start(lb[:, :], d["L0_lb"]).then_inc(c_in.sem, 16)
                sp.dma_start(qkvb[:, :], d["L0_qkvb"].partition_broadcast(P)).then_inc(c_in.sem, 16)
                sp.dma_start(starts[:, :], d["L0_starts"].partition_broadcast(P)).then_inc(c_in.sem, 16)
                sp.dma_start(kcol[:, :], d["L0_kcol"]).then_inc(c_in.sem, 16)
                sp.dma_start(wo[:, :], d["L0_wo"]).then_inc(c_in.sem, 16)

            @block.scalar
            def _(act):
                act.wait_ge(a_in.sem, 16)
                for n, (src, h, _) in enumerate(parts):
                    if n == 1:
                        act.wait_ge(f_in.sem, 32)
                    nc.scalar.activation(h[:, :, :], src[:, :, :], ACT.Copy).then_inc(hi.sem, 1)

            @block.gpsimd
            def _(pool):
                for n, (src, h, l) in enumerate(parts):
                    pool.wait_ge(hi.sem, n + 1)
                    nc.gpsimd.tensor_tensor(l[:, :, :], src[:, :, :], h[:, :, :].bitcast(F32), ALU.subtract).then_inc(lo.sem, 1)

            @block.tensor
            def _(pe):
                pe.wait_ge(lo.sem, 1)
                for t in range(TT):
                    if t >= 2:
                        pe.wait_ge(q_out.sem, t - 1)
                    tok = slice(t * P, (t + 1) * P)
                    for a in range(KT):
                        ins = matmul3(nc, k.bank[t % 2][:, 0:NQKV], k.xTh[:, a, tok], k.xTl[:, a, tok],
                                      wah[:, a, :], wal[:, a, :], a == 0, a == KT - 1)
                    ins.then_inc(q_mm.sem, 1)
                pe.wait_ge(lo.sem, 2)
                for b in range(BATCH):
                    tok = slice(b * SEQ, (b + 1) * SEQ)
                    for a in range(KT):
                        ins = matmul3(nc, k.bank[2 + b][:, :], lah[:, a, :], lal[:, a, :], k.xTh[:, a, tok],
                                      k.xTl[:, a, tok], a == 0, a == KT - 1)
                    ins.then_inc(u_mm.sem, 1)
                pe.wait_ge(lo.sem, 3)
                pe.wait_ge(ones.sem, 1)
                pe.wait_ge(c_in.sem, 80)
                for t in range(TT):
                    if t >= 4:
                        pe.wait_ge(y_out.sem, t - 3)
                    tok, bank = slice(t * P, (t + 1) * P), k.bank[4 + t % 4]
                    for a in range(KT):
                        matmul3(nc, bank[:, :], k.xTh[:, a, tok], k.xTl[:, a, tok], wfh[:, a, :], wfl[:, a, :], a == 0, False)
                    pe.wait_ge(u_out.sem, t // QT + 1)
                    nc.tensor.matmul(bank[:, :], uT[:, tok], lb[:, :], start=False, stop=True).then_inc(y_mm.sem, 1)

            @block.vector
            def _(dve):
                steps = [0]

                def link(ins):
                    steps[0] += 1
                    ins.then_inc(chain.sem, 1)
                    dve.wait_ge(chain.sem, steps[0])

                nc.vector.memset(uT[64:66, :], 1.0).then_inc(ones.sem, 1)
                dve.wait_ge(c_in.sem, 80)
                link(nc.vector.tensor_copy(startsf[:, :], starts[:, :]))
                for b in range(BATCH):
                    ins = nc.vector.tensor_scalar(cmp[:, b, :], startsf[:, :], float(b), None, ALU.is_le)
                link(ins)
                link(nc.vector.tensor_reduce(cnt[:, :], cmp[:, :, :], AX, ALU.add))
                link(nc.vector.tensor_tensor(amask[:, :], cnt[:, :], kcol[:, :].broadcast_to([P, BATCH]), ALU.is_equal))
                for t in range(TT):
                    b, tt = t // QT, t % QT
                    dve.wait_ge(q_mm.sem, t + 1)
                    qk = k.bank[t % 2][:, 0:P].rearrange("p (a h e z) -> p a h e z", a=2, h=4, e=DH)
                    qb = qkvb[:, 0:P].rearrange("p (a h e z) -> p a h e z", a=2, h=4, e=DH)
                    for z, dst in ((0, qr), (1, kr)):
                        nc.vector.tensor_tensor(dst[:, b, :, tt, :, :], qk[:, :, :, :, z], qb[:, :, :, :, z], ALU.add)
                    nc.vector.tensor_tensor(vr[:, b, tt, :], k.bank[t % 2][:, P:NQKV], qkvb[:, P:NQKV], ALU.add).then_inc(q_out.sem, 1)
                for b in range(BATCH):
                    dve.wait_ge(u_mm.sem, b + 1)
                    nc.vector.tensor_scalar(uT[0:64, b * SEQ:(b + 1) * SEQ], k.bank[2 + b][0:64, :], amask[0:64, b:b + 1], None,
                                            ALU.mult).then_inc(u_out.sem, 1)
                for t in range(TT):
                    dve.wait_ge(y_mm.sem, t + 1)
                    nc.vector.tensor_tensor(k.x[:, t, :], k.bank[4 + t % 4][:, :], k.x[:, t, :], ALU.add).then_inc(y_out.sem, 1)

        def turn_outs(g):
            return outs[:, bass.ds(g, 1), :, :].rearrange("p g (m h) e -> p (g m) h e", h=4)

        narrow_attention(k, "n0", BATCH, DH, False, qr, kr, vr, turn_outs, False, float(H * DH) ** 0.5)
        project_narrow(k, "n0", wo, 1, H * DH, lambda t, a: outs[:, t // QT, (t % QT) * H:(t % QT + 1) * H, :].rearrange("p h e -> p (h e)"))


def project_narrow(k, name, wo, chunks, rows, piece):
    nc = k.nc
    with ExitStack() as st:
        oT = k.sb(name + "oT", [rows, 2, chunks, P], F32, st)
        turned, copied, mm, added = (k.sem("pn_" + n) for n in "turned copied mm added".split())
        b = [s.base for s in (turned, copied, mm, added)]
        block = st.enter_context(nc.Block())

        @block.tensor
        def _(pe):
            def turn(t):
                if t >= 2:
                    pe.wait_ge(copied.sem, b[1] + t - 1)
                for a in range(chunks):
                    ins = nc.tensor.transpose(k.bank[t % 2][0:rows, a * P:(a + 1) * P], piece(t, a), k.ident[:, :])
                ins.then_inc(turned.sem, 1)

            turn(0)
            for t in range(TT):
                if t + 1 < TT:
                    turn(t + 1)
                pe.wait_ge(copied.sem, b[1] + t + 1)
                if t >= 4:
                    pe.wait_ge(added.sem, b[3] + t - 3)
                for a in range(chunks):
                    w = wo[:, :] if chunks == 1 else wo[:, a, :]
                    ins = nc.tensor.matmul(k.bank[4 + t % 4][:, :], oT[:, t % 2, a, :], w, start=(a == 0), stop=(a == chunks - 1))
                ins.then_inc(mm.sem, 1)

        @block.scalar
        def _(act):
            for t in range(TT):
                act.wait_ge(turned.sem, b[0] + t + 1)
                if t >= 2:
                    act.wait_ge(mm.sem, b[2] + t - 1)
                nc.scalar.activation(oT[:, t % 2, :, :], k.bank[t % 2][0:rows, 0:chunks * P].rearrange("p (a q) -> p a q", a=chunks),
                                     ACT.Copy).then_inc(copied.sem, 1)

        @block.vector
        def _(dve):
            for t in range(TT):
                dve.wait_ge(mm.sem, b[2] + t + 1)
                nc.vector.tensor_tensor(k.x[:, t, :], k.bank[4 + t % 4][:, :], k.x[:, t, :], ALU.add).then_inc(added.sem, 1)

        for s in (turned, copied, mm, added):
            s.base += TT


def narrow_attention2(k, d):
    nc = k.nc
    DH, H, G = 16, 32, 8
    NQ, NKV = H * DH, 2 * G * DH
    with ExitStack() as outer:
        def keep(nm, shape, dt=F32):
            return k.sb("n2" + nm, shape, dt, outer)

        qr = keep("qr", [P, G, BATCH, QT, 4, DH])
        kr, vr = keep("kr", [P, G, BATCH, QT, DH]), keep("vr", [P, G, BATCH, QT, DH])
        outs = keep("outs", [P, QT * BATCH, G, 4 * DH])
        wo = keep("wo", [P, KT, D])
        with ExitStack() as st:
            def sb(nm, shape, dt=F32):
                return k.sb("n2" + nm, shape, dt, st)

            NW = NQ + NKV
            wa, wah, wal = sb("wa", [P, KT, NW]), sb("wah", [P, KT, NW], F32R), sb("wal", [P, KT, NW], F32R)
            tab = sb("tab", [P, QT, 4, DH])
            ra, rb = sb("ra", [P, 2, NQ + G * DH]), sb("rb", [P, 2, NQ + G * DH])
            a_in, c_in, hi, lo, mm, rot, summed = (k.sem("n2_" + n) for n in "a_in c_in hi lo mm rot summed".split())
            block = st.enter_context(nc.Block())

            @block.sync
            def _(sp):
                sp.dma_start(wa[:, :, :], d["L2_wqkv"]).then_inc(a_in.sem, 16)
                sp.dma_start(tab[:, :, :, :], d["L2_tab"]).then_inc(c_in.sem, 16)
                sp.dma_start(wo[:, :, :], d["L2_wo"]).then_inc(c_in.sem, 16)

            @block.scalar
            def _(act):
                act.wait_ge(a_in.sem, 16)
                for a in range(KT):
                    nc.scalar.activation(wah[:, a, :], wa[:, a, :], ACT.Copy).then_inc(hi.sem, 1)

            @block.tensor
            def _(pe):
                for t in range(TT):
                    if t >= 2:
                        pe.wait_ge(rot.sem, t - 1)
                    tok = slice(t * P, (t + 1) * P)
                    for a in range(KT):
                        if t == 0:
                            pe.wait_ge(lo.sem, a + 1)
                        q, kv = k.bank[2 * (t % 2)][:, :], k.bank[2 * (t % 2) + 1][:, 0:NKV]
                        matmul3(nc, q, k.xTh[:, a, tok], k.xTl[:, a, tok], wah[:, a, 0:NQ], wal[:, a, 0:NQ], a == 0, a == KT - 1)
                        ins = matmul3(nc, kv, k.xTh[:, a, tok], k.xTl[:, a, tok], wah[:, a, NQ:], wal[:, a, NQ:], a == 0, a == KT - 1)
                    ins.then_inc(mm.sem, 1)

            @block.vector
            def _(dve):
                for a in range(KT):
                    dve.wait_ge(hi.sem, a + 1)
                    nc.vector.tensor_tensor(wal[:, a, :], wa[:, a, :], wah[:, a, :].bitcast(F32), ALU.subtract).then_inc(lo.sem, 1)
                dve.wait_ge(c_in.sem, 32)
                for t in range(TT):
                    dve.wait_ge(mm.sem, t + 1)
                    if t >= 2:
                        dve.wait_ge(summed.sem, t - 1)
                    nc.vector.tensor_copy(vr[:, :, t // QT, t % QT, :],
                                          k.bank[2 * (t % 2) + 1][:, G * DH:NKV].rearrange("p (g e) -> p g e", g=G))
                    HF = DH // 2
                    for bank, heads, c, at in ((k.bank[2 * (t % 2)], H, 0, 0), (k.bank[2 * (t % 2) + 1], G, 2, NQ)):
                        src = bank[:, 0:heads * DH].rearrange("p (h e) -> p h e", h=heads)
                        a_ = ra[:, t % 2, at:at + heads * DH].rearrange("p (h e) -> p h e", h=heads)
                        b_ = rb[:, t % 2, at:at + heads * DH].rearrange("p (h e) -> p h e", h=heads)
                        cos = tab[:, t % QT, c:c + 1, :].broadcast_to([P, heads, DH])
                        sin = tab[:, t % QT, c + 1:c + 2, :].broadcast_to([P, heads, DH])
                        nc.vector.tensor_tensor(a_, src, cos, ALU.mult)
                        nc.vector.tensor_tensor(b_[:, :, 0:HF], src[:, :, HF:DH], sin[:, :, 0:HF], ALU.mult)
                        ins = nc.vector.tensor_tensor(b_[:, :, HF:DH], src[:, :, 0:HF], sin[:, :, HF:DH], ALU.mult)
                    ins.then_inc(rot.sem, 1)

            @block.gpsimd
            def _(pool):
                for t in range(TT):
                    pool.wait_ge(rot.sem, t + 1)
                    b, tt = t // QT, t % QT
                    nc.gpsimd.tensor_tensor(qr[:, :, b, tt, :, :].rearrange("p g h e -> p g (h e)"),
                                            ra[:, t % 2, 0:NQ].rearrange("p (g e) -> p g e", g=G),
                                            rb[:, t % 2, 0:NQ].rearrange("p (g e) -> p g e", g=G), ALU.add)
                    nc.gpsimd.tensor_tensor(kr[:, :, b, tt, :], ra[:, t % 2, NQ:].rearrange("p (g e) -> p g e", g=G),
                                            rb[:, t % 2, NQ:].rearrange("p (g e) -> p g e", g=G), ALU.add).then_inc(summed.sem, 1)

        def turn_outs(g):
            return outs[:, :, bass.ds(g, 1), :].rearrange("p m g (h e) -> p (m g) h e", h=4)

        narrow_attention(k, "n2", G, DH, True, qr, kr, vr, turn_outs, True, 1.0)

        def piece(t, a):
            m = (t % QT) * BATCH + t // QT
            return outs[:, m, 2 * a:2 * a + 2, :].rearrange("p g e -> p (g e)")

        project_narrow(k, "n2", wo, KT, P, piece)


def memory_ffn(k, d, name):
    nc = k.nc
    with ExitStack() as st:
        def sb(nm, shape, dt=F32):
            return k.sb(name + "m_" + nm, shape, dt, st)

        wq, wqh, wql = sb("wq", [P, KT, P]), sb("wqh", [P, KT, P], F32R), sb("wql", [P, KT, P], F32R)
        wu, wuh, wul = sb("wu", [P, KT, P]), sb("wuh", [P, KT, P], F32R), sb("wul", [P, KT, P], F32R)
        wr = sb("wr", [BOT, BOT])
        keysT = sb("keysT", [BOT, NSLOT])
        rkT, keysA = sb("rkT", [BOT + 1, NSLOT]), sb("keysA", [BOT + 1, NSLOT])
        qA, rqA = sb("qA", [BOT + 1, TOK]), sb("rqA", [BOT + 1, TOK])
        valsT, wvd, wvu = sb("valsT", [P, KT, NSLOT]), sb("wvd", [P, KT, VB]), sb("wvu", [VB, D])
        vw, mix = sb("vw", [VB, NSLOT]), sb("mix", [NSLOT, D])
        bu1, wu2 = sb("bu1", [P, 1]), sb("wu2", [P, 1])
        scal = sb("scal", [P, 3])
        ones = sb("ones", [P, P])
        gl = sb("gl", [P, TOK])
        lv, lsum, rl = sb("lv", [P, TT]), sb("lsum", [P, 1]), sb("rl", [P, 1])
        sg, u, gate, ge, fac = sb("sg", [P, TT]), sb("u", [P, TT]), sb("gate", [P, TT]), sb("ge", [P, TT]), sb("fac", [P, TT])
        top, rep = sb("top", [P, TT, TOPK]), sb("rep", [P, 2, NSLOT])
        att = sb("att", [P, 2, NSLOT])
        negmax, rowsum, rinv = sb("negmax", [P, TT]), sb("rowsum", [P, TT]), sb("rinv", [P, TT])
        wts, wT = sb("wts", [P, 2, NSLOT]), sb("wT", [P, 2, P])
        names = "w_in c_in hi lo pe_mm mid chain gelu q_out s_mm masked exp wt_mm wt_cp y_mm y_add lrn ln sig sig2 ones".split()
        s = {n: k.sem("m_" + n) for n in names}
        b0 = {n: s[n].base for n in names}
        counts = dict.fromkeys(names, 0)

        def inc(ins, n, by=1):
            counts[n] += by
            return ins.then_inc(s[n].sem, by)

        block = st.enter_context(nc.Block())
        B = k.bank

        @block.sync
        def _(sp):
            inc(sp.dma_start(wq[:, :, :], d[name + "m_wq"]), "w_in", 16)
            inc(sp.dma_start(wu[:, :, :], d[name + "m_wu1"]), "w_in", 16)
            for buf, n in ((wr[:, :], "wr"), (keysT[:, :], "keysT"), (valsT[:, :, :], "valsT"), (wvd[:, :, :], "wvd"), (wvu[:, :], "wvu"),
                           (bu1[:, :], "bu1"), (wu2[:, :], "wu2"), (rkT[BOT:BOT + 1, :], "log_rel"), (keysA[BOT:BOT + 1, :], "log_rel")):
                inc(sp.dma_start(buf, d[name + "m_" + n]), "c_in", 16)
            inc(sp.dma_start(scal[:, :], d[name + "m_scal"].partition_broadcast(P)), "c_in", 16)

        C_IN = b0["c_in"] + 160

        @block.gpsimd
        def _(pool):
            for n, (src, h, l) in enumerate(((wq, wqh, wql), (wu, wuh, wul))):
                pool.wait_ge(s["hi"].sem, b0["hi"] + n + 1)
                inc(nc.gpsimd.tensor_tensor(l[:, :, :], src[:, :, :], h[:, :, :].bitcast(F32), ALU.subtract), "lo")

        @block.tensor
        def _(pe):
            pe.wait_ge(s["c_in"].sem, C_IN)
            for a in range(KT):
                ins = nc.tensor.matmul(B[0][0:VB, 0:NSLOT], wvd[:, a, :], valsT[:, a, :], start=(a == 0), stop=(a == KT - 1))
            inc(ins, "pe_mm")
            inc(nc.tensor.matmul(B[1][0:BOT, 0:NSLOT], wr[:, :], keysT[:, :], start=True, stop=True), "pe_mm")
            pe.wait_ge(s["lo"].sem, b0["lo"] + 1)
            for b in range(BATCH):
                tok = slice(b * SEQ, (b + 1) * SEQ)
                for a in range(KT):
                    ins = matmul3(nc, B[2 + b][:, :], wqh[:, a, :], wql[:, a, :], k.xTh[:, a, tok], k.xTl[:, a, tok], a == 0, a == KT - 1)
                inc(ins, "pe_mm")
            pe.wait_ge(s["lo"].sem, b0["lo"] + 2)
            for b in range(BATCH):
                tok = slice(b * SEQ, (b + 1) * SEQ)
                for a in range(KT):
                    ins = matmul3(nc, B[4 + b][:, :], wuh[:, a, :], wul[:, a, :], k.xTh[:, a, tok], k.xTl[:, a, tok], a == 0, a == KT - 1)
                inc(ins, "pe_mm")
            pe.wait_ge(s["mid"].sem, b0["mid"] + 1)
            inc(nc.tensor.matmul(B[6][:, :], vw[:, :], wvu[:, :], start=True, stop=True), "pe_mm")
            for b in range(BATCH):
                pe.wait_ge(s["q_out"].sem, b0["q_out"] + b + 1)
                inc(nc.tensor.matmul(B[2 + b][0:BOT, :], wr[:, :], qA[0:BOT, b * SEQ:(b + 1) * SEQ], start=True, stop=True), "pe_mm")
            pe.wait_ge(s["gelu"].sem, b0["gelu"] + 2)
            pe.wait_ge(s["mid"].sem, b0["mid"] + 3)
            for t in range(TT):
                ins = nc.tensor.matmul(B[7][:, t:t + 1], gl[:, t * P:(t + 1) * P], wu2[:, :], start=True, stop=True)
            pe.wait_ge(s["ones"].sem, b0["ones"] + 1)
            pe.wait_ge(s["ln"].sem, b0["ln"] + 1)
            inc(nc.tensor.matmul(B[7][:, 16:16 + TT], ones[:, :], lv[:, :], start=True, stop=True), "lrn")
            pe.wait_ge(s["mid"].sem, b0["mid"] + 5)

            def slot_scores(t):
                if t >= 2:
                    pe.wait_ge(s["masked"].sem, b0["masked"] + t - 1)
                tok = slice(t * P, (t + 1) * P)
                nc.tensor.matmul(B[t % 2][:, 0:NSLOT], rqA[:, tok], rkT[:, :], start=True, stop=True)
                inc(nc.tensor.matmul(B[t % 2][:, NSLOT:2 * NSLOT], qA[:, tok], keysA[:, :], start=True, stop=True), "s_mm")

            slot_scores(0)
            for t in range(TT):
                if t + 1 < TT:
                    slot_scores(t + 1)
                pe.wait_ge(s["exp"].sem, b0["exp"] + t + 1)
                if t >= 2:
                    pe.wait_ge(s["wt_cp"].sem, b0["wt_cp"] + t - 1)
                inc(nc.tensor.transpose(B[2 + t % 2][:, 0:P], wts[:, t % 2, :], k.ident[:, :]), "wt_mm")
                pe.wait_ge(s["wt_cp"].sem, b0["wt_cp"] + t + 1)
                if t >= 2:
                    pe.wait_ge(s["y_add"].sem, b0["y_add"] + t - 1)
                inc(nc.tensor.matmul(B[4 + t % 2][:, :], wT[:, t % 2, :], mix[:, :], start=True, stop=True), "y_mm")

        @block.scalar
        def _(act):
            act.wait_ge(s["w_in"].sem, b0["w_in"] + 32)
            for src, h in ((wq, wqh), (wu, wuh)):
                inc(nc.scalar.activation(h[:, :, :], src[:, :, :], ACT.Copy), "hi")
            act.wait_ge(s["c_in"].sem, C_IN)
            for b in range(BATCH):
                act.wait_ge(s["pe_mm"].sem, b0["pe_mm"] + 5 + b)
                inc(nc.scalar.activation(gl[:, b * SEQ:(b + 1) * SEQ], B[4 + b][:, :], ACT.Gelu_apprx_tanh, bias=bu1[:, :]), "gelu")
            inc(nc.scalar.activation(lv[:, :], k.xvar[:, :], ACT.Ln, bias=1.0), "ln")
            act.wait_ge(s["chain"].sem, b0["chain"] + 1)
            inc(nc.scalar.activation(sg[:, :], B[7][:, 0:TT], ACT.Sigmoid, bias=scal[:, 0:1]), "sig")
            act.wait_ge(s["chain"].sem, b0["chain"] + 8)
            inc(nc.scalar.activation(gate[:, :], u[:, :], ACT.Sigmoid, bias=scal[:, 2:3], scale=scal[:, 1:2]), "sig2")
            for t in range(TT):
                act.wait_ge(s["masked"].sem, b0["masked"] + t + 1)
                if t >= 2:
                    act.wait_ge(s["wt_mm"].sem, b0["wt_mm"] + t - 1)
                inc(nc.scalar.activation(wts[:, t % 2, :], att[:, t % 2, :], ACT.Exp, bias=negmax[:, t:t + 1],
                                         accum_out=rowsum[:, t:t + 1]), "exp")
                act.wait_ge(s["wt_mm"].sem, b0["wt_mm"] + t + 1)
                if t >= 2:
                    act.wait_ge(s["y_mm"].sem, b0["y_mm"] + t - 1)
                inc(nc.scalar.activation(wT[:, t % 2, :], B[2 + t % 2][:, 0:P], ACT.Copy), "wt_cp")

        @block.vector
        def _(dve):
            steps = [0]

            def link(ins):
                steps[0] += 1
                inc(ins, "chain")
                dve.wait_ge(s["chain"].sem, b0["chain"] + steps[0])

            nc.vector.memset(qA[BOT:BOT + 1, :], 1.0)
            nc.vector.memset(rqA[BOT:BOT + 1, :], 1.0)
            inc(nc.vector.memset(ones[:, :], 1.0), "ones")
            dve.wait_ge(s["c_in"].sem, C_IN)
            dve.wait_ge(s["pe_mm"].sem, b0["pe_mm"] + 1)
            inc(nc.vector.tensor_copy(vw[:, :], B[0][0:VB, 0:NSLOT]), "mid")
            dve.wait_ge(s["pe_mm"].sem, b0["pe_mm"] + 2)
            inc(nc.vector.tensor_scalar(rkT[0:BOT, :], B[1][0:BOT, 0:NSLOT], float(1.0 / np.sqrt(RDIM)), None, ALU.mult), "mid")
            inc(nc.vector.tensor_scalar(keysA[0:BOT, :], keysT[:, :], float(1.0 / np.sqrt(BOT)), None, ALU.mult), "mid")
            for b in range(BATCH):
                dve.wait_ge(s["pe_mm"].sem, b0["pe_mm"] + 3 + b)
                inc(nc.vector.tensor_copy(qA[0:BOT, b * SEQ:(b + 1) * SEQ], B[2 + b][0:BOT, :]), "q_out")
            dve.wait_ge(s["pe_mm"].sem, b0["pe_mm"] + 7)
            nc.vector.tensor_copy(mix[:, :], B[6][:, :])
            for b in range(BATCH):
                dve.wait_ge(s["pe_mm"].sem, b0["pe_mm"] + 8 + b)
                inc(nc.vector.tensor_copy(rqA[0:BOT, b * SEQ:(b + 1) * SEQ], B[2 + b][0:BOT, :]), "mid")
            dve.wait_ge(s["lrn"].sem, b0["lrn"] + 1)
            link(nc.vector.tensor_reduce(lsum[:, :], B[7][:, 16:16 + TT], AX, ALU.add))
            link(nc.vector.tensor_scalar(lsum[:, :], lsum[:, :], 1.0 / TOK, 1e-6, ALU.mult, ALU.add))
            link(nc.vector.reciprocal(rl[:, :], lsum[:, :]))
            dve.wait_ge(s["sig"].sem, b0["sig"] + 1)
            dve.wait_ge(s["ln"].sem, b0["ln"] + 1)
            nc.vector.tensor_scalar(u[:, :], lv[:, :], rl[:, 0:1], 0.5, ALU.mult, ALU.mult)
            link(nc.vector.tensor_scalar(ge[:, :], sg[:, :], 2.5, None, ALU.mult))
            link(nc.vector.tensor_tensor(u[:, :], u[:, :], ge[:, :], ALU.add))
            link(nc.vector.tensor_scalar(u[:, :], u[:, :], 0.0, 5.0, ALU.max, ALU.min))
            TAU_LOW, TAU_HIGH = 0.5, 2.0
            link(nc.vector.tensor_scalar(fac[:, :], u[:, :], -TAU_LOW, 1.0 / (TAU_HIGH - TAU_LOW), ALU.add, ALU.mult))
            link(nc.vector.tensor_scalar(u[:, :], fac[:, :], 0.0, 1.0, ALU.max, ALU.min))
            dve.wait_ge(s["sig2"].sem, b0["sig2"] + 1)
            link(nc.vector.tensor_scalar(ge[:, :], gate[:, :], 0.05, None, ALU.is_ge))
            link(nc.vector.tensor_tensor(gate[:, :], gate[:, :], ge[:, :], ALU.mult))

            def choose(t):
                dve.wait_ge(s["s_mm"].sem, b0["s_mm"] + t + 1)
                sc = B[t % 2][:, 0:NSLOT]
                link(nc.vector.max(top[:, t, :], sc))
                link(nc.vector.match_replace(rep[:, t % 2, :], top[:, t, :], sc, -3e38))
                link(nc.vector.tensor_tensor(rep[:, t % 2, :], rep[:, t % 2, :], sc, ALU.is_equal))
                if t >= 2:
                    dve.wait_ge(s["exp"].sem, b0["exp"] + t - 1)
                link(nc.vector.scalar_tensor_tensor(out=att[:, t % 2, :], in0=rep[:, t % 2, :], scalar=MASKED,
                                                    in1=B[t % 2][:, NSLOT:2 * NSLOT], op0=ALU.mult, op1=ALU.add))
                inc(nc.vector.tensor_reduce(negmax[:, t:t + 1], att[:, t % 2, :], AX, ALU.max, negate=True), "masked")

            def add(t):
                dve.wait_ge(s["exp"].sem, b0["exp"] + t + 1)
                link(nc.vector.reciprocal(rinv[:, t:t + 1], rowsum[:, t:t + 1]))
                link(nc.vector.tensor_tensor(fac[:, t:t + 1], rinv[:, t:t + 1], gate[:, t:t + 1], ALU.mult))
                dve.wait_ge(s["y_mm"].sem, b0["y_mm"] + t + 1)
                inc(nc.vector.scalar_tensor_tensor(out=k.x[:, t, :], in0=B[4 + t % 2][:, :], scalar=fac[:, t:t + 1],
                                                   in1=k.x[:, t, :], op0=ALU.mult, op1=ALU.add), "y_add")

            choose(0)
            for t in range(TT):
                if t + 1 < TT:
                    choose(t + 1)
                add(t)

        for n in names:
            s[n].base += counts[n]


def rotary(inv, dim, length):
    freqs = np.arange(length, dtype=np.float32)[:, None] * inv.astype(np.float32)[None, :]
    emb = np.concatenate([freqs, freqs], axis=-1)
    return np.cos(emb).T.astype(np.float32), np.sin(emb).T.astype(np.float32)


def llama_inv_freq(theta, factor, high, low, ctx, dim):
    inv = 1.0 / theta ** (np.arange(0, dim, 2, dtype=np.float64) / dim)
    wavelen = 2.0 * np.pi / inv
    smooth = (ctx / wavelen - low) / (high - low)
    scaled = np.where(wavelen > ctx / low, inv / factor, inv)
    mid = (wavelen <= ctx / low) & (wavelen >= ctx / high)
    return np.where(mid, (1 - smooth) * inv / factor + smooth * inv, scaled).astype(np.float32)


def wide_tables(inv, key_scale):
    cos, sin = rotary(inv, HD, SEQ)
    sign = np.where(np.arange(HD) < HD // 2, 1.0, -1.0).astype(np.float32)[:, None]
    ks = (key_scale / np.sqrt(np.float32(HD))).astype(np.float32)[None, :]
    return np.ascontiguousarray(np.stack([cos, sin * sign, cos * ks, sin * sign * ks], axis=1).astype(np.float32))


def constant_arrays():
    pos = np.arange(SEQ)
    key_scale = np.where(pos < SYS_LEN, SUP, np.where(pos < SYS_LEN + IMG_LEN, ENH, 1.0)).astype(np.float32)
    inv1 = 1.0 / np.float32(10000.0) ** (np.arange(0, HD, 2, dtype=np.float32) / np.float32(HD))
    back = 1.0 / key_scale[:P]
    t0s = np.where(np.arange(P)[:, None] >= SYS_LEN + IMG_LEN, 1.0, back[None, :]).astype(np.float32)
    mask = np.where(np.arange(P)[None, :] > np.arange(P)[:, None], MASKED, 0.0).astype(np.float32)
    consts = np.stack([np.eye(P, dtype=np.float32), mask], axis=1)
    a = {
        "consts": consts,
        "L1_tables": wide_tables(inv1, key_scale),
        "L1_t0s": t0s,
        "tri_g": np.tril(np.ones((MGROUPS, MGROUPS), np.float32), -1),
        "tri_e": np.tril(np.ones((EXPERTS, EXPERTS), np.float32), -1),
        "L3_tables": wide_tables(llama_inv_freq(500000.0, 8.0, 4.0, 1.0, 1024, HD), np.ones(SEQ, np.float32)),
    }
    a["L0_kcol"] = (np.arange(P) // 16 + 2).astype(np.float32).reshape(P, 1)
    dh = 16
    inv2 = 1.0 / np.float32(500000.0) ** (np.arange(0, dh, 2, dtype=np.float32) / np.float32(dh))
    inv2 = np.where(2.0 * np.pi / inv2 > 1024.0, inv2 / np.float32(32.0), inv2).astype(np.float32)
    cos, sin = (m.T for m in rotary(inv2, dh, SEQ))
    sin = sin * np.where(np.arange(dh) < dh // 2, -1.0, 1.0).astype(np.float32)
    sc = np.float32(1.0 / np.sqrt(dh))
    tab = np.stack([cos * sc, sin * sc, cos, sin], axis=1).astype(np.float32)
    a["L2_tab"] = tab.reshape(QT, P, 4, dh).transpose(1, 0, 2, 3)
    return a


def by_feature(w):
    return w.reshape(KT, P, -1).transpose(1, 0, 2)


def input_arrays(i):
    a = {"x": i["L0_attn_x"].reshape(TOK, D)}

    def heads(w):
        return w.reshape(KT, P, -1, HD).transpose(2, 1, 0, 3)

    for name, t in (("L1_", True), ("L3_", False)):
        w = {n: (i[f"{name}attn_w{n}"].T if t else i[f"{name}attn_w{n}"]) for n in "qkvo"}
        for n in "qkv":
            a[f"{name}w{n}"] = heads(w[n])
        a[f"{name}wo"] = w["o"].reshape(HEADS, HD, D)

    def slabs(routed, shared):
        return np.concatenate([routed, shared])

    f = {n: i["L1_ffn_" + n] for n in ("router_w", "router_b", "router_bias", "ew1", "eb1", "ew2", "eb2", "ew3", "eb3",
                                       "sw1", "sb1", "sw2", "sb2", "sw3", "sb3")}
    a["router_w"] = by_feature(f["router_w"])
    a["router_rows"] = np.stack([f["router_b"], f["router_bias"]])
    for n in "12":
        w = slabs(f["ew" + n], f["sw" + n].reshape(D, 2, INTER).transpose(1, 0, 2))
        a["ew" + n] = w.reshape(SLABS, KT, P, INTER).transpose(0, 2, 1, 3)
    a["ew3"] = slabs(f["ew3"], f["sw3"].reshape(2, INTER, D))
    a["eb12"] = np.stack([slabs(f["eb" + n], f["sb" + n].reshape(2, INTER)) for n in "12"], axis=2)
    a["b3"] = np.concatenate([f["eb3"], f["sb3"].reshape(1, D)])

    def padded(w, rows, cols):
        out = np.zeros((rows, cols), w.dtype)
        out[:w.shape[0], :w.shape[1]] = w
        return out

    g = lambda n: i["L0_attn_" + n]
    a["L0_wqkv"] = by_feature(np.concatenate([g("Wqk_w"), g("Wv_w")]).T)
    a["L0_qkvb"] = np.concatenate([g("Wqk_b"), g("Wv_b")])
    a["L0_wo"] = g("Wo_w").T
    a["L0_wf"] = by_feature(i["L0_ffn_weight"].T)
    a["L0_la"] = by_feature(padded(i["L0_ffn_lora_A"].reshape(-1, D).T, D, P))
    lb = i["L0_ffn_lora_B"].transpose(0, 2, 1).reshape(-1, D)
    a["L0_lb"] = np.concatenate([lb, np.zeros((64 - lb.shape[0], D), lb.dtype), i["L0_ffn_bias"].reshape(1, D), g("Wo_b").reshape(1, D)])
    a["L0_starts"] = i["L0_ffn_lora_start_indices"]
    g = lambda n: i["L2_attn_" + n]
    a["L2_wqkv"] = by_feature(np.concatenate([g("Wq"), g("Wk"), g("Wv")]).T)
    a["L2_wo"] = by_feature(g("Wo").T)
    for name in ("L2_", "L3_"):
        g = lambda n: i[name + "ffn_" + n]
        a[name + "m_wq"] = by_feature(padded(g("Wq").T, D, P))
        a[name + "m_wu1"] = by_feature(g("Wu1").T)
        a[name + "m_wr"] = padded(g("Wr").T, BOT, BOT)
        a[name + "m_keysT"] = g("aux_keys").T
        a[name + "m_valsT"] = by_feature(g("aux_values").T)
        a[name + "m_wvd"] = by_feature(g("Wvd").T)
        a[name + "m_wvu"] = g("Wvu").T
        a[name + "m_bu1"] = g("bu1").reshape(P, 1)
        a[name + "m_wu2"] = g("Wu2").reshape(P, 1)
        a[name + "m_log_rel"] = g("log_rel").reshape(1, NSLOT)
        a[name + "m_scal"] = np.concatenate([g("bu2").reshape(1), g("gate_w1").reshape(1), g("gate_bias").reshape(1)])
    return a


def store(k, out):
    nc = k.nc
    with ExitStack() as st:
        y_out = k.sem("y_out")
        block = st.enter_context(nc.Block())

        @block.sync
        def _(sp):
            sp.dma_start(out.rearrange("(t p) n -> p t n", p=P), k.x[:, :, :]).then_inc(y_out.sem, 16)
            sp.wait_ge(y_out.sem, 16)


def program(nc, d, out):
    with ExitStack() as ctx:
        k = make_shared(nc, ctx)
        load_constants(k, d)
        layer_norm(k, 0, False)
        narrow_layer0(k, d)
        layer_norm(k, 1, False)
        wide_attention(k, d, "L1_", True)
        experts(k, d)
        layer_norm(k, 2, True)
        narrow_attention2(k, d)
        memory_ffn(k, d, "L2_")
        layer_norm(k, 3, True)
        wide_attention(k, d, "L3_", False)
        memory_ffn(k, d, "L3_")
        store(k, out)


def kernel(**inputs):
    import concourse.bacc as bacc
    from concourse.bass_utils import run_bass_kernel_spmd as run

    arrays = {n: np.ascontiguousarray(a) for n, a in {**input_arrays(inputs), **constant_arrays()}.items()}
    nc = bacc.Bacc("TRN2", target_bir_lowering=False, num_devices=1)
    d = {n: nc.dram_tensor("in_" + n, a.shape, mybir.dt.from_np(a.dtype), kind="ExternalInput").ap() for n, a in arrays.items()}
    out = nc.dram_tensor("out_y", (TOK, D), F32, kind="ExternalOutput").ap()
    program(nc, d, out)
    r = run(nc, [{"in_" + n: a for n, a in arrays.items()}], core_ids=[0])
    return r.results[0]["out_y"].reshape(BATCH, SEQ, D)
```

```python
from contextlib import ExitStack

import numpy as np
import concourse.bass as bass
from concourse import mybir

F32 = mybir.dt.float32
F32R = mybir.dt.float32r
BF16 = mybir.dt.bfloat16
I32 = mybir.dt.int32
ACT = mybir.ActivationFunctionType
ALU = mybir.AluOpType
AX = mybir.AxisListType.X

P = 128
D = 512
KT = D // P
BATCH, SEQ = 2, 512
QT = SEQ // P
TT = BATCH * QT
TOK = BATCH * SEQ
EPS = 1e-5
MASKED = -1e30

HD, HEADS, GROUPS = 128, 32, 8
HPG = HEADS // GROUPS
SYS_LEN, IMG_LEN, SUP, ENH = 35, 72, 0.5, 1.5

EXPERTS, INTER, MGROUPS = 16, 128, 4
SLABS = EXPERTS + 2

BOT, RDIM, NSLOT, TOPK, VB = 64, 48, 128, 8, 32


class Count:

    def __init__(self, sem):
        self.sem, self.base, self.per = sem, 0, 0

    def start(self, per):
        first = self.per == 0
        assert first or self.per == per
        self.per = per
        return first


class Shared:
    pass


def make_shared(nc, ctx):
    k = Shared()
    k.nc = nc

    def sb(name, shape, dt=F32, stack=ctx):
        return stack.enter_context(nc.sbuf_tensor(name, shape, dt))

    k.sb = sb
    k.sems = {}

    def sem(name):
        if name not in k.sems:
            k.sems[name] = Count(ctx.enter_context(nc.semaphore(name)))
        return k.sems[name]

    k.sem = sem
    k.ctx = ctx
    k.x = sb("x", [P, TT, D])
    k.xTh = sb("xTh", [P, KT, TOK], F32R)
    k.xTl = sb("xTl", [P, KT, TOK], F32R)
    k.ident = sb("ident", [P, P])
    k.identb = sb("identb", [P, P], BF16)
    k.maskb = sb("maskb", [P, P], BF16)
    k.xvar = sb("xvar", [P, TT])
    k.bank = [ctx.enter_context(nc.psum_tensor(f"bank{n}", [P, 512], F32)) for n in range(8)]
    return k


def matmul3(nc, out, ah, al, bh, bl, first, last):
    nc.tensor.matmul(out, ah, bh, start=first, stop=False)
    nc.tensor.matmul(out, ah, bl, start=False, stop=False)
    return nc.tensor.matmul(out, al, bh, start=False, stop=last)


def load_constants(k, d):
    nc = k.nc
    with ExitStack() as st:
        cst = k.sb("cst", [P, 2, P], F32, st)
        c_in, c_cast, x_in = k.sem("c_in"), k.sem("c_cast"), k.sem("x_in")
        block = st.enter_context(nc.Block())

        @block.sync
        def _(sp):
            sp.dma_start(cst[:, :, :], d["consts"]).then_inc(c_in.sem, 16)
            sp.dma_start(k.x[:, :, :], d["x"].rearrange("(t p) n -> p t n", p=P)).then_inc(x_in.sem, 16)

        @block.vector
        def _(dve):
            dve.wait_ge(c_in.sem, 16)
            nc.vector.tensor_copy(k.ident[:, :], cst[:, 0, :])
            nc.vector.tensor_copy(k.identb[:, :], cst[:, 0, :])
            nc.vector.tensor_copy(k.maskb[:, :], cst[:, 1, :]).then_inc(c_cast.sem, 1)
            dve.wait_ge(x_in.sem, 16)


def layer_norm(k, n, add_normed):
    nc = k.nc
    with ExitStack() as st:
        xn = k.sb(f"xn{n}", [P, TT, D], F32, st)
        stats = k.sb(f"stats{n}", [P, TT, 6], F32, st)
        mv = k.sb(f"mv{n}", [P, TT, 2], F32, st)
        stats2 = k.sb(f"stats2{n}", [P, TT, 6], F32, st)
        mv2 = k.sb(f"mv2{n}", [P, TT, 2], F32, st)
        veps = k.sb(f"veps{n}", [P, TT], F32, st)
        sd = k.sb(f"sd{n}", [P, TT], F32, st)
        rstd = k.sb(f"rstd{n}", [P, TT], F32, st)
        chain, sq, normed, turned, hi, lo = (k.sem("ln_" + s) for s in "chain sqrt normed turned hi lo".split())
        c0, s0, n0, t0, h0, l0 = (s.base for s in (chain, sq, normed, turned, hi, lo))
        banks = k.bank[0:4]
        block = st.enter_context(nc.Block())
        steps = [0]

        @block.vector
        def _(dve):
            def link(ins):
                steps[0] += 1
                ins.then_inc(chain.sem, 1)
                dve.wait_ge(chain.sem, c0 + steps[0])

            for t in range(TT):
                ins = nc.vector.bn_stats(stats[:, t, :], k.x[:, t, :])
            link(ins)
            for t in range(TT):
                ins = nc.vector.bn_aggr(mv[:, t, :], stats[:, t, :])
            link(ins)
            nc.vector.tensor_scalar(veps[:, :], mv[:, :, 1], EPS, None, ALU.add).then_inc(chain.sem, 1)
            steps[0] += 1
            dve.wait_ge(sq.sem, s0 + 1)
            link(nc.vector.reciprocal(rstd[:, :], sd[:, :]))

            def low_part(t):
                dve.wait_ge(hi.sem, h0 + t + 1)
                nc.vector.tensor_tensor(
                    k.xTl[:, :, t * P:(t + 1) * P], banks[t % 4][:, :].rearrange("p (a q) -> p a q", a=KT),
                    k.xTh[:, :, t * P:(t + 1) * P].bitcast(F32), ALU.subtract).then_inc(lo.sem, 1)

            for t in range(TT):
                nc.vector.tensor_scalar(xn[:, t, :], k.x[:, t, :], mv[:, t, 0:1], rstd[:, t:t + 1],
                                        ALU.subtract, ALU.mult).then_inc(normed.sem, 1)
                if t >= 1:
                    low_part(t - 1)
            low_part(TT - 1)
            if add_normed:
                dve.wait_ge(normed.sem, n0 + TT)
                for t in range(TT):
                    ins = nc.vector.bn_stats(stats2[:, t, :], xn[:, t, :])
                link(ins)
                for t in range(TT):
                    ins = nc.vector.bn_aggr(mv2[:, t, :], stats2[:, t, :])
                link(ins)
                nc.vector.tensor_copy(k.xvar[:, :], mv2[:, :, 1])

        @block.scalar
        def _(act):
            act.wait_ge(chain.sem, c0 + 3)
            nc.scalar.activation(sd[:, :], veps[:, :], ACT.Sqrt).then_inc(sq.sem, 1)
            for t in range(TT):
                act.wait_ge(turned.sem, t0 + t + 1)
                nc.scalar.activation(k.xTh[:, :, t * P:(t + 1) * P],
                                     banks[t % 4][:, :].rearrange("p (a q) -> p a q", a=KT), ACT.Copy).then_inc(hi.sem, 1)

        @block.tensor
        def _(pe):
            for t in range(TT):
                pe.wait_ge(normed.sem, n0 + t + 1)
                if t >= 4:
                    pe.wait_ge(lo.sem, l0 + t - 3)
                for a in range(KT):
                    ins = nc.tensor.transpose(banks[t % 4][:, a * P:(a + 1) * P], xn[:, t, a * P:(a + 1) * P], k.ident[:, :])
                ins.then_inc(turned.sem, 1)

        @block.gpsimd
        def _(pool):
            if add_normed:
                for t in range(TT):
                    pool.wait_ge(normed.sem, n0 + t + 1)
                    nc.gpsimd.tensor_tensor(k.x[:, t, :], k.x[:, t, :], xn[:, t, :], ALU.add)

        chain.base += steps[0]
        sq.base += 1
        for s in (normed, turned, hi, lo):
            s.base += TT


def wide_attention(k, d, name, tile0_scale):
    nc = k.nc
    UNITS = BATCH * HPG
    ACC, SM, TR = 20, 4 * UNITS, 4 * UNITS
    W_SEQ = ["wk", "wq0", "wq1", "wv", "wq2", "wq3", "wo0", "wo1", "wo2", "wo3"]
    w_at = {w: n for n, w in enumerate(W_SEQ)}
    beside = {-1: ["K0", "Q0", "Q1", "V0"], 0: ["Q2"], 1: ["K1", "Q3"], 2: ["V1", "Q4"], 3: ["Q5"], 4: ["Q6"], 5: ["Q7"]}
    acc_seq = [a for u in range(-1, 6) for a in beside[u]] + [f"W{t}" for t in range(TT)]
    assert len(acc_seq) == ACC
    acc_at = {a: n for n, a in enumerate(acc_seq)}
    row_off = [P * i * (i + 1) // 2 for i in range(QT + 1)]
    ORDER = [3, 2, 1, 0]

    with ExitStack() as st:
        def sb(nm, shape, dt=F32):
            return k.sb(name + nm, shape, dt, st)

        wq_st = sb("wq_st", [P, 2, KT, HD])
        wo_st = sb("wo_st", [P, 2, D])
        wk_st = sb("wk_st", [P, KT, HD])
        wv_st = sb("wv_st", [P, KT, HD])
        wqh, wql = sb("wqh", [P, HPG, KT, HD], F32R), sb("wql", [P, HPG, KT, HD], F32R)
        woh, wol = sb("woh", [P, HPG, D], F32R), sb("wol", [P, HPG, D], F32R)
        wkh, wkl = sb("wkh", [P, KT, HD], F32R), sb("wkl", [P, KT, HD], F32R)
        wvh, wvl = sb("wvh", [P, KT, HD], F32R), sb("wvl", [P, KT, HD], F32R)
        kh, kl = sb("kh", [P, BATCH, SEQ], F32R), sb("kl", [P, BATCH, SEQ], F32R)
        vh, vl = sb("vh", [P, TT, HD], F32R), sb("vl", [P, TT, HD], F32R)
        rope_a, rope_b, rope_s = sb("rope_a", [P, SEQ]), sb("rope_b", [P, SEQ]), sb("rope_s", [P, SEQ])
        qh, ql = sb("qh", [P, 3, SEQ], F32R), sb("ql", [P, 3, SEQ], F32R)
        probs = sb("probs", [P, 2, row_off[QT]])
        pth, ptl = sb("pth", [P, 2, SEQ], F32R), sb("ptl", [P, 2, SEQ], F32R)
        oth, otl = sb("oth", [P, UNITS, SEQ], F32R), sb("otl", [P, UNITS, SEQ], F32R)
        tables = sb("tables", [P, 4, SEQ])
        t0s = sb("t0s", [P, P]) if tile0_scale else None
        negmax, rowsum, rinv = sb("negmax", [P, UNITS, QT]), sb("rowsum", [P, UNITS, QT]), sb("rinv", [P, UNITS, QT])

        acc, sbank, tbank, obank = k.bank[0:2], k.bank[2:5], k.bank[5:7], k.bank[7]

        pers = dict(acc_mm=ACC, s_mm=SM, t_mm=TR, pv_mm=TR,
                    acc_out=ACC, maxed=SM, rinv_ok=UNITS, pt_lo=TR, o_lo=UNITS,
                    exp_ok=SM, pt_hi=TR, o_hi=UNITS, qk_hi=10, v_hi=2, w_hi=10,
                    qk_sum=10, qk_lo=10, norm_ok=SM, w_lo=10)
        s = {n: k.sem("wa_" + n) for n in pers}
        due = {n: s[n].start(pers[n]) for n in pers}
        d_in = {n: k.sem("wa_in_" + n) for n in ("wq0", "wq1", "wo0", "wo1", "wk", "wv", "tab")}
        d_base = {n: d_in[n].base for n in d_in}
        swaps = k.sem("wa_tab_seen")
        base = {n: s[n].base for n in pers}

        def credit(eng, *names):
            for n in names:
                if due[n]:
                    eng.sem_inc(s[n].sem, pers[n])

        def waits(eng, g):
            def w(n, count):
                eng.wait_ge(s[n].sem, base[n] + pers[n] + g * pers[n] + count)
            return w

        block = st.enter_context(nc.Block())

        @block.sync
        def _(sp):
            sp.dma_start(tables[:, :, :], d[name + "tables"]).then_inc(d_in["tab"].sem, 16)
            if tile0_scale:
                sp.dma_start(t0s[:, :], d[name + "t0s"]).then_inc(d_in["tab"].sem, 16)
            with sp.Fori(0, GROUPS) as g:
                w = waits(sp, g)

                def load(buf, src, sem):
                    sp.dma_start(buf, src).then_inc(d_in[sem].sem, 16)

                def wq(h):
                    w("w_lo", w_at[f"wq{h - 2}"] + 1 if h >= 2 else w_at[f"wq{h + 2}"] + 1 - 10)
                    load(wq_st[:, h % 2, :, :], d[name + "wq"][bass.ds(g * HPG + h, 1)].rearrange("a p k n -> p (a k) n"), f"wq{h % 2}")

                def wo(h):
                    w("w_lo", w_at[f"wo{h - 2}"] + 1 if h >= 2 else w_at[f"wo{h + 2}"] + 1 - 10)
                    load(wo_st[:, h % 2, :], d[name + "wo"][bass.ds(g * HPG + h, 1)].rearrange("a p n -> p (a n)"), f"wo{h % 2}")

                w("w_lo", w_at["wk"] + 1 - 10)
                load(wk_st[:, :, :], d[name + "wk"][bass.ds(g, 1)].rearrange("a p k n -> p (a k) n"), "wk")
                wq(0)
                wq(1)
                w("w_lo", w_at["wv"] + 1 - 10)
                load(wv_st[:, :, :], d[name + "wv"][bass.ds(g, 1)].rearrange("a p k n -> p (a k) n"), "wv")
                wq(2)
                wq(3)
                for h in range(HPG):
                    wo(h)

        def weight_parts(wname):
            h = int(wname[2]) if len(wname) == 3 else 0
            if wname.startswith("wq"):
                return wq_st[:, h % 2, :, :], wqh[:, h, :, :], wql[:, h, :, :], f"wq{h % 2}", 2, h // 2 + 1
            if wname.startswith("wo"):
                return wo_st[:, h % 2, :], woh[:, h, :], wol[:, h, :], f"wo{h % 2}", 2, h // 2 + 1
            if wname == "wk":
                return wk_st[:, :, :], wkh[:, :, :], wkl[:, :, :], "wk", 1, 1
            return wv_st[:, :, :], wvh[:, :, :], wvl[:, :, :], "wv", 1, 1

        def qk_parts(a):
            n = int(a[1:])
            if a[0] == "K":
                return kh[:, n, :], kl[:, n, :]
            return qh[:, n % 3, :], ql[:, n % 3, :]

        qk_seq = [a for a in acc_seq if a[0] in "KQ"]
        qk_at = {a: n for n, a in enumerate(qk_seq)}

        @block.tensor
        def _(pe):
            credit(pe, "acc_mm", "s_mm", "t_mm", "pv_mm")
            with pe.Fori(0, GROUPS) as g:
                w = waits(pe, g)

                def acc_bank(a):
                    w("acc_out", acc_at[a] - 1)
                    return acc[acc_at[a] % 2]

                def project_qk(a, wh, wl, b, wname):
                    bank = acc_bank(a)
                    w("w_lo", w_at[wname] + 1)
                    for t in range(KT):
                        ins = matmul3(nc, bank[:, :], wh[:, t, :], wl[:, t, :], k.xTh[:, t, b * SEQ:(b + 1) * SEQ],
                                      k.xTl[:, t, b * SEQ:(b + 1) * SEQ], t == 0, t == KT - 1)
                    ins.then_inc(s["acc_mm"].sem, 1)

                def project_q(u):
                    h = u % HPG
                    project_qk(f"Q{u}", wqh[:, h, :, :], wql[:, h, :, :], u // HPG, f"wq{h}")

                def project_v(half):
                    bank = acc_bank(f"V{half}")
                    w("w_lo", w_at["wv"] + 1)
                    for t in range(QT):
                        tok = slice((half * QT + t) * P, (half * QT + t + 1) * P)
                        for a in range(KT):
                            ins = matmul3(nc, bank[:, t * HD:(t + 1) * HD], k.xTh[:, a, tok], k.xTl[:, a, tok],
                                          wvh[:, a, :], wvl[:, a, :], a == 0, a == KT - 1)
                    ins.then_inc(s["acc_mm"].sem, 1)

                def scores(u, n):
                    i, m, b = ORDER[n], 4 * u + n, u // HPG
                    w("exp_ok", m - 2 if m >= 3 else 0)
                    w("qk_lo", qk_at[f"Q{u}"] + 1)
                    keys = (i + 1) * P
                    out = sbank[m % 3][:, 0:keys]
                    rows = slice(i * P, (i + 1) * P)
                    matmul3(nc, out, qh[:, u % 3, rows], ql[:, u % 3, rows], kh[:, b, 0:keys], kl[:, b, 0:keys], True, False)
                    nc.tensor.matmul(sbank[m % 3][:, i * P:keys], k.identb[:, :], k.maskb[:, :],
                                     start=False, stop=True).then_inc(s["s_mm"].sem, 1)

                def turn_probs(u, j):
                    n = 4 * u + j
                    w("pt_lo", n - 1)
                    if j == 0:
                        w("norm_ok", 4 * u + 4)
                    for i in range(j, QT):
                        ins = nc.tensor.transpose(tbank[n % 2][:, i * P:(i + 1) * P],
                                                  probs[:, u % 2, row_off[i] + j * P:row_off[i] + (j + 1) * P], k.ident[:, :])
                    ins.then_inc(s["t_mm"].sem, 1)

                def values(u, j):
                    n, vt = 4 * u + j, (u // HPG) * QT + j
                    if j == 0:
                        w("o_lo", u)
                        w("acc_out", acc_at[f"V{u // HPG}"] + 1)
                    w("pt_lo", n + 1)
                    cols = slice(j * P, SEQ)
                    matmul3(nc, obank[:, cols], vh[:, vt, :], vl[:, vt, :], pth[:, n % 2, cols], ptl[:, n % 2, cols],
                            j == 0, j == QT - 1).then_inc(s["pv_mm"].sem, 1)

                def unit_out(u):
                    values(u, 0)
                    turn_probs(u, 2)
                    values(u, 1)
                    turn_probs(u, 3)
                    values(u, 2)
                    values(u, 3)

                def project_out(t):
                    bank, b = acc_bank(f"W{t}"), t // QT
                    rows = slice((t % QT) * P, (t % QT + 1) * P)
                    for h in range(HPG):
                        u = b * HPG + h
                        w("o_lo", u + 1)
                        w("w_lo", w_at[f"wo{h}"] + 1)
                        ins = matmul3(nc, bank[:, :], oth[:, u, rows], otl[:, u, rows], woh[:, h, :], wol[:, h, :],
                                      h == 0, h == HPG - 1)
                    ins.then_inc(s["acc_mm"].sem, 1)

                def project(u):
                    for a in beside.get(u, []):
                        n = int(a[1])
                        if a[0] == "K":
                            project_qk(a, wkh, wkl, n, "wk")
                        elif a[0] == "Q":
                            project_q(n)
                        else:
                            project_v(n)

                project(-1)
                for u in range(UNITS + 1):
                    if u < UNITS:
                        scores(u, 0)
                        scores(u, 1)
                        scores(u, 2)
                    if u == 1:
                        project(u)
                    if u >= 1:
                        turn_probs(u - 1, 0)
                        turn_probs(u - 1, 1)
                    if u != 1:
                        project(u)
                    if u < UNITS:
                        scores(u, 3)
                    if u >= 1:
                        unit_out(u - 1)
                    if u >= 5:
                        project_out(u - 5)
                for t in range(QT, TT):
                    project_out(t)

        @block.vector
        def _(dve):
            credit(dve, "acc_out", "maxed", "rinv_ok", "pt_lo", "o_lo")
            dve.wait_ge(d_in["tab"].sem, d_base["tab"] + (32 if tile0_scale else 16))
            with dve.Fori(0, GROUPS) as g:
                w = waits(dve, g)

                def rope(a):
                    bank, c = acc[acc_at[a] % 2], 2 if a[0] == "K" else 0
                    w("acc_mm", acc_at[a] + 1)
                    w("qk_sum", qk_at[a])
                    H = HD // 2
                    nc.vector.tensor_tensor(rope_a[:, :], bank[:, :], tables[:, c, :], ALU.mult)
                    nc.vector.tensor_tensor(rope_b[0:H, :], bank[H:HD, :], tables[H:HD, c + 1, :], ALU.mult)
                    nc.vector.tensor_tensor(rope_b[H:HD, :], bank[0:H, :], tables[0:H, c + 1, :],
                                            ALU.mult).then_inc(s["acc_out"].sem, 1)

                def v_low(half):
                    bank = acc[acc_at[f"V{half}"] % 2]
                    w("v_hi", half + 1)
                    tiles = slice(half * QT, (half + 1) * QT)
                    nc.vector.tensor_tensor(vl[:, tiles, :], bank[:, :].rearrange("p (t n) -> p t n", t=QT),
                                            vh[:, tiles, :].bitcast(F32), ALU.subtract).then_inc(s["acc_out"].sem, 1)

                def row_max(u, n):
                    i, m = ORDER[n], 4 * u + n
                    w("s_mm", m + 1)
                    sc = sbank[m % 3][:, 0:(i + 1) * P]
                    if i == 0 and tile0_scale:
                        nc.vector.tensor_tensor(sc, sc, t0s[:, :], ALU.mult).then_inc(swaps.sem, 1)
                        dve.wait_ge(swaps.sem, swaps.base + g * UNITS + u + 1)
                    nc.vector.tensor_reduce(negmax[:, u, i:i + 1], sc, AX, ALU.max, negate=True).then_inc(s["maxed"].sem, 1)

                def probs_low(u, j):
                    n = 4 * u + j
                    w("pt_hi", n + 1)
                    cols = slice(j * P, SEQ)
                    nc.vector.tensor_tensor(ptl[:, n % 2, cols], tbank[n % 2][:, cols], pth[:, n % 2, cols].bitcast(F32),
                                            ALU.subtract).then_inc(s["pt_lo"].sem, 1)

                def out_low(u):
                    w("o_hi", u + 1)
                    nc.vector.tensor_tensor(otl[:, u, :], obank[:, :], oth[:, u, :].bitcast(F32),
                                            ALU.subtract).then_inc(s["o_lo"].sem, 1)

                def add_out(t):
                    w("acc_mm", acc_at[f"W{t}"] + 1)
                    nc.vector.tensor_tensor(k.x[:, t, :], acc[acc_at[f"W{t}"] % 2][:, :], k.x[:, t, :],
                                            ALU.add).then_inc(s["acc_out"].sem, 1)

                def projected(u):
                    for a in beside.get(u, []):
                        if a[0] == "V":
                            v_low(int(a[1]))
                        else:
                            rope(a)

                projected(-1)
                for u in range(UNITS + 1):
                    if u < UNITS:
                        row_max(u, 0)
                        row_max(u, 1)
                        row_max(u, 2)
                    if u >= 1:
                        probs_low(u - 1, 0)
                        probs_low(u - 1, 1)
                    if u < UNITS:
                        row_max(u, 3)
                    if u >= 1:
                        probs_low(u - 1, 2)
                    if u < UNITS:
                        w("exp_ok", 4 * u + 4)
                        nc.vector.reciprocal(rinv[:, u, :], rowsum[:, u, :]).then_inc(s["rinv_ok"].sem, 1)
                    if u >= 1:
                        probs_low(u - 1, 3)
                    projected(u)
                    if u >= 1:
                        out_low(u - 1)
                    if u >= 5:
                        add_out(u - 5)
                for t in range(QT, TT):
                    add_out(t)

        @block.scalar
        def _(act):
            credit(act, "exp_ok", "pt_hi", "o_hi", "qk_hi", "v_hi", "w_hi")
            with act.Fori(0, GROUPS) as g:
                w = waits(act, g)

                def weight_high(wname):
                    src, hi, _, sem, per, at = weight_parts(wname)
                    act.wait_ge(d_in[sem].sem, d_base[sem] + g * 16 * per + 16 * at)
                    if wname == "wk":
                        w("acc_mm", acc_at["K1"] + 1 - ACC)
                    elif wname == "wv":
                        w("acc_mm", acc_at["V1"] + 1 - ACC)
                    elif wname[1] == "q":
                        w("acc_mm", acc_at[f"Q{int(wname[2]) + HPG}"] + 1 - ACC)
                    else:
                        w("acc_mm", 0)
                    w("w_lo", w_at[wname] - 10 + 1)
                    nc.scalar.activation(hi, src, ACT.Copy).then_inc(s["w_hi"].sem, 1)

                def qk_high(a):
                    w("qk_sum", qk_at[a] + 1)
                    w("s_mm", 4 * (int(a[1:]) - 2) if a[0] == "Q" and int(a[1:]) >= 3 else 0)
                    nc.scalar.activation(qk_parts(a)[0], rope_s[:, :], ACT.Copy).then_inc(s["qk_hi"].sem, 1)

                def v_high(half):
                    w("acc_mm", acc_at[f"V{half}"] + 1)
                    w("pv_mm", 0)
                    tiles = slice(half * QT, (half + 1) * QT)
                    nc.scalar.activation(vh[:, tiles, :], acc[acc_at[f"V{half}"] % 2][:, :].rearrange("p (t n) -> p t n", t=QT),
                                         ACT.Copy).then_inc(s["v_hi"].sem, 1)

                def exps(u, n):
                    i, m = ORDER[n], 4 * u + n
                    w("maxed", m + 1)
                    if n == 0:
                        w("t_mm", 4 * (u - 1))
                        w("rinv_ok", u - 1)
                    nc.scalar.activation(probs[:, u % 2, row_off[i]:row_off[i + 1]], sbank[m % 3][:, 0:(i + 1) * P], ACT.Exp,
                                         bias=negmax[:, u, i:i + 1], accum_out=rowsum[:, u, i:i + 1]).then_inc(s["exp_ok"].sem, 1)

                def probs_high(u, j):
                    n = 4 * u + j
                    w("t_mm", n + 1)
                    w("pv_mm", n - 1)
                    cols = slice(j * P, SEQ)
                    nc.scalar.activation(pth[:, n % 2, cols], tbank[n % 2][:, cols], ACT.Copy).then_inc(s["pt_hi"].sem, 1)

                def out_high(u):
                    w("pv_mm", 4 * u + 4)
                    w("acc_mm", -QT if u < HPG else 0)
                    nc.scalar.activation(oth[:, u, :], obank[:, :], ACT.Copy).then_inc(s["o_hi"].sem, 1)

                for wname in W_SEQ[:5]:
                    weight_high(wname)

                def projected(u):
                    for a in beside.get(u, []):
                        if a[0] == "V":
                            v_high(int(a[1]))
                        else:
                            qk_high(a)

                projected(-1)
                for u in range(UNITS + 1):
                    if u < UNITS:
                        exps(u, 0)
                        exps(u, 1)
                        exps(u, 2)
                    if u >= 1:
                        probs_high(u - 1, 0)
                        probs_high(u - 1, 1)
                    if u < UNITS:
                        exps(u, 3)
                    if u == 0:
                        weight_high("wq3")
                    if u >= 1:
                        probs_high(u - 1, 2)
                        probs_high(u - 1, 3)
                        out_high(u - 1)
                    projected(u)
                    if 0 <= u < HPG:
                        weight_high(f"wo{u}")

        @block.gpsimd
        def _(pool):
            credit(pool, "qk_sum", "qk_lo", "norm_ok", "w_lo")
            with pool.Fori(0, GROUPS) as g:
                w = waits(pool, g)

                def weight_low(wname):
                    src, hi, lo, _, _, _ = weight_parts(wname)
                    w("w_hi", w_at[wname] + 1)
                    nc.gpsimd.tensor_tensor(lo, src, hi.bitcast(F32), ALU.subtract).then_inc(s["w_lo"].sem, 1)

                def rope_sum(a):
                    n = qk_at[a]
                    w("acc_out", acc_at[a] + 1)
                    w("qk_lo", n)
                    nc.gpsimd.tensor_tensor(rope_s[:, :], rope_a[:, :], rope_b[:, :], ALU.add).then_inc(s["qk_sum"].sem, 1)

                def qk_low(a):
                    n = qk_at[a]
                    w("qk_hi", n + 1)
                    w("qk_sum", n + 1)
                    hi, lo = qk_parts(a)
                    nc.gpsimd.tensor_tensor(lo, rope_s[:, :], hi.bitcast(F32), ALU.subtract).then_inc(s["qk_lo"].sem, 1)

                def normalise(u, n):
                    i = ORDER[n]
                    w("rinv_ok", u + 1)
                    tile = probs[:, u % 2, row_off[i]:row_off[i + 1]]
                    nc.gpsimd.tensor_tensor(tile, tile, rinv[:, u, i:i + 1].broadcast_to([P, (i + 1) * P]), ALU.mult).then_inc(s["norm_ok"].sem, 1)

                for wname in W_SEQ[:5]:
                    weight_low(wname)

                def projected(u):
                    for a in beside.get(u, []):
                        if a[0] != "V":
                            rope_sum(a)
                            qk_low(a)

                projected(-1)
                for u in range(UNITS):
                    for n in range(QT):
                        normalise(u, n)
                    if u == 0:
                        weight_low("wq3")
                    projected(u)
                    if u < HPG:
                        weight_low(f"wo{u}")

        for n in pers:
            s[n].base += pers[n] * GROUPS
        for n, loads in (("wq0", 2), ("wq1", 2), ("wo0", 2), ("wo1", 2), ("wk", 1), ("wv", 1)):
            d_in[n].base += 16 * loads * GROUPS
        d_in["tab"].base += 32 if tile0_scale else 16
        if tile0_scale:
            swaps.base += GROUPS * UNITS


def experts(k, d):
    nc = k.nc
    E, G, EG = EXPERTS, MGROUPS, EXPERTS // MGROUPS
    with ExitStack() as st:
        def sb(nm, shape, dt=F32):
            return k.sb("mo_" + nm, shape, dt, st)

        rw, rwh, rwl = sb("rw", [P, KT, E]), sb("rwh", [P, KT, E], F32R), sb("rwl", [P, KT, E], F32R)
        rows = sb("rows", [P, 2, E])
        tri_g, tri_e = sb("tri_g", [P, G, G]), sb("tri_e", [P, E, E])
        z = sb("z", [P, TT, E])
        sc = sb("sc", [P, TT, E])
        mx, sm, ri = sb("mx", [P, TT]), sb("sm", [P, TT]), sb("ri", [P, TT])
        gm = sb("gm", [P, TT, G])
        cg, cg2 = sb("cg", [P, TT * G, G]), sb("cg2", [P, TT * G, G])
        rg, keep, pen = sb("rg", [P, TT, G]), sb("keep", [P, TT, G]), sb("pen", [P, TT, G])
        ce, ce2 = sb("ce", [P, TT * E, E]), sb("ce2", [P, TT * E, E])
        re_ = sb("re", [P, TT, E])
        gates = sb("gates", [P, TT, SLABS])
        gates_e = sb("gates_e", [P, SLABS, TT])
        gate = sb("gate", [P, TT])
        gT = sb("gT", [E + 1, TT, P])
        b3 = sb("b3", [E + 1, D])
        w1s, w2s, w3s = sb("w1s", [P, KT, INTER]), sb("w2s", [P, KT, INTER]), sb("w3s", [P, D])
        w1h, w1l = sb("w1h", [P, KT, INTER], F32R), sb("w1l", [P, KT, INTER], F32R)
        w2h, w2l = sb("w2h", [P, KT, INTER], F32R), sb("w2l", [P, KT, INTER], F32R)
        w3h, w3l = sb("w3h", [P, D], F32R), sb("w3l", [P, D], F32R)
        b12s, b12 = sb("b12s", [P, 2]), sb("b12", [P, 2, 2])
        act1 = sb("act1", [P, 2, SEQ])
        hf = sb("hf", [P, 2, SEQ])
        hh, hl = sb("hh", [P, 2, SEQ], F32R), sb("hl", [P, 2, SEQ], F32R)

        chain, r_in, r_split, r_mm, r_exp, g_mm, g_cp, b_mm, b_add = (
            k.sem("mo_" + n) for n in "chain r_in r_split r_mm r_exp g_mm g_cp b_mm b_add".split())
        pers = dict(up_mm=4, out_mm=TT, silu=2, h=2, x_add=TT, gate=1, h_hi=2, h_lo=2, w_hi=3, w_lo=3, b_cp=1)
        s = {n: k.sem("mo_" + n) for n in pers}
        for n in pers:
            s[n].start(pers[n])
        w_in = {n: k.sem("mo_in_" + n) for n in ("w1", "w2", "w3")}
        up = k.bank[0:4]
        ob = k.bank[4:8]
        block = st.enter_context(nc.Block())

        def waits(eng, e):
            def w(n, count):
                eng.wait_ge(s[n].sem, pers[n] * (e + 1) + count)
            return w

        @block.sync
        def _(sp):
            sp.dma_start(rw[:, :, :], d["router_w"]).then_inc(r_in.sem, 16)
            sp.dma_start(rows[:, :, :], d["router_rows"].partition_broadcast(P)).then_inc(r_in.sem, 16)
            sp.dma_start(tri_g[:, :, :], d["tri_g"].partition_broadcast(P)).then_inc(r_in.sem, 16)
            sp.dma_start(tri_e[:, :, :], d["tri_e"].partition_broadcast(P)).then_inc(r_in.sem, 16)
            sp.dma_start(b3[:, :], d["b3"]).then_inc(r_in.sem, 16)
            with sp.Fori(0, SLABS) as e:
                w = waits(sp, e)
                w("w_lo", -2)
                w("b_cp", 0)
                sp.dma_start(w1s[:, :, :], d["ew1"][bass.ds(e, 1)].rearrange("a p k n -> p (a k) n")).then_inc(w_in["w1"].sem, 16)
                sp.dma_start(b12s[:, :], d["eb12"][bass.ds(e, 1)].rearrange("a p n -> p (a n)")).then_inc(w_in["w1"].sem, 16)
                w("w_lo", -1)
                sp.dma_start(w2s[:, :, :], d["ew2"][bass.ds(e, 1)].rearrange("a p k n -> p (a k) n")).then_inc(w_in["w2"].sem, 16)
                w("w_lo", 0)
                sp.dma_start(w3s[:, :], d["ew3"][bass.ds(e, 1)].rearrange("a p n -> p (a n)")).then_inc(w_in["w3"].sem, 16)

        @block.tensor
        def _(pe):
            pe.wait_ge(r_split.sem, 2)
            for t in range(TT):
                for a in range(KT):
                    ins = matmul3(nc, ob[0][:, t * E:(t + 1) * E], k.xTh[:, a, t * P:(t + 1) * P], k.xTl[:, a, t * P:(t + 1) * P],
                                  rwh[:, a, :], rwl[:, a, :], a == 0, a == KT - 1)
            ins.then_inc(r_mm.sem, 1)
            pe.sem_inc(s["up_mm"].sem, 4)
            pe.sem_inc(s["out_mm"].sem, TT)
            with pe.Fori(0, SLABS) as e:
                w = waits(pe, e)
                for half in range(BATCH):
                    tok = slice(half * SEQ, (half + 1) * SEQ)
                    for n, (wh, wl) in enumerate(((w1h, w1l), (w2h, w2l))):
                        w("h", half - 1)
                        w("w_lo", n + 1)
                        for a in range(KT):
                            ins = matmul3(nc, up[2 * half + n][:, :], wh[:, a, :], wl[:, a, :], k.xTh[:, a, tok],
                                          k.xTl[:, a, tok], a == 0, a == KT - 1)
                        ins.then_inc(s["up_mm"].sem, 1)
                w("w_lo", 3)
                for t in range(TT):
                    w("h_lo", t // QT + 1)
                    w("x_add", t - 3)
                    tok = slice((t % QT) * P, (t % QT + 1) * P)
                    matmul3(nc, ob[t % 4][:, :], hh[:, t // QT, tok], hl[:, t // QT, tok], w3h[:, :], w3l[:, :],
                            True, True).then_inc(s["out_mm"].sem, 1)
            for t in range(TT):
                pe.wait_ge(g_cp.sem, t)
                if t == 0:
                    pe.wait_ge(s["h"].sem, 2 * (SLABS + 1))
                    pe.wait_ge(chain.sem, 1)
                nc.tensor.transpose(up[0][0:E + 1, 0:P], gates[:, t, 0:E + 1], k.ident[:, :]).then_inc(g_mm.sem, 1)
            pe.wait_ge(s["x_add"].sem, TT * (SLABS + 1))
            pe.wait_ge(g_cp.sem, TT)
            for t in range(TT):
                if t >= 4:
                    pe.wait_ge(b_add.sem, t - 3)
                nc.tensor.matmul(ob[t % 4][:, :], gT[:, t, :], b3[:, :], start=True, stop=True).then_inc(b_mm.sem, 1)

        steps = [0]

        @block.vector
        def _(dve):
            def link(ins):
                steps[0] += 1
                ins.then_inc(chain.sem, 1)
                dve.wait_ge(chain.sem, steps[0])

            def over(ap, n):
                return ap.unsqueeze(2).broadcast_to([P, ap.shape[1], n])

            flat = lambda t: t[:, :, :].rearrange("p a b -> p (a b)")
            dve.wait_ge(r_in.sem, 80)
            nc.vector.tensor_copy(rwh[:, :, :], rw[:, :, :]).then_inc(r_split.sem, 1)
            dve.wait_ge(r_split.sem, 1)
            nc.vector.tensor_tensor(rwl[:, :, :], rw[:, :, :], rwh[:, :, :].bitcast(F32), ALU.subtract).then_inc(r_split.sem, 1)
            dve.wait_ge(r_mm.sem, 1)
            link(nc.vector.tensor_tensor(z[:, :, :], ob[0][:, 0:TT * E].rearrange("p (t e) -> p t e", t=TT),
                                         rows[:, 0:1, :].broadcast_to([P, TT, E]), ALU.add))
            link(nc.vector.tensor_reduce(mx[:, :], z[:, :, :], AX, ALU.max))
            link(nc.vector.tensor_tensor(z[:, :, :], z[:, :, :], over(mx[:, :], E), ALU.subtract))
            dve.wait_ge(r_exp.sem, 1)
            link(nc.vector.tensor_reduce(sm[:, :], sc[:, :, :], AX, ALU.add))
            link(nc.vector.reciprocal(ri[:, :], sm[:, :]))
            link(nc.vector.tensor_tensor(sc[:, :, :], sc[:, :, :], over(ri[:, :], E), ALU.mult))
            link(nc.vector.tensor_tensor(sc[:, :, :], sc[:, :, :], rows[:, 1:2, :].broadcast_to([P, TT, E]), ALU.add))
            link(nc.vector.tensor_reduce(gm[:, :, :], sc[:, :, :].rearrange("p t (g n) -> p t g n", g=G), AX, ALU.max))

            def choose(vals, n, cmp, cmp2, tri, rank, chosen, limit):
                mine = vals[:, :, :].rearrange("p t n -> p (t n)").unsqueeze(2).broadcast_to([P, TT * n, n])
                for t in range(TT):
                    theirs = vals[:, t:t + 1, :].broadcast_to([P, n, n])
                    own = mine[:, t * n:(t + 1) * n, :]
                    nc.vector.tensor_tensor(cmp[:, t * n:(t + 1) * n, :], theirs, own, ALU.is_gt)
                    ins = nc.vector.tensor_tensor(cmp2[:, t * n:(t + 1) * n, :], theirs, own, ALU.is_equal)
                link(ins)
                for t in range(TT):
                    ins = nc.vector.tensor_tensor(cmp2[:, t * n:(t + 1) * n, :], cmp2[:, t * n:(t + 1) * n, :], tri[:, :, :], ALU.mult)
                link(ins)
                link(nc.vector.tensor_tensor(cmp[:, :, :], cmp[:, :, :], cmp2[:, :, :], ALU.add))
                link(nc.vector.tensor_reduce(rank[:, :, :].rearrange("p t n -> p (t n)"), cmp[:, :, :], AX, ALU.add))
                link(nc.vector.tensor_scalar(chosen[:, :, :], rank[:, :, :], float(limit), None, ALU.is_lt))

            choose(gm, G, cg, cg2, tri_g, rg, keep, 2)
            link(nc.vector.tensor_scalar(pen[:, :, :], keep[:, :, :], -MASKED, MASKED, ALU.mult, ALU.add))
            link(nc.vector.tensor_tensor(z[:, :, :].rearrange("p t (g n) -> p (t g) n", g=G),
                                         sc[:, :, :].rearrange("p t (g n) -> p (t g) n", g=G), over(flat(keep), EG), ALU.mult))
            link(nc.vector.tensor_tensor(z[:, :, :].rearrange("p t (g n) -> p (t g) n", g=G),
                                         z[:, :, :].rearrange("p t (g n) -> p (t g) n", g=G), over(flat(pen), EG), ALU.add))
            choose(z, E, ce, ce2, tri_e, re_, re_, 2)
            nc.vector.memset(gates[:, :, E:SLABS], 1.0)
            link(nc.vector.tensor_tensor(gates[:, :, 0:E], sc[:, :, :], re_[:, :, :], ALU.mult))
            link(nc.vector.tensor_copy(gates_e[:, :, :], gates[:, :, :].rearrange("p t e -> p e t")))

            for n in ("h", "x_add", "gate"):
                dve.sem_inc(s[n].sem, pers[n])
            with dve.Fori(0, SLABS) as e:
                w = waits(dve, e)
                w("x_add", 0)
                nc.vector.tensor_copy(gate[:, :], gates_e[:, bass.ds(e, 1), :].rearrange("p a t -> p (a t)")).then_inc(s["gate"].sem, 1)
                for half in range(BATCH):
                    w("silu", half + 1)
                    w("up_mm", 2 * half + 2)
                    w("h_lo", half - 1)
                    nc.vector.scalar_tensor_tensor(out=hf[:, half, :], in0=up[2 * half + 1][:, :], scalar=b12[:, 1, 0:1],
                                                   in1=act1[:, half, :], op0=ALU.add, op1=ALU.mult).then_inc(s["h"].sem, 1)
                w("gate", 1)
                for t in range(TT):
                    w("out_mm", t + 1)
                    nc.vector.scalar_tensor_tensor(out=k.x[:, t, :], in0=ob[t % 4][:, :], scalar=gate[:, t:t + 1],
                                                   in1=k.x[:, t, :], op0=ALU.mult, op1=ALU.add).then_inc(s["x_add"].sem, 1)
            for t in range(TT):
                dve.wait_ge(g_mm.sem, t + 1)
                nc.vector.tensor_copy(gT[:, t, :], up[0][0:E + 1, 0:P]).then_inc(g_cp.sem, 1)
            for t in range(TT):
                dve.wait_ge(b_mm.sem, t + 1)
                nc.vector.tensor_tensor(k.x[:, t, :], ob[t % 4][:, :], k.x[:, t, :], ALU.add).then_inc(b_add.sem, 1)

        @block.scalar
        def _(act):
            act.wait_ge(chain.sem, 3)
            nc.scalar.activation(sc[:, :, :], z[:, :, :], ACT.Exp).then_inc(r_exp.sem, 1)
            for n in ("silu", "h_hi", "w_hi", "b_cp"):
                act.sem_inc(s[n].sem, pers[n])
            with act.Fori(0, SLABS) as e:
                w = waits(act, e)

                def weight_high(n, src, hi):
                    act.wait_ge(w_in[f"w{n + 1}"].sem, (32 if n == 0 else 16) * (e + 1))
                    w("up_mm", (-1, 0)[n]) if n < 2 else w("out_mm", 0)
                    w("w_lo", n + 1 - 3)
                    nc.scalar.activation(hi, src, ACT.Copy).then_inc(s["w_hi"].sem, 1)

                weight_high(0, w1s[:, :, :], w1h[:, :, :])
                w("h", 0)
                nc.scalar.activation(b12[:, :, 0], b12s[:, :], ACT.Copy).then_inc(s["b_cp"].sem, 1)
                weight_high(1, w2s[:, :, :], w2h[:, :, :])
                w("b_cp", 1)
                for half in range(BATCH):
                    w("up_mm", 2 * half + 1)
                    w("h", half - 1)
                    nc.scalar.activation(act1[:, half, :], up[2 * half][:, :], ACT.Silu, bias=b12[:, 0, 0:1]).then_inc(s["silu"].sem, 1)
                    if half == 0:
                        weight_high(2, w3s[:, :], w3h[:, :])
                for half in range(BATCH):
                    w("h", half + 1)
                    w("out_mm", -4 if half == 0 else 0)
                    nc.scalar.activation(hh[:, half, :], hf[:, half, :], ACT.Copy).then_inc(s["h_hi"].sem, 1)

        @block.gpsimd
        def _(pool):
            for n in ("h_lo", "w_lo"):
                pool.sem_inc(s[n].sem, pers[n])
            with pool.Fori(0, SLABS) as e:
                w = waits(pool, e)

                def weight_low(n, src, hi, lo):
                    w("w_hi", n + 1)
                    nc.gpsimd.tensor_tensor(lo, src, hi.bitcast(F32), ALU.subtract).then_inc(s["w_lo"].sem, 1)

                weight_low(0, w1s[:, :, :], w1h[:, :, :], w1l[:, :, :])
                weight_low(1, w2s[:, :, :], w2h[:, :, :], w2l[:, :, :])
                weight_low(2, w3s[:, :], w3h[:, :], w3l[:, :])
                for half in range(BATCH):
                    w("h_hi", half + 1)
                    nc.gpsimd.tensor_tensor(hl[:, half, :], hf[:, half, :], hh[:, half, :].bitcast(F32), ALU.subtract).then_inc(s["h_lo"].sem, 1)


SLOTS = 6
Q_H, Q_M, Q_L = slice(0, 3), slice(3, 6, 2), slice(4, 5)
K_H, K_M, K_L = slice(2, 5), slice(1, 6, 4), slice(0, 1)


def by_slot(stack, slots, dh):
    return stack.rearrange("p h (s e) -> p h s e", e=dh)[:, :, slots, :]


def into_slots(part, copies):
    return part.unsqueeze(2).broadcast_to([part.shape[0], part.shape[1], copies, part.shape[2]])


def narrow_attention(k, name, turns, dh, causal, staging, q_tile, k_tile, v_tile, outs, shared_kv, divisor):
    nc = k.nc
    UNITS = 8
    ROWS = SLOTS * dh
    KV = UNITS // 4 if shared_kv else UNITS
    PER_KV = UNITS // KV
    SM = 4 * UNITS
    keys = [(i + 1) * P if causal else SEQ for i in range(QT)]
    first = [j if causal else 0 for j in range(QT)]
    row_off = [sum(keys[:i]) for i in range(QT + 1)]
    col_off = [sum((QT - first[m]) * P for m in range(j)) for j in range(QT + 1)]
    ORDER = [3, 2, 1, 0]

    def ahead(u):
        n = u + 1
        if n >= UNITS:
            return []
        return ([f"K{n // PER_KV}"] if n % PER_KV == 0 else []) + [f"Q{n}"]

    t_seq = ahead(-1)
    for u in range(UNITS + 1):
        if u >= 1:
            t_seq += [f"P{u - 1}.{j}" for j in range(QT)]
        t_seq += ahead(u)
    t_at = {a: n for n, a in enumerate(t_seq)}
    TR = len(t_seq)
    assert TR % 3 == 0
    act_seq, dve_seq = t_seq[3::2], t_seq[0:2] + t_seq[2::2]
    STAGED = len(staging(0))
    with ExitStack() as st:
        def sb(nm, shape, dt=F32):
            return k.sb(name + nm, shape, dt, st)

        qT, kT = sb("qT", [ROWS, UNITS, SEQ], BF16), sb("kT", [ROWS, KV, SEQ], BF16)
        probs, pt = sb("probs", [P, 2, row_off[QT]]), sb("pt", [P, 2, col_off[QT]])
        negmax = sb("negmax", [P, QT, UNITS])
        rowsum, rinv = sb("rowsum", [P, QT, UNITS]), sb("rinv", [P, QT, UNITS])
        sbank, tbank, obank = k.bank[0:3] + k.bank[7:8], k.bank[3:6], k.bank[6]
        pers = dict(s_mm=SM, t_mm=TR, pv_mm=UNITS, maxed=SM, t_dve=len(dve_seq), o_norm=1, rinv_ok=2,
                    exp_ok=SM, t_act=len(act_seq), staged=STAGED)
        s = {n: k.sem(name + "_" + n) for n in pers}
        due = {n: s[n].start(pers[n]) for n in pers}
        base = {n: s[n].base for n in pers}
        block = st.enter_context(nc.Block())

        def credit(eng, *names):
            for n in names:
                if due[n]:
                    eng.sem_inc(s[n].sem, pers[n])

        def waits(eng, g):
            def w(n, count):
                eng.wait_ge(s[n].sem, base[n] + pers[n] * (g + 1) + count)
            return w

        def copied(w, n):
            a, before = t_seq[n], n < 0
            if a in act_seq:
                w("t_act", act_seq.index(a) + 1 - before * len(act_seq))
            else:
                w("t_dve", dve_seq.index(a) + 1 - before * len(dve_seq))

        def copy_out(eng_copy, w, a):
            n = t_at[a]
            w("t_mm", n + 1)
            if a[0] == "P":
                u, j = int(a[1]), int(a[3])
                w("pv_mm", u - 1)
                return eng_copy(pt[:, u % 2, col_off[j]:col_off[j + 1]], tbank[n % 3][:, first[j] * P:SEQ])
            i = int(a[1])
            w("s_mm", 4 * (i + 1) * (PER_KV if a[0] == "K" else 1) - SM)
            return eng_copy((qT if a[0] == "Q" else kT)[:, i, :], tbank[n % 3][0:ROWS, :])

        @block.gpsimd
        def _(pool):
            credit(pool, "staged")
            with pool.Fori(0, turns) as g:
                w = waits(pool, g)
                for n, (dst, src) in enumerate(staging(g)):
                    if n == 0:
                        w("t_mm", t_at[f"Q{UNITS - 1}"] + 1 - TR)
                    if n == STAGED - 1:
                        w("pv_mm", 0)
                    nc.gpsimd.tensor_copy(dst, src).then_inc(s["staged"].sem, 1)

        @block.tensor
        def _(pe):
            credit(pe, "s_mm", "t_mm", "pv_mm")
            with pe.Fori(0, turns) as g:
                w = waits(pe, g)

                def turn_stack(a):
                    n, i = t_at[a], int(a[1])
                    copied(w, n - 3)
                    for t in range(QT):
                        tile = q_tile(i, t) if a[0] == "Q" else k_tile(i, t)
                        ins = nc.tensor.matmul(tbank[n % 3][0:ROWS, t * P:(t + 1) * P], tile, k.identb[:, :], start=True, stop=True)
                    ins.then_inc(s["t_mm"].sem, 1)

                def scores(u, n):
                    i, m, kv = ORDER[n], 4 * u + n, u // PER_KV
                    w("exp_ok", m - 3)
                    if n == 0:
                        copied(w, t_at[f"Q{u}"])
                        copied(w, t_at[f"K{kv}"])
                    ins = nc.tensor.matmul(sbank[n][:, 0:keys[i]], qT[:, u, i * P:(i + 1) * P], kT[:, kv, 0:keys[i]],
                                           start=True, stop=not causal)
                    if causal:
                        ins = nc.tensor.matmul(sbank[n][:, i * P:keys[i]], k.identb[:, :], k.maskb[:, :],
                                               start=False, stop=True)
                    ins.then_inc(s["s_mm"].sem, 1)

                def turn_probs(u, j):
                    n = t_at[f"P{u}.{j}"]
                    copied(w, n - 3)
                    if j == 0:
                        w("exp_ok", 4 * u + 4)
                    for i in range(first[j], QT):
                        ins = nc.tensor.transpose(tbank[n % 3][:, i * P:(i + 1) * P],
                                                  probs[:, u % 2, row_off[i] + j * P:row_off[i] + (j + 1) * P], k.ident[:, :])
                    ins.then_inc(s["t_mm"].sem, 1)

                def values(u):
                    copied(w, t_at[f"P{u}.2"])
                    copied(w, t_at[f"P{u}.3"])
                    if u == 0:
                        w("staged", STAGED)
                        w("o_norm", 0)
                    for i in range(QT):
                        out = obank[:, (i * UNITS + u) * dh:(i * UNITS + u + 1) * dh]
                        seen = keys[i] // P
                        for j in range(seen):
                            at = col_off[j] + (i - first[j]) * P
                            ins = nc.tensor.matmul(out, pt[:, u % 2, at:at + P], v_tile(u, j), start=(j == 0), stop=(j == seen - 1))
                    ins.then_inc(s["pv_mm"].sem, 1)

                w("staged", STAGED - 1)
                for a in ahead(-1):
                    turn_stack(a)
                for u in range(UNITS + 2):
                    if u < UNITS:
                        scores(u, 0)
                        scores(u, 1)
                    if 1 <= u <= UNITS:
                        turn_probs(u - 1, 0)
                        turn_probs(u - 1, 1)
                    if u < UNITS:
                        scores(u, 2)
                    if 1 <= u <= UNITS:
                        turn_probs(u - 1, 2)
                        turn_probs(u - 1, 3)
                    if u < UNITS:
                        scores(u, 3)
                    for a in ahead(u):
                        turn_stack(a)
                    if u >= 2:
                        values(u - 2)

        @block.vector
        def _(dve):
            credit(dve, "maxed", "t_dve", "o_norm", "rinv_ok")
            with dve.Fori(0, turns) as g:
                w = waits(dve, g)

                def row_max(u, n):
                    i, m = ORDER[n], 4 * u + n
                    w("s_mm", m + 1)
                    nc.vector.tensor_reduce(negmax[:, i, u:u + 1], sbank[n][:, 0:keys[i]], AX, ALU.max,
                                            negate=True).then_inc(s["maxed"].sem, 1)

                def copy(*stacks):
                    for a in stacks:
                        if a in dve_seq:
                            copy_out(nc.vector.tensor_copy, w, a).then_inc(s["t_dve"].sem, 1)

                copy(*ahead(-1))
                for u in range(UNITS + 1):
                    if u < UNITS:
                        row_max(u, 0)
                        row_max(u, 1)
                    if u >= 1:
                        copy(f"P{u - 1}.0", f"P{u - 1}.1")
                    if u < UNITS:
                        row_max(u, 2)
                    if u >= 1:
                        copy(f"P{u - 1}.2", f"P{u - 1}.3")
                    if u < UNITS:
                        row_max(u, 3)
                    copy(*ahead(u))
                w("exp_ok", SM)
                nc.vector.tensor_scalar(rinv[:, :, :], rowsum[:, :, :], float(divisor), None, ALU.mult).then_inc(s["rinv_ok"].sem, 1)
                w("rinv_ok", 1)
                nc.vector.reciprocal(rinv[:, :, :], rinv[:, :, :]).then_inc(s["rinv_ok"].sem, 1)
                w("pv_mm", UNITS)
                w("rinv_ok", 2)
                nc.vector.tensor_tensor(outs(g), obank[:, 0:QT * UNITS * dh].rearrange("p (m h e) -> p m h e", h=4, e=dh),
                                        rinv[:, :, :].rearrange("p i (b h) -> p (i b) h", h=4).unsqueeze(3).broadcast_to([P, 2 * QT, 4, dh]),
                                        ALU.mult).then_inc(s["o_norm"].sem, 1)

        @block.scalar
        def _(act):
            credit(act, "exp_ok", "t_act")
            with act.Fori(0, turns) as g:
                w = waits(act, g)

                def exps(u, n):
                    i, m = ORDER[n], 4 * u + n
                    w("maxed", m + 1)
                    if n == 0:
                        w("t_mm", t_at[f"P{u - 2}.3"] + 1 if u >= 2 else t_at[f"P{u + UNITS - 2}.3"] + 1 - TR)
                        w("o_norm", 0)
                    nc.scalar.activation(probs[:, u % 2, row_off[i]:row_off[i + 1]], sbank[n][:, 0:keys[i]], ACT.Exp,
                                         bias=negmax[:, i, u:u + 1], accum_out=rowsum[:, i, u:u + 1]).then_inc(s["exp_ok"].sem, 1)

                def copy(*stacks):
                    for a in stacks:
                        if a in act_seq:
                            copy_out(lambda o, i: nc.scalar.activation(o, i, ACT.Copy), w, a).then_inc(s["t_act"].sem, 1)

                for u in range(UNITS + 1):
                    if u < UNITS:
                        exps(u, 0)
                        exps(u, 1)
                    if u >= 1:
                        copy(f"P{u - 1}.0", f"P{u - 1}.1")
                    if u < UNITS:
                        exps(u, 2)
                    if u >= 1:
                        copy(f"P{u - 1}.2", f"P{u - 1}.3")
                    if u < UNITS:
                        exps(u, 3)
                    copy(*ahead(u))

        for n in pers:
            s[n].base += pers[n] * turns


def copy_parts(nc, part, q, kk, q_stack, k_stack, dh):
    q_slots, k_slots, copies = (Q_H, K_H, 3) if part == "high" else (Q_M, K_M, 2)
    nc.scalar.activation(by_slot(q_stack, q_slots, dh), into_slots(q, copies), ACT.Copy)
    return nc.scalar.activation(by_slot(k_stack, k_slots, dh), into_slots(kk, copies), ACT.Copy)


def subtract_parts(nc, part, q, kk, q_stack, k_stack, dh, rest=None):
    q_at, k_at = (Q_H, K_H) if part == "high" else (Q_M, K_M)
    q_rest, k_rest = rest or (by_slot(q_stack, Q_L, dh)[:, :, 0, :], by_slot(k_stack, K_L, dh)[:, :, 0, :])
    eng = nc.gpsimd if rest else nc.vector
    eng.tensor_tensor(q_rest, q, by_slot(q_stack, q_at, dh)[:, :, 0, :], ALU.subtract)
    return eng.tensor_tensor(k_rest, kk, by_slot(k_stack, k_at, dh)[:, :, 0, :], ALU.subtract)


def narrow_layer0(k, d):
    nc = k.nc
    DH, H, NQKV, RANKS = 8, 8, 192, 48
    with ExitStack() as outer:
        def keep(nm, shape, dt=F32):
            return k.sb("n0" + nm, shape, dt, outer)

        qk = keep("qk", [P, 2, BATCH, QT * H, SLOTS * DH], BF16)
        vr = keep("vr", [P, BATCH, QT, H * DH])
        qk_st = keep("qk_st", [P, 2, QT, H, SLOTS * DH], BF16)
        v_st = keep("v_st", [P, QT, H * DH])
        outs = keep("outs", [P, BATCH, QT * H, DH])
        wo = keep("wo", [H * DH, D])
        with ExitStack() as st:
            def sb(nm, shape, dt=F32):
                return k.sb("n0" + nm, shape, dt, st)

            wa, wah, wal = sb("wa", [P, KT, NQKV]), sb("wah", [P, KT, NQKV], F32R), sb("wal", [P, KT, NQKV], F32R)
            wf, wfh, wfl = sb("wf", [P, KT, D]), sb("wfh", [P, KT, D], F32R), sb("wfl", [P, KT, D], F32R)
            la, lah, lal = sb("la", [P, KT, P]), sb("lah", [P, KT, P], F32R), sb("lal", [P, KT, P], F32R)
            lb = sb("lb", [66, D])
            uT = sb("uT", [66, TOK])
            qkvb = sb("qkvb", [P, NQKV])
            qk_sum, qk_rest = sb("qk_sum", [P, 2, 2 * H, DH]), sb("qk_rest", [P, 2, 2 * H, DH])
            starts, startsf, cmp = sb("starts", [P, 4], I32), sb("startsf", [P, 4]), sb("cmp", [P, BATCH, 4])
            cnt, kcol, amask = sb("cnt", [P, BATCH]), sb("kcol", [P, 1]), sb("amask", [P, BATCH])
            a_in, f_in, c_in, hi, lo, chain, q_mm, q_out, u_mm, u_out, y_mm, y_out, ones = (
                k.sem("n0_" + n) for n in "a_in f_in c_in hi lo chain q_mm q_out u_mm u_out y_mm y_add ones".split())
            summed, high, rest, middle, low = (k.sem("n0_stack_" + n) for n in "sum high rest middle low".split())
            parts = ((wa, wah, wal), (la, lah, lal), (wf, wfh, wfl))

            def stacks(t):
                heads = slice((t % QT) * H, (t % QT + 1) * H)
                return qk[:, 0, t // QT, heads, :], qk[:, 1, t // QT, heads, :]

            block = st.enter_context(nc.Block())

            @block.sync
            def _(sp):
                sp.dma_start(wa[:, :, :], d["L0_wqkv"]).then_inc(a_in.sem, 16)
                sp.dma_start(la[:, :, :], d["L0_la"]).then_inc(f_in.sem, 16)
                sp.dma_start(wf[:, :, :], d["L0_wf"]).then_inc(f_in.sem, 16)
                sp.dma_start(lb[:, :], d["L0_lb"]).then_inc(c_in.sem, 16)
                sp.dma_start(qkvb[:, :], d["L0_qkvb"].partition_broadcast(P)).then_inc(c_in.sem, 16)
                sp.dma_start(starts[:, :], d["L0_starts"].partition_broadcast(P)).then_inc(c_in.sem, 16)
                sp.dma_start(kcol[:, :], d["L0_kcol"]).then_inc(c_in.sem, 16)
                sp.dma_start(wo[:, :], d["L0_wo"]).then_inc(c_in.sem, 16)

            @block.scalar
            def _(act):
                act.wait_ge(a_in.sem, 16)
                for n, (src, h, _) in enumerate(parts):
                    if n == 1:
                        act.wait_ge(f_in.sem, 32)
                    nc.scalar.activation(h[:, :, :], src[:, :, :], ACT.Copy).then_inc(hi.sem, 1)

                def high_part(t):
                    act.wait_ge(summed.sem, t + 1)
                    copy_parts(nc, "high", qk_sum[:, t % 2, 0:H, :], qk_sum[:, t % 2, H:, :], *stacks(t), DH).then_inc(high.sem, 1)

                high_part(0)
                for t in range(TT):
                    if t + 1 < TT:
                        high_part(t + 1)
                    act.wait_ge(rest.sem, t + 1)
                    copy_parts(nc, "middle", qk_rest[:, t % 2, 0:H, :], qk_rest[:, t % 2, H:, :], *stacks(t), DH).then_inc(middle.sem, 1)

            @block.gpsimd
            def _(pool):
                for n, (src, h, l) in enumerate(parts):
                    pool.wait_ge(hi.sem, n + 1)
                    nc.gpsimd.tensor_tensor(l[:, :, :], src[:, :, :], h[:, :, :].bitcast(F32), ALU.subtract).then_inc(lo.sem, 1)
                for t in range(TT):
                    pool.wait_ge(high.sem, t + 1)
                    if t >= 2:
                        pool.wait_ge(low.sem, t - 1)
                    subtract_parts(nc, "high", qk_sum[:, t % 2, 0:H, :], qk_sum[:, t % 2, H:, :], *stacks(t), DH,
                                   (qk_rest[:, t % 2, 0:H, :], qk_rest[:, t % 2, H:, :])).then_inc(rest.sem, 1)

            @block.tensor
            def _(pe):
                pe.wait_ge(lo.sem, 1)
                for t in range(TT):
                    if t >= 2:
                        pe.wait_ge(q_out.sem, t - 1)
                    tok = slice(t * P, (t + 1) * P)
                    for a in range(KT):
                        ins = matmul3(nc, k.bank[t % 2][:, 0:NQKV], k.xTh[:, a, tok], k.xTl[:, a, tok],
                                      wah[:, a, :], wal[:, a, :], a == 0, a == KT - 1)
                    ins.then_inc(q_mm.sem, 1)
                pe.wait_ge(lo.sem, 2)
                for b in range(BATCH):
                    tok = slice(b * SEQ, (b + 1) * SEQ)
                    for a in range(KT):
                        ins = matmul3(nc, k.bank[2 + b][:, :], lah[:, a, :], lal[:, a, :], k.xTh[:, a, tok],
                                      k.xTl[:, a, tok], a == 0, a == KT - 1)
                    ins.then_inc(u_mm.sem, 1)
                pe.wait_ge(lo.sem, 3)
                pe.wait_ge(ones.sem, 1)
                pe.wait_ge(c_in.sem, 80)
                for t in range(TT):
                    if t >= 4:
                        pe.wait_ge(y_out.sem, t - 3)
                    tok, bank = slice(t * P, (t + 1) * P), k.bank[4 + t % 4]
                    for a in range(KT):
                        matmul3(nc, bank[:, :], k.xTh[:, a, tok], k.xTl[:, a, tok], wfh[:, a, :], wfl[:, a, :], a == 0, False)
                    pe.wait_ge(u_out.sem, t // QT + 1)
                    nc.tensor.matmul(bank[:, :], uT[:, tok], lb[:, :], start=False, stop=True).then_inc(y_mm.sem, 1)

            @block.vector
            def _(dve):
                steps = [0]

                def link(ins):
                    steps[0] += 1
                    ins.then_inc(chain.sem, 1)
                    dve.wait_ge(chain.sem, steps[0])

                nc.vector.memset(uT[64:66, :], 1.0).then_inc(ones.sem, 1)
                dve.wait_ge(c_in.sem, 80)
                link(nc.vector.tensor_copy(startsf[:, :], starts[:, :]))
                for b in range(BATCH):
                    ins = nc.vector.tensor_scalar(cmp[:, b, :], startsf[:, :], float(b), None, ALU.is_le)
                link(ins)
                link(nc.vector.tensor_reduce(cnt[:, :], cmp[:, :, :], AX, ALU.add))
                link(nc.vector.tensor_tensor(amask[:, :], cnt[:, :], kcol[:, :].broadcast_to([P, BATCH]), ALU.is_equal))

                def low_part(t):
                    dve.wait_ge(middle.sem, t + 1)
                    subtract_parts(nc, "middle", qk_rest[:, t % 2, 0:H, :], qk_rest[:, t % 2, H:, :], *stacks(t), DH).then_inc(low.sem, 1)

                for t in range(TT):
                    b, tt = t // QT, t % QT
                    dve.wait_ge(q_mm.sem, t + 1)
                    if t >= 2:
                        dve.wait_ge(rest.sem, t - 1)
                    both = k.bank[t % 2][:, 0:P].rearrange("p (h e z) -> p h e z", h=H, e=DH)
                    qb = qkvb[:, 0:P].rearrange("p (h e z) -> p h e z", h=H, e=DH)
                    for z in range(2):
                        ins = nc.vector.tensor_tensor(qk_sum[:, t % 2, z * H:(z + 1) * H, :], both[:, :, :, z], qb[:, :, :, z], ALU.add)
                    ins.then_inc(summed.sem, 1)
                    nc.vector.tensor_tensor(vr[:, b, tt, :], k.bank[t % 2][:, P:NQKV], qkvb[:, P:NQKV], ALU.add).then_inc(q_out.sem, 1)
                    if t >= 2:
                        low_part(t - 2)
                low_part(TT - 2)
                low_part(TT - 1)
                for b in range(BATCH):
                    dve.wait_ge(u_mm.sem, b + 1)
                    nc.vector.tensor_scalar(uT[0:64, b * SEQ:(b + 1) * SEQ], k.bank[2 + b][0:64, :], amask[0:64, b:b + 1], None,
                                            ALU.mult).then_inc(u_out.sem, 1)
                for t in range(TT):
                    dve.wait_ge(y_mm.sem, t + 1)
                    nc.vector.tensor_tensor(k.x[:, t, :], k.bank[4 + t % 4][:, :], k.x[:, t, :], ALU.add).then_inc(y_out.sem, 1)

        def turn_outs(g):
            return outs[:, bass.ds(g, 1), :, :].rearrange("p g (m h) e -> p (g m) h e", h=4)

        def staging(g):
            return [(qk_st[:, z, :, :, :].rearrange("p t h r -> p (t h r)").bitcast(I32),
                     qk[:, z, bass.ds(g, 1), :, :].rearrange("p b h r -> p (b h r)").bitcast(I32)) for z in range(2)] + [
                    (v_st[:, :, :].rearrange("p t e -> p (t e)"), vr[:, bass.ds(g, 1), :, :].rearrange("p b t e -> p (b t e)"))]

        narrow_attention(k, "n0", BATCH, DH, False, staging, lambda u, t: qk_st[:, 0, t, u, :], lambda u, t: qk_st[:, 1, t, u, :],
                         lambda u, t: v_st[:, t, u * DH:(u + 1) * DH], turn_outs, False, float(H * DH) ** 0.5)
        project_narrow(k, "n0", wo, 1, H * DH, lambda t, a: outs[:, t // QT, (t % QT) * H:(t % QT + 1) * H, :].rearrange("p h e -> p (h e)"))


def project_narrow(k, name, wo, chunks, rows, piece):
    nc = k.nc
    with ExitStack() as st:
        oT = k.sb(name + "oT", [rows, 2, chunks, P], F32, st)
        turned, copied, mm, added = (k.sem("pn_" + n) for n in "turned copied mm added".split())
        b = [s.base for s in (turned, copied, mm, added)]
        block = st.enter_context(nc.Block())

        @block.tensor
        def _(pe):
            def turn(t):
                if t >= 2:
                    pe.wait_ge(copied.sem, b[1] + t - 1)
                for a in range(chunks):
                    ins = nc.tensor.transpose(k.bank[t % 2][0:rows, a * P:(a + 1) * P], piece(t, a), k.ident[:, :])
                ins.then_inc(turned.sem, 1)

            turn(0)
            for t in range(TT):
                if t + 1 < TT:
                    turn(t + 1)
                pe.wait_ge(copied.sem, b[1] + t + 1)
                if t >= 4:
                    pe.wait_ge(added.sem, b[3] + t - 3)
                for a in range(chunks):
                    w = wo[:, :] if chunks == 1 else wo[:, a, :]
                    ins = nc.tensor.matmul(k.bank[4 + t % 4][:, :], oT[:, t % 2, a, :], w, start=(a == 0), stop=(a == chunks - 1))
                ins.then_inc(mm.sem, 1)

        @block.scalar
        def _(act):
            for t in range(TT):
                act.wait_ge(turned.sem, b[0] + t + 1)
                if t >= 2:
                    act.wait_ge(mm.sem, b[2] + t - 1)
                nc.scalar.activation(oT[:, t % 2, :, :], k.bank[t % 2][0:rows, 0:chunks * P].rearrange("p (a q) -> p a q", a=chunks),
                                     ACT.Copy).then_inc(copied.sem, 1)

        @block.vector
        def _(dve):
            for t in range(TT):
                dve.wait_ge(mm.sem, b[2] + t + 1)
                nc.vector.tensor_tensor(k.x[:, t, :], k.bank[4 + t % 4][:, :], k.x[:, t, :], ALU.add).then_inc(added.sem, 1)

        for s in (turned, copied, mm, added):
            s.base += TT


def narrow_attention2(k, d):
    nc = k.nc
    DH, H, G = 16, 32, 8
    NQ, NKV = H * DH, 2 * G * DH
    with ExitStack() as outer:
        def keep(nm, shape, dt=F32):
            return k.sb("n2" + nm, shape, dt, outer)

        qs, ks = keep("qs", [P, TT, H, SLOTS * DH], BF16), keep("ks", [P, TT, G, SLOTS * DH], BF16)
        vr = keep("vr", [P, TT, G, DH])
        q_st, k_st = keep("q_st", [P, TT, HPG, SLOTS * DH], BF16), keep("k_st", [P, TT, SLOTS * DH], BF16)
        v_st = keep("v_st", [P, TT, DH])
        outs = keep("outs", [P, QT * BATCH, G, 4 * DH])
        wo = keep("wo", [P, KT, D])
        with ExitStack() as st:
            def sb(nm, shape, dt=F32):
                return k.sb("n2" + nm, shape, dt, st)

            NW = NQ + NKV
            wa, wah, wal = sb("wa", [P, KT, NW]), sb("wah", [P, KT, NW], F32R), sb("wal", [P, KT, NW], F32R)
            tab = sb("tab", [P, QT, 4, DH])
            ra, rb = sb("ra", [P, 2, NQ + G * DH]), sb("rb", [P, 2, NQ + G * DH])
            qk_sum, qk_rest = sb("qk_sum", [P, 2, H + G, DH]), sb("qk_rest", [P, 2, H + G, DH])
            a_in, c_in, hi, lo, mm, rot, summed, high, rest, middle, low = (
                k.sem("n2_" + n) for n in "a_in c_in hi lo mm rot summed high rest middle low".split())
            block = st.enter_context(nc.Block())

            @block.sync
            def _(sp):
                sp.dma_start(wa[:, :, :], d["L2_wqkv"]).then_inc(a_in.sem, 16)
                sp.dma_start(tab[:, :, :, :], d["L2_tab"]).then_inc(c_in.sem, 16)
                sp.dma_start(wo[:, :, :], d["L2_wo"]).then_inc(c_in.sem, 16)

            @block.scalar
            def _(act):
                act.wait_ge(a_in.sem, 16)
                for a in range(KT):
                    nc.scalar.activation(wah[:, a, :], wa[:, a, :], ACT.Copy).then_inc(hi.sem, 1)

                def high_part(t):
                    act.wait_ge(summed.sem, t + 1)
                    copy_parts(nc, "high", qk_sum[:, t % 2, 0:H, :], qk_sum[:, t % 2, H:, :], qs[:, t, :, :], ks[:, t, :, :],
                               DH).then_inc(high.sem, 1)

                high_part(0)
                for t in range(TT):
                    if t + 1 < TT:
                        high_part(t + 1)
                    act.wait_ge(rest.sem, t + 1)
                    copy_parts(nc, "middle", qk_rest[:, t % 2, 0:H, :], qk_rest[:, t % 2, H:, :], qs[:, t, :, :], ks[:, t, :, :],
                               DH).then_inc(middle.sem, 1)

            @block.tensor
            def _(pe):
                for t in range(TT):
                    if t >= 2:
                        pe.wait_ge(rot.sem, t - 1)
                    tok = slice(t * P, (t + 1) * P)
                    for a in range(KT):
                        if t == 0:
                            pe.wait_ge(lo.sem, a + 1)
                        q, kv = k.bank[2 * (t % 2)][:, :], k.bank[2 * (t % 2) + 1][:, 0:NKV]
                        matmul3(nc, q, k.xTh[:, a, tok], k.xTl[:, a, tok], wah[:, a, 0:NQ], wal[:, a, 0:NQ], a == 0, a == KT - 1)
                        ins = matmul3(nc, kv, k.xTh[:, a, tok], k.xTl[:, a, tok], wah[:, a, NQ:], wal[:, a, NQ:], a == 0, a == KT - 1)
                    ins.then_inc(mm.sem, 1)

            @block.vector
            def _(dve):
                for a in range(KT):
                    dve.wait_ge(hi.sem, a + 1)
                    nc.vector.tensor_tensor(wal[:, a, :], wa[:, a, :], wah[:, a, :].bitcast(F32), ALU.subtract).then_inc(lo.sem, 1)
                dve.wait_ge(c_in.sem, 32)

                def low_part(t):
                    dve.wait_ge(middle.sem, t + 1)
                    subtract_parts(nc, "middle", qk_rest[:, t % 2, 0:H, :], qk_rest[:, t % 2, H:, :], qs[:, t, :, :], ks[:, t, :, :],
                                   DH).then_inc(low.sem, 1)

                for t in range(TT):
                    dve.wait_ge(mm.sem, t + 1)
                    if t >= 2:
                        dve.wait_ge(summed.sem, t - 1)
                    nc.vector.tensor_copy(vr[:, t, :, :],
                                          k.bank[2 * (t % 2) + 1][:, G * DH:NKV].rearrange("p (g e) -> p g e", g=G))
                    HF = DH // 2
                    for bank, heads, c, at in ((k.bank[2 * (t % 2)], H, 0, 0), (k.bank[2 * (t % 2) + 1], G, 2, NQ)):
                        src = bank[:, 0:heads * DH].rearrange("p (h e) -> p h e", h=heads)
                        a_ = ra[:, t % 2, at:at + heads * DH].rearrange("p (h e) -> p h e", h=heads)
                        b_ = rb[:, t % 2, at:at + heads * DH].rearrange("p (h e) -> p h e", h=heads)
                        cos = tab[:, t % QT, c:c + 1, :].broadcast_to([P, heads, DH])
                        sin = tab[:, t % QT, c + 1:c + 2, :].broadcast_to([P, heads, DH])
                        nc.vector.tensor_tensor(a_, src, cos, ALU.mult)
                        nc.vector.tensor_tensor(b_[:, :, 0:HF], src[:, :, HF:DH], sin[:, :, 0:HF], ALU.mult)
                        ins = nc.vector.tensor_tensor(b_[:, :, HF:DH], src[:, :, 0:HF], sin[:, :, HF:DH], ALU.mult)
                    ins.then_inc(rot.sem, 1)
                    if t >= 2:
                        low_part(t - 2)
                low_part(TT - 2)
                low_part(TT - 1)

            @block.gpsimd
            def _(pool):

                def add(t):
                    pool.wait_ge(rot.sem, t + 1)
                    if t >= 2:
                        pool.wait_ge(rest.sem, t - 1)
                    nc.gpsimd.tensor_tensor(qk_sum[:, t % 2, :, :].rearrange("p h e -> p (h e)"), ra[:, t % 2, :], rb[:, t % 2, :],
                                            ALU.add).then_inc(summed.sem, 1)

                add(0)
                for t in range(TT):
                    if t + 1 < TT:
                        add(t + 1)
                    pool.wait_ge(high.sem, t + 1)
                    if t >= 2:
                        pool.wait_ge(low.sem, t - 1)
                    subtract_parts(nc, "high", qk_sum[:, t % 2, 0:H, :], qk_sum[:, t % 2, H:, :], qs[:, t, :, :], ks[:, t, :, :], DH,
                                   (qk_rest[:, t % 2, 0:H, :], qk_rest[:, t % 2, H:, :])).then_inc(rest.sem, 1)

        def turn_outs(g):
            return outs[:, :, bass.ds(g, 1), :].rearrange("p m g (h e) -> p (m g) h e", h=4)

        def staging(g):
            heads = qs[:, :, :, :].rearrange("p t (g h) r -> p t g (h r)", h=HPG)[:, :, bass.ds(g, 1), :]
            return [(q_st[:, :, :, :].rearrange("p t h r -> p t (h r)").bitcast(I32), heads.rearrange("p t g r -> p (t g) r").bitcast(I32)),
                    (k_st[:, :, :].bitcast(I32), ks[:, :, bass.ds(g, 1), :].rearrange("p t g r -> p (t g) r").bitcast(I32)),
                    (v_st[:, :, :], vr[:, :, bass.ds(g, 1), :].rearrange("p t g e -> p (t g) e"))]

        narrow_attention(k, "n2", G, DH, True, staging, lambda u, t: q_st[:, (u // 4) * QT + t, u % 4, :],
                         lambda a, t: k_st[:, a * QT + t, :], lambda u, t: v_st[:, (u // 4) * QT + t, :], turn_outs, True, 1.0)

        def piece(t, a):
            m = (t % QT) * BATCH + t // QT
            return outs[:, m, 2 * a:2 * a + 2, :].rearrange("p g e -> p (g e)")

        project_narrow(k, "n2", wo, KT, P, piece)


def memory_ffn(k, d, name):
    nc = k.nc
    with ExitStack() as st:
        def sb(nm, shape, dt=F32):
            return k.sb(name + "m_" + nm, shape, dt, st)

        wq, wqh, wql = sb("wq", [P, KT, P]), sb("wqh", [P, KT, P], F32R), sb("wql", [P, KT, P], F32R)
        wu, wuh, wul = sb("wu", [P, KT, P]), sb("wuh", [P, KT, P], F32R), sb("wul", [P, KT, P], F32R)
        wr = sb("wr", [BOT, BOT])
        keysT = sb("keysT", [BOT, NSLOT])
        rkT, keysA = sb("rkT", [BOT + 1, NSLOT]), sb("keysA", [BOT + 1, NSLOT])
        qA, rqA = sb("qA", [BOT + 1, TOK]), sb("rqA", [BOT + 1, TOK])
        valsT, wvd, wvu = sb("valsT", [P, KT, NSLOT]), sb("wvd", [P, KT, VB]), sb("wvu", [VB, D])
        vw, mix = sb("vw", [VB, NSLOT]), sb("mix", [NSLOT, D])
        bu1, wu2 = sb("bu1", [P, 1]), sb("wu2", [P, 1])
        scal = sb("scal", [P, 3])
        ones = sb("ones", [P, P])
        gl = sb("gl", [P, TOK])
        lv, lsum, rl = sb("lv", [P, TT]), sb("lsum", [P, 1]), sb("rl", [P, 1])
        sg, u, gate, ge, fac = sb("sg", [P, TT]), sb("u", [P, TT]), sb("gate", [P, TT]), sb("ge", [P, TT]), sb("fac", [P, TT])
        top, rep = sb("top", [P, TT, TOPK]), sb("rep", [P, 2, NSLOT])
        att = sb("att", [P, 2, NSLOT])
        negmax, rowsum, rinv = sb("negmax", [P, TT]), sb("rowsum", [P, TT]), sb("rinv", [P, TT])
        wts, wT = sb("wts", [P, 2, NSLOT]), sb("wT", [P, 2, P])
        names = "w_in c_in hi lo pe_mm mid chain gelu q_out s_mm masked exp wt_mm wt_cp y_mm y_add lrn ln sig sig2 ones".split()
        s = {n: k.sem("m_" + n) for n in names}
        b0 = {n: s[n].base for n in names}
        counts = dict.fromkeys(names, 0)

        def inc(ins, n, by=1):
            counts[n] += by
            return ins.then_inc(s[n].sem, by)

        block = st.enter_context(nc.Block())
        B = k.bank

        @block.sync
        def _(sp):
            inc(sp.dma_start(wq[:, :, :], d[name + "m_wq"]), "w_in", 16)
            inc(sp.dma_start(wu[:, :, :], d[name + "m_wu1"]), "w_in", 16)
            for buf, n in ((wr[:, :], "wr"), (keysT[:, :], "keysT"), (valsT[:, :, :], "valsT"), (wvd[:, :, :], "wvd"), (wvu[:, :], "wvu"),
                           (bu1[:, :], "bu1"), (wu2[:, :], "wu2"), (rkT[BOT:BOT + 1, :], "log_rel"), (keysA[BOT:BOT + 1, :], "log_rel")):
                inc(sp.dma_start(buf, d[name + "m_" + n]), "c_in", 16)
            inc(sp.dma_start(scal[:, :], d[name + "m_scal"].partition_broadcast(P)), "c_in", 16)

        C_IN = b0["c_in"] + 160

        @block.gpsimd
        def _(pool):
            for n, (src, h, l) in enumerate(((wq, wqh, wql), (wu, wuh, wul))):
                pool.wait_ge(s["hi"].sem, b0["hi"] + n + 1)
                inc(nc.gpsimd.tensor_tensor(l[:, :, :], src[:, :, :], h[:, :, :].bitcast(F32), ALU.subtract), "lo")

        @block.tensor
        def _(pe):
            pe.wait_ge(s["c_in"].sem, C_IN)
            for a in range(KT):
                ins = nc.tensor.matmul(B[0][0:VB, 0:NSLOT], wvd[:, a, :], valsT[:, a, :], start=(a == 0), stop=(a == KT - 1))
            inc(ins, "pe_mm")
            inc(nc.tensor.matmul(B[1][0:BOT, 0:NSLOT], wr[:, :], keysT[:, :], start=True, stop=True), "pe_mm")
            pe.wait_ge(s["lo"].sem, b0["lo"] + 1)
            for b in range(BATCH):
                tok = slice(b * SEQ, (b + 1) * SEQ)
                for a in range(KT):
                    ins = matmul3(nc, B[2 + b][:, :], wqh[:, a, :], wql[:, a, :], k.xTh[:, a, tok], k.xTl[:, a, tok], a == 0, a == KT - 1)
                inc(ins, "pe_mm")
            pe.wait_ge(s["lo"].sem, b0["lo"] + 2)
            for b in range(BATCH):
                tok = slice(b * SEQ, (b + 1) * SEQ)
                for a in range(KT):
                    ins = matmul3(nc, B[4 + b][:, :], wuh[:, a, :], wul[:, a, :], k.xTh[:, a, tok], k.xTl[:, a, tok], a == 0, a == KT - 1)
                inc(ins, "pe_mm")
            pe.wait_ge(s["mid"].sem, b0["mid"] + 1)
            inc(nc.tensor.matmul(B[6][:, :], vw[:, :], wvu[:, :], start=True, stop=True), "pe_mm")
            for b in range(BATCH):
                pe.wait_ge(s["q_out"].sem, b0["q_out"] + b + 1)
                inc(nc.tensor.matmul(B[2 + b][0:BOT, :], wr[:, :], qA[0:BOT, b * SEQ:(b + 1) * SEQ], start=True, stop=True), "pe_mm")
            pe.wait_ge(s["gelu"].sem, b0["gelu"] + 2)
            pe.wait_ge(s["mid"].sem, b0["mid"] + 3)
            for t in range(TT):
                ins = nc.tensor.matmul(B[7][:, t:t + 1], gl[:, t * P:(t + 1) * P], wu2[:, :], start=True, stop=True)
            pe.wait_ge(s["ones"].sem, b0["ones"] + 1)
            pe.wait_ge(s["ln"].sem, b0["ln"] + 1)
            inc(nc.tensor.matmul(B[7][:, 16:16 + TT], ones[:, :], lv[:, :], start=True, stop=True), "lrn")
            pe.wait_ge(s["mid"].sem, b0["mid"] + 5)

            def slot_scores(t):
                if t >= 2:
                    pe.wait_ge(s["masked"].sem, b0["masked"] + t - 1)
                tok = slice(t * P, (t + 1) * P)
                nc.tensor.matmul(B[t % 2][:, 0:NSLOT], rqA[:, tok], rkT[:, :], start=True, stop=True)
                inc(nc.tensor.matmul(B[t % 2][:, NSLOT:2 * NSLOT], qA[:, tok], keysA[:, :], start=True, stop=True), "s_mm")

            slot_scores(0)
            for t in range(TT):
                if t + 1 < TT:
                    slot_scores(t + 1)
                pe.wait_ge(s["exp"].sem, b0["exp"] + t + 1)
                if t >= 2:
                    pe.wait_ge(s["wt_cp"].sem, b0["wt_cp"] + t - 1)
                inc(nc.tensor.transpose(B[2 + t % 2][:, 0:P], wts[:, t % 2, :], k.ident[:, :]), "wt_mm")
                pe.wait_ge(s["wt_cp"].sem, b0["wt_cp"] + t + 1)
                if t >= 2:
                    pe.wait_ge(s["y_add"].sem, b0["y_add"] + t - 1)
                inc(nc.tensor.matmul(B[4 + t % 2][:, :], wT[:, t % 2, :], mix[:, :], start=True, stop=True), "y_mm")

        @block.scalar
        def _(act):
            act.wait_ge(s["w_in"].sem, b0["w_in"] + 32)
            for src, h in ((wq, wqh), (wu, wuh)):
                inc(nc.scalar.activation(h[:, :, :], src[:, :, :], ACT.Copy), "hi")
            act.wait_ge(s["c_in"].sem, C_IN)
            for b in range(BATCH):
                act.wait_ge(s["pe_mm"].sem, b0["pe_mm"] + 5 + b)
                inc(nc.scalar.activation(gl[:, b * SEQ:(b + 1) * SEQ], B[4 + b][:, :], ACT.Gelu_apprx_tanh, bias=bu1[:, :]), "gelu")
            inc(nc.scalar.activation(lv[:, :], k.xvar[:, :], ACT.Ln, bias=1.0), "ln")
            act.wait_ge(s["chain"].sem, b0["chain"] + 1)
            inc(nc.scalar.activation(sg[:, :], B[7][:, 0:TT], ACT.Sigmoid, bias=scal[:, 0:1]), "sig")
            act.wait_ge(s["chain"].sem, b0["chain"] + 8)
            inc(nc.scalar.activation(gate[:, :], u[:, :], ACT.Sigmoid, bias=scal[:, 2:3], scale=scal[:, 1:2]), "sig2")
            for t in range(TT):
                act.wait_ge(s["masked"].sem, b0["masked"] + t + 1)
                if t >= 2:
                    act.wait_ge(s["wt_mm"].sem, b0["wt_mm"] + t - 1)
                inc(nc.scalar.activation(wts[:, t % 2, :], att[:, t % 2, :], ACT.Exp, bias=negmax[:, t:t + 1],
                                         accum_out=rowsum[:, t:t + 1]), "exp")
                act.wait_ge(s["wt_mm"].sem, b0["wt_mm"] + t + 1)
                if t >= 2:
                    act.wait_ge(s["y_mm"].sem, b0["y_mm"] + t - 1)
                inc(nc.scalar.activation(wT[:, t % 2, :], B[2 + t % 2][:, 0:P], ACT.Copy), "wt_cp")

        @block.vector
        def _(dve):
            steps = [0]

            def link(ins):
                steps[0] += 1
                inc(ins, "chain")
                dve.wait_ge(s["chain"].sem, b0["chain"] + steps[0])

            nc.vector.memset(qA[BOT:BOT + 1, :], 1.0)
            nc.vector.memset(rqA[BOT:BOT + 1, :], 1.0)
            inc(nc.vector.memset(ones[:, :], 1.0), "ones")
            dve.wait_ge(s["c_in"].sem, C_IN)
            dve.wait_ge(s["pe_mm"].sem, b0["pe_mm"] + 1)
            inc(nc.vector.tensor_copy(vw[:, :], B[0][0:VB, 0:NSLOT]), "mid")
            dve.wait_ge(s["pe_mm"].sem, b0["pe_mm"] + 2)
            inc(nc.vector.tensor_scalar(rkT[0:BOT, :], B[1][0:BOT, 0:NSLOT], float(1.0 / np.sqrt(RDIM)), None, ALU.mult), "mid")
            inc(nc.vector.tensor_scalar(keysA[0:BOT, :], keysT[:, :], float(1.0 / np.sqrt(BOT)), None, ALU.mult), "mid")
            for b in range(BATCH):
                dve.wait_ge(s["pe_mm"].sem, b0["pe_mm"] + 3 + b)
                inc(nc.vector.tensor_copy(qA[0:BOT, b * SEQ:(b + 1) * SEQ], B[2 + b][0:BOT, :]), "q_out")
            dve.wait_ge(s["pe_mm"].sem, b0["pe_mm"] + 7)
            nc.vector.tensor_copy(mix[:, :], B[6][:, :])
            for b in range(BATCH):
                dve.wait_ge(s["pe_mm"].sem, b0["pe_mm"] + 8 + b)
                inc(nc.vector.tensor_copy(rqA[0:BOT, b * SEQ:(b + 1) * SEQ], B[2 + b][0:BOT, :]), "mid")
            dve.wait_ge(s["lrn"].sem, b0["lrn"] + 1)
            link(nc.vector.tensor_reduce(lsum[:, :], B[7][:, 16:16 + TT], AX, ALU.add))
            link(nc.vector.tensor_scalar(lsum[:, :], lsum[:, :], 1.0 / TOK, 1e-6, ALU.mult, ALU.add))
            link(nc.vector.reciprocal(rl[:, :], lsum[:, :]))
            dve.wait_ge(s["sig"].sem, b0["sig"] + 1)
            dve.wait_ge(s["ln"].sem, b0["ln"] + 1)
            nc.vector.tensor_scalar(u[:, :], lv[:, :], rl[:, 0:1], 0.5, ALU.mult, ALU.mult)
            link(nc.vector.tensor_scalar(ge[:, :], sg[:, :], 2.5, None, ALU.mult))
            link(nc.vector.tensor_tensor(u[:, :], u[:, :], ge[:, :], ALU.add))
            link(nc.vector.tensor_scalar(u[:, :], u[:, :], 0.0, 5.0, ALU.max, ALU.min))
            TAU_LOW, TAU_HIGH = 0.5, 2.0
            link(nc.vector.tensor_scalar(fac[:, :], u[:, :], -TAU_LOW, 1.0 / (TAU_HIGH - TAU_LOW), ALU.add, ALU.mult))
            link(nc.vector.tensor_scalar(u[:, :], fac[:, :], 0.0, 1.0, ALU.max, ALU.min))
            dve.wait_ge(s["sig2"].sem, b0["sig2"] + 1)
            link(nc.vector.tensor_scalar(ge[:, :], gate[:, :], 0.05, None, ALU.is_ge))
            link(nc.vector.tensor_tensor(gate[:, :], gate[:, :], ge[:, :], ALU.mult))

            def choose(t):
                dve.wait_ge(s["s_mm"].sem, b0["s_mm"] + t + 1)
                sc = B[t % 2][:, 0:NSLOT]
                link(nc.vector.max(top[:, t, :], sc))
                link(nc.vector.match_replace(rep[:, t % 2, :], top[:, t, :], sc, -3e38))
                link(nc.vector.tensor_tensor(rep[:, t % 2, :], rep[:, t % 2, :], sc, ALU.is_equal))
                if t >= 2:
                    dve.wait_ge(s["exp"].sem, b0["exp"] + t - 1)
                link(nc.vector.scalar_tensor_tensor(out=att[:, t % 2, :], in0=rep[:, t % 2, :], scalar=MASKED,
                                                    in1=B[t % 2][:, NSLOT:2 * NSLOT], op0=ALU.mult, op1=ALU.add))
                inc(nc.vector.tensor_reduce(negmax[:, t:t + 1], att[:, t % 2, :], AX, ALU.max, negate=True), "masked")

            def add(t):
                dve.wait_ge(s["exp"].sem, b0["exp"] + t + 1)
                link(nc.vector.reciprocal(rinv[:, t:t + 1], rowsum[:, t:t + 1]))
                link(nc.vector.tensor_tensor(fac[:, t:t + 1], rinv[:, t:t + 1], gate[:, t:t + 1], ALU.mult))
                dve.wait_ge(s["y_mm"].sem, b0["y_mm"] + t + 1)
                inc(nc.vector.scalar_tensor_tensor(out=k.x[:, t, :], in0=B[4 + t % 2][:, :], scalar=fac[:, t:t + 1],
                                                   in1=k.x[:, t, :], op0=ALU.mult, op1=ALU.add), "y_add")

            choose(0)
            for t in range(TT):
                if t + 1 < TT:
                    choose(t + 1)
                add(t)

        for n in names:
            s[n].base += counts[n]


def rotary(inv, dim, length):
    freqs = np.arange(length, dtype=np.float32)[:, None] * inv.astype(np.float32)[None, :]
    emb = np.concatenate([freqs, freqs], axis=-1)
    return np.cos(emb).T.astype(np.float32), np.sin(emb).T.astype(np.float32)


def llama_inv_freq(theta, factor, high, low, ctx, dim):
    inv = 1.0 / theta ** (np.arange(0, dim, 2, dtype=np.float64) / dim)
    wavelen = 2.0 * np.pi / inv
    smooth = (ctx / wavelen - low) / (high - low)
    scaled = np.where(wavelen > ctx / low, inv / factor, inv)
    mid = (wavelen <= ctx / low) & (wavelen >= ctx / high)
    return np.where(mid, (1 - smooth) * inv / factor + smooth * inv, scaled).astype(np.float32)


def wide_tables(inv, key_scale):
    cos, sin = rotary(inv, HD, SEQ)
    sign = np.where(np.arange(HD) < HD // 2, 1.0, -1.0).astype(np.float32)[:, None]
    ks = (key_scale / np.sqrt(np.float32(HD))).astype(np.float32)[None, :]
    return np.ascontiguousarray(np.stack([cos, sin * sign, cos * ks, sin * sign * ks], axis=1).astype(np.float32))


def constant_arrays():
    pos = np.arange(SEQ)
    key_scale = np.where(pos < SYS_LEN, SUP, np.where(pos < SYS_LEN + IMG_LEN, ENH, 1.0)).astype(np.float32)
    inv1 = 1.0 / np.float32(10000.0) ** (np.arange(0, HD, 2, dtype=np.float32) / np.float32(HD))
    back = 1.0 / key_scale[:P]
    t0s = np.where(np.arange(P)[:, None] >= SYS_LEN + IMG_LEN, 1.0, back[None, :]).astype(np.float32)
    mask = np.where(np.arange(P)[None, :] > np.arange(P)[:, None], MASKED, 0.0).astype(np.float32)
    consts = np.stack([np.eye(P, dtype=np.float32), mask], axis=1)
    a = {
        "consts": consts,
        "L1_tables": wide_tables(inv1, key_scale),
        "L1_t0s": t0s,
        "tri_g": np.tril(np.ones((MGROUPS, MGROUPS), np.float32), -1),
        "tri_e": np.tril(np.ones((EXPERTS, EXPERTS), np.float32), -1),
        "L3_tables": wide_tables(llama_inv_freq(500000.0, 8.0, 4.0, 1.0, 1024, HD), np.ones(SEQ, np.float32)),
    }
    a["L0_kcol"] = (np.arange(P) // 16 + 2).astype(np.float32).reshape(P, 1)
    dh = 16
    inv2 = 1.0 / np.float32(500000.0) ** (np.arange(0, dh, 2, dtype=np.float32) / np.float32(dh))
    inv2 = np.where(2.0 * np.pi / inv2 > 1024.0, inv2 / np.float32(32.0), inv2).astype(np.float32)
    cos, sin = (m.T for m in rotary(inv2, dh, SEQ))
    sin = sin * np.where(np.arange(dh) < dh // 2, -1.0, 1.0).astype(np.float32)
    sc = np.float32(1.0 / np.sqrt(dh))
    tab = np.stack([cos * sc, sin * sc, cos, sin], axis=1).astype(np.float32)
    a["L2_tab"] = tab.reshape(QT, P, 4, dh).transpose(1, 0, 2, 3)
    return a


def by_feature(w):
    return w.reshape(KT, P, -1).transpose(1, 0, 2)


def input_arrays(i):
    a = {"x": i["L0_attn_x"].reshape(TOK, D)}

    def heads(w):
        return w.reshape(KT, P, -1, HD).transpose(2, 1, 0, 3)

    for name, t in (("L1_", True), ("L3_", False)):
        w = {n: (i[f"{name}attn_w{n}"].T if t else i[f"{name}attn_w{n}"]) for n in "qkvo"}
        for n in "qkv":
            a[f"{name}w{n}"] = heads(w[n])
        a[f"{name}wo"] = w["o"].reshape(HEADS, HD, D)

    def slabs(routed, shared):
        return np.concatenate([routed, shared])

    f = {n: i["L1_ffn_" + n] for n in ("router_w", "router_b", "router_bias", "ew1", "eb1", "ew2", "eb2", "ew3", "eb3",
                                       "sw1", "sb1", "sw2", "sb2", "sw3", "sb3")}
    a["router_w"] = by_feature(f["router_w"])
    a["router_rows"] = np.stack([f["router_b"], f["router_bias"]])
    for n in "12":
        w = slabs(f["ew" + n], f["sw" + n].reshape(D, 2, INTER).transpose(1, 0, 2))
        a["ew" + n] = w.reshape(SLABS, KT, P, INTER).transpose(0, 2, 1, 3)
    a["ew3"] = slabs(f["ew3"], f["sw3"].reshape(2, INTER, D))
    a["eb12"] = np.stack([slabs(f["eb" + n], f["sb" + n].reshape(2, INTER)) for n in "12"], axis=2)
    a["b3"] = np.concatenate([f["eb3"], f["sb3"].reshape(1, D)])

    def padded(w, rows, cols):
        out = np.zeros((rows, cols), w.dtype)
        out[:w.shape[0], :w.shape[1]] = w
        return out

    g = lambda n: i["L0_attn_" + n]
    a["L0_wqkv"] = by_feature(np.concatenate([g("Wqk_w"), g("Wv_w")]).T)
    a["L0_qkvb"] = np.concatenate([g("Wqk_b"), g("Wv_b")])
    a["L0_wo"] = g("Wo_w").T
    a["L0_wf"] = by_feature(i["L0_ffn_weight"].T)
    a["L0_la"] = by_feature(padded(i["L0_ffn_lora_A"].reshape(-1, D).T, D, P))
    lb = i["L0_ffn_lora_B"].transpose(0, 2, 1).reshape(-1, D)
    a["L0_lb"] = np.concatenate([lb, np.zeros((64 - lb.shape[0], D), lb.dtype), i["L0_ffn_bias"].reshape(1, D), g("Wo_b").reshape(1, D)])
    a["L0_starts"] = i["L0_ffn_lora_start_indices"]
    g = lambda n: i["L2_attn_" + n]
    a["L2_wqkv"] = by_feature(np.concatenate([g("Wq"), g("Wk"), g("Wv")]).T)
    a["L2_wo"] = by_feature(g("Wo").T)
    for name in ("L2_", "L3_"):
        g = lambda n: i[name + "ffn_" + n]
        a[name + "m_wq"] = by_feature(padded(g("Wq").T, D, P))
        a[name + "m_wu1"] = by_feature(g("Wu1").T)
        a[name + "m_wr"] = padded(g("Wr").T, BOT, BOT)
        a[name + "m_keysT"] = g("aux_keys").T
        a[name + "m_valsT"] = by_feature(g("aux_values").T)
        a[name + "m_wvd"] = by_feature(g("Wvd").T)
        a[name + "m_wvu"] = g("Wvu").T
        a[name + "m_bu1"] = g("bu1").reshape(P, 1)
        a[name + "m_wu2"] = g("Wu2").reshape(P, 1)
        a[name + "m_log_rel"] = g("log_rel").reshape(1, NSLOT)
        a[name + "m_scal"] = np.concatenate([g("bu2").reshape(1), g("gate_w1").reshape(1), g("gate_bias").reshape(1)])
    return a


def store(k, out):
    nc = k.nc
    with ExitStack() as st:
        y_out = k.sem("y_out")
        block = st.enter_context(nc.Block())

        @block.sync
        def _(sp):
            sp.dma_start(out.rearrange("(t p) n -> p t n", p=P), k.x[:, :, :]).then_inc(y_out.sem, 16)
            sp.wait_ge(y_out.sem, 16)


def program(nc, d, out):
    with ExitStack() as ctx:
        k = make_shared(nc, ctx)
        load_constants(k, d)
        layer_norm(k, 0, False)
        narrow_layer0(k, d)
        layer_norm(k, 1, False)
        wide_attention(k, d, "L1_", True)
        experts(k, d)
        layer_norm(k, 2, True)
        narrow_attention2(k, d)
        memory_ffn(k, d, "L2_")
        layer_norm(k, 3, True)
        wide_attention(k, d, "L3_", False)
        memory_ffn(k, d, "L3_")
        store(k, out)


def kernel(**inputs):
    import concourse.bacc as bacc
    from concourse.bass_utils import run_bass_kernel_spmd as run

    arrays = {n: np.ascontiguousarray(a) for n, a in {**input_arrays(inputs), **constant_arrays()}.items()}
    nc = bacc.Bacc("TRN2", target_bir_lowering=False, num_devices=1)
    d = {n: nc.dram_tensor("in_" + n, a.shape, mybir.dt.from_np(a.dtype), kind="ExternalInput").ap() for n, a in arrays.items()}
    out = nc.dram_tensor("out_y", (TOK, D), F32, kind="ExternalOutput").ap()
    program(nc, d, out)
    r = run(nc, [{"in_" + n: a for n, a in arrays.items()}], core_ids=[0])
    return r.results[0]["out_y"].reshape(BATCH, SEQ, D)
```

```python
from contextlib import ExitStack

import numpy as np
import concourse.bass as bass
from concourse import mybir

F32 = mybir.dt.float32
F32R = mybir.dt.float32r
BF16 = mybir.dt.bfloat16
I32 = mybir.dt.int32
ACT = mybir.ActivationFunctionType
ALU = mybir.AluOpType
AX = mybir.AxisListType.X

P = 128
D = 512
KT = D // P
BATCH, SEQ = 2, 512
QT = SEQ // P
TT = BATCH * QT
TOK = BATCH * SEQ
EPS = 1e-5
MASKED = -1e30

HD, HEADS, GROUPS = 128, 32, 8
HPG = HEADS // GROUPS
SYS_LEN, IMG_LEN, SUP, ENH = 35, 72, 0.5, 1.5

EXPERTS, INTER, MGROUPS = 16, 128, 4
SLABS = EXPERTS + 2

BOT, RDIM, NSLOT, TOPK, VB = 64, 48, 128, 8, 32


class Count:

    def __init__(self, sem):
        self.sem, self.base, self.per = sem, 0, 0

    def start(self, per):
        first = self.per == 0
        assert first or self.per == per
        self.per = per
        return first


class Shared:
    pass


def make_shared(nc, ctx):
    k = Shared()
    k.nc = nc

    def sb(name, shape, dt=F32, stack=ctx):
        return stack.enter_context(nc.sbuf_tensor(name, shape, dt))

    k.sb = sb
    k.sems = {}

    def sem(name):
        if name not in k.sems:
            k.sems[name] = Count(ctx.enter_context(nc.semaphore(name)))
        return k.sems[name]

    k.sem = sem
    k.ctx = ctx
    k.x = sb("x", [P, TT, D])
    k.xTh = sb("xTh", [P, KT, TOK], F32R)
    k.xTl = sb("xTl", [P, KT, TOK], F32R)
    k.ident = sb("ident", [P, P])
    k.identb = sb("identb", [P, P], BF16)
    k.maskb = sb("maskb", [P, P], BF16)
    k.xvar = sb("xvar", [P, TT])
    k.bank = [ctx.enter_context(nc.psum_tensor(f"bank{n}", [P, 512], F32)) for n in range(8)]
    return k


def matmul3(nc, out, ah, al, bh, bl, first, last):
    nc.tensor.matmul(out, ah, bh, start=first, stop=False)
    nc.tensor.matmul(out, ah, bl, start=False, stop=False)
    return nc.tensor.matmul(out, al, bh, start=False, stop=last)


def load_constants(k, d):
    nc = k.nc
    with ExitStack() as st:
        cst = k.sb("cst", [P, 2, P], F32, st)
        c_in, c_cast = k.sem("c_in"), k.sem("c_cast")

        def load_x(eng, n):
            eng.dma_start(k.x[:, 2 * n:2 * n + 2, :],
                          d["x"][2 * n * P:(2 * n + 2) * P, :].rearrange("(t p) n -> p t n", p=P)).then_inc(k.sem(f"x_in{n}").sem, 16)

        block = st.enter_context(nc.Block())

        @block.sync
        def _(sp):
            sp.dma_start(cst[:, :, :], d["consts"]).then_inc(c_in.sem, 16)
            for n in (0, 2):
                load_x(sp, n)

        @block.scalar
        def _(act):
            for n in (1, 3):
                load_x(act, n)

        @block.vector
        def _(dve):
            dve.wait_ge(c_in.sem, 16)
            nc.vector.tensor_copy(k.ident[:, :], cst[:, 0, :])
            nc.vector.tensor_copy(k.identb[:, :], cst[:, 0, :])
            nc.vector.tensor_copy(k.maskb[:, :], cst[:, 1, :]).then_inc(c_cast.sem, 1)


def layer_norm(k, n, add_normed, load_ahead=None):
    nc = k.nc
    with ExitStack() as st:
        xn = k.sb(f"xn{n}", [P, TT, D], F32, st)
        stats = k.sb(f"stats{n}", [P, TT, 6], F32, st)
        mv = k.sb(f"mv{n}", [P, TT, 2], F32, st)
        stats2 = k.sb(f"stats2{n}", [P, TT, 6], F32, st)
        mv2 = k.sb(f"mv2{n}", [P, TT, 2], F32, st)
        veps = k.sb(f"veps{n}", [P, TT], F32, st)
        sd = k.sb(f"sd{n}", [P, TT], F32, st)
        rstd = k.sb(f"rstd{n}", [P, TT], F32, st)
        chain, sq, normed, turned, hi, lo = (k.sem("ln_" + s) for s in "chain sqrt normed turned hi lo".split())
        c0, s0, n0, t0, h0, l0 = (s.base for s in (chain, sq, normed, turned, hi, lo))
        banks = k.bank[0:4]
        block = st.enter_context(nc.Block())
        steps = [0]

        @block.sync
        def _(sp):
            if load_ahead:
                load_ahead(sp)

        @block.vector
        def _(dve):
            def link(ins):
                steps[0] += 1
                ins.then_inc(chain.sem, 1)
                dve.wait_ge(chain.sem, c0 + steps[0])

            for t in range(TT):
                if n == 0 and t % 2 == 0:
                    dve.wait_ge(k.sem(f"x_in{t // 2}").sem, 16)
                ins = nc.vector.bn_stats(stats[:, t, :], k.x[:, t, :])
            link(ins)
            for t in range(TT):
                ins = nc.vector.bn_aggr(mv[:, t, :], stats[:, t, :])
            link(ins)
            nc.vector.tensor_scalar(veps[:, :], mv[:, :, 1], EPS, None, ALU.add).then_inc(chain.sem, 1)
            steps[0] += 1
            dve.wait_ge(sq.sem, s0 + 1)
            link(nc.vector.reciprocal(rstd[:, :], sd[:, :]))

            def low_part(t):
                dve.wait_ge(hi.sem, h0 + t + 1)
                nc.vector.tensor_tensor(
                    k.xTl[:, :, t * P:(t + 1) * P], banks[t % 4][:, :].rearrange("p (a q) -> p a q", a=KT),
                    k.xTh[:, :, t * P:(t + 1) * P].bitcast(F32), ALU.subtract).then_inc(lo.sem, 1)

            for t in range(TT):
                nc.vector.tensor_scalar(xn[:, t, :], k.x[:, t, :], mv[:, t, 0:1], rstd[:, t:t + 1],
                                        ALU.subtract, ALU.mult).then_inc(normed.sem, 1)
                if t >= 2:
                    low_part(t - 2)
            low_part(TT - 2)
            low_part(TT - 1)
            if add_normed:
                dve.wait_ge(normed.sem, n0 + TT)
                for t in range(TT):
                    ins = nc.vector.bn_stats(stats2[:, t, :], xn[:, t, :])
                link(ins)
                for t in range(TT):
                    ins = nc.vector.bn_aggr(mv2[:, t, :], stats2[:, t, :])
                link(ins)
                nc.vector.tensor_copy(k.xvar[:, :], mv2[:, :, 1])

        @block.scalar
        def _(act):
            act.wait_ge(chain.sem, c0 + 3)
            nc.scalar.activation(sd[:, :], veps[:, :], ACT.Sqrt).then_inc(sq.sem, 1)
            for t in range(TT):
                act.wait_ge(turned.sem, t0 + t + 1)
                nc.scalar.activation(k.xTh[:, :, t * P:(t + 1) * P],
                                     banks[t % 4][:, :].rearrange("p (a q) -> p a q", a=KT), ACT.Copy).then_inc(hi.sem, 1)

        @block.tensor
        def _(pe):
            for t in range(TT):
                pe.wait_ge(normed.sem, n0 + t + 1)
                if t >= 4:
                    pe.wait_ge(lo.sem, l0 + t - 3)
                for a in range(KT):
                    ins = nc.tensor.transpose(banks[t % 4][:, a * P:(a + 1) * P], xn[:, t, a * P:(a + 1) * P], k.ident[:, :])
                ins.then_inc(turned.sem, 1)

        @block.gpsimd
        def _(pool):
            if add_normed:
                for t in range(TT):
                    pool.wait_ge(normed.sem, n0 + t + 1)
                    nc.gpsimd.tensor_tensor(k.x[:, t, :], k.x[:, t, :], xn[:, t, :], ALU.add)

        chain.base += steps[0]
        sq.base += 1
        for s in (normed, turned, hi, lo):
            s.base += TT


def rotary_buffers(k, d, name, tile0_scale, stack):
    tables = k.sb(name + "tables", [P, 4, SEQ], F32, stack)
    t0s = k.sb(name + "t0s", [P, P], F32, stack) if tile0_scale else None
    tab = k.sem("wa_in_tab")

    def load(eng):
        eng.dma_start(tables[:, :, :], d[name + "tables"]).then_inc(tab.sem, 16)
        if tile0_scale:
            eng.dma_start(t0s[:, :], d[name + "t0s"]).then_inc(tab.sem, 16)

    return tables, t0s, load


def wide_attention(k, d, name, tables, t0s):
    nc = k.nc
    tile0_scale = t0s is not None
    UNITS = BATCH * HPG
    ACC, SM, TR = 22, 4 * UNITS, 4 * UNITS
    W_SEQ = ["wk", "wq0", "wq1", "wv", "wq2", "wq3", "wo0", "wo1", "wo2", "wo3"]
    w_at = {w: n for n, w in enumerate(W_SEQ)}
    beside = {-1: ["K0", "Q0", "V0", "K1", "U0"], 0: ["Q1", "Q2", "V1"], 1: ["U1", "Q3"], 2: ["Q4"], 3: ["Q5"], 4: ["Q6"],
              5: ["Q7"], 6: ["W1"], 7: ["W2"], 8: ["W3"]}
    acc_seq = [a for u in range(-1, 6) for a in beside[u]] + [f"W{t}" for t in range(TT)]
    assert len(acc_seq) == ACC
    acc_at = {a: n for n, a in enumerate(acc_seq)}
    row_off = [P * i * (i + 1) // 2 for i in range(QT + 1)]
    ORDER = [3, 2, 1, 0]

    with ExitStack() as st:
        def sb(nm, shape, dt=F32):
            return k.sb(name + nm, shape, dt, st)

        wq_st = sb("wq_st", [P, 2, KT, HD])
        wo_st = sb("wo_st", [P, 2, D])
        wk_st = sb("wk_st", [P, KT, HD])
        wv_st = sb("wv_st", [P, KT, HD])
        wqh, wql = sb("wqh", [P, HPG, KT, HD], F32R), sb("wql", [P, HPG, KT, HD], F32R)
        woh, wol = sb("woh", [P, HPG, D], F32R), sb("wol", [P, HPG, D], F32R)
        wkh, wkl = sb("wkh", [P, KT, HD], F32R), sb("wkl", [P, KT, HD], F32R)
        wvh, wvl = sb("wvh", [P, KT, HD], F32R), sb("wvl", [P, KT, HD], F32R)
        kh, kl = sb("kh", [P, BATCH, SEQ], F32R), sb("kl", [P, BATCH, SEQ], F32R)
        vT = sb("vT", [P, SEQ])
        vh, vl = sb("vh", [P, TT, HD], F32R), sb("vl", [P, TT, HD], F32R)
        rope_a, rope_b, rope_s = sb("rope_a", [P, SEQ]), sb("rope_b", [P, SEQ]), sb("rope_s", [P, SEQ])
        qh, ql = sb("qh", [P, 3, SEQ], F32R), sb("ql", [P, 3, SEQ], F32R)
        probs = sb("probs", [P, 2, row_off[QT]])
        pth, ptl = sb("pth", [P, 2, SEQ], F32R), sb("ptl", [P, 2, SEQ], F32R)
        oth, otl = sb("oth", [P, UNITS, SEQ], F32R), sb("otl", [P, UNITS, SEQ], F32R)
        negmax, rowsum, rinv = sb("negmax", [P, UNITS, QT]), sb("rowsum", [P, UNITS, QT]), sb("rinv", [P, UNITS, QT])

        acc, sbank, tbank, obank = k.bank[0:2], k.bank[2:5], k.bank[5:7], k.bank[7]

        pers = dict(acc_mm=ACC, s_mm=SM, t_mm=TR, pv_mm=TR,
                    acc_out=ACC, maxed=SM, rinv_ok=UNITS, norm_dve=UNITS, pt_lo=TR, o_lo=UNITS,
                    exp_ok=SM, pt_hi=TR, o_hi=UNITS, qk_hi=10, v_hi=2, w_hi=10,
                    qk_sum=10, qk_lo=10, norm_ok=3 * UNITS, w_lo=10)
        s = {n: k.sem("wa_" + n) for n in pers}
        due = {n: s[n].start(pers[n]) for n in pers}
        d_in = {n: k.sem("wa_in_" + n) for n in ("wq0", "wq1", "wo0", "wo1", "wk", "wv", "tab")}
        d_base = {n: d_in[n].base for n in d_in}
        swaps = k.sem("wa_tab_seen")
        base = {n: s[n].base for n in pers}

        def credit(eng, *names):
            for n in names:
                if due[n]:
                    eng.sem_inc(s[n].sem, pers[n])

        def waits(eng, g):
            def w(n, count):
                eng.wait_ge(s[n].sem, base[n] + pers[n] + g * pers[n] + count)
            return w

        block = st.enter_context(nc.Block())

        @block.sync
        def _(sp):
            with sp.Fori(0, GROUPS) as g:
                w = waits(sp, g)

                def load(buf, src, sem):
                    sp.dma_start(buf, src).then_inc(d_in[sem].sem, 16)

                def wq(h):
                    w("w_lo", w_at[f"wq{h - 2}"] + 1 if h >= 2 else w_at[f"wq{h + 2}"] + 1 - 10)
                    load(wq_st[:, h % 2, :, :], d[name + "wq"][bass.ds(g * HPG + h, 1)].rearrange("a p k n -> p (a k) n"), f"wq{h % 2}")

                def wo(h):
                    w("w_lo", w_at[f"wo{h - 2}"] + 1 if h >= 2 else w_at[f"wo{h + 2}"] + 1 - 10)
                    load(wo_st[:, h % 2, :], d[name + "wo"][bass.ds(g * HPG + h, 1)].rearrange("a p n -> p (a n)"), f"wo{h % 2}")

                w("w_lo", w_at["wk"] + 1 - 10)
                load(wk_st[:, :, :], d[name + "wk"][bass.ds(g, 1)].rearrange("a p k n -> p (a k) n"), "wk")
                wq(0)
                wq(1)
                w("w_lo", w_at["wv"] + 1 - 10)
                load(wv_st[:, :, :], d[name + "wv"][bass.ds(g, 1)].rearrange("a p k n -> p (a k) n"), "wv")
                wq(2)
                wq(3)
                for h in range(HPG):
                    wo(h)

        def weight_parts(wname):
            h = int(wname[2]) if len(wname) == 3 else 0
            if wname.startswith("wq"):
                return wq_st[:, h % 2, :, :], wqh[:, h, :, :], wql[:, h, :, :], f"wq{h % 2}", 2, h // 2 + 1
            if wname.startswith("wo"):
                return wo_st[:, h % 2, :], woh[:, h, :], wol[:, h, :], f"wo{h % 2}", 2, h // 2 + 1
            if wname == "wk":
                return wk_st[:, :, :], wkh[:, :, :], wkl[:, :, :], "wk", 1, 1
            return wv_st[:, :, :], wvh[:, :, :], wvl[:, :, :], "wv", 1, 1

        def qk_parts(a):
            n = int(a[1:])
            if a[0] == "K":
                return kh[:, n, :], kl[:, n, :]
            return qh[:, n % 3, :], ql[:, n % 3, :]

        qk_seq = [a for a in acc_seq if a[0] in "KQ"]
        qk_at = {a: n for n, a in enumerate(qk_seq)}

        @block.tensor
        def _(pe):
            credit(pe, "acc_mm", "s_mm", "t_mm", "pv_mm")
            with pe.Fori(0, GROUPS) as g:
                w = waits(pe, g)

                ALL, FIRST, SECOND = range(0, 4), range(0, 2), range(2, 4)

                def acc_bank(a, part=ALL):
                    if part[0] == 0:
                        w("acc_out", acc_at[a] - 1)
                    return acc[acc_at[a] % 2]

                def project_qk(a, wh, wl, b, wname, part=ALL):
                    bank = acc_bank(a, part)
                    w("w_lo", w_at[wname] + 1)
                    for t in part:
                        ins = matmul3(nc, bank[:, :], wh[:, t, :], wl[:, t, :], k.xTh[:, t, b * SEQ:(b + 1) * SEQ],
                                      k.xTl[:, t, b * SEQ:(b + 1) * SEQ], t == 0, t == KT - 1)
                    if part[-1] == KT - 1:
                        ins.then_inc(s["acc_mm"].sem, 1)

                def project_q(u, part=ALL):
                    h = u % HPG
                    project_qk(f"Q{u}", wqh[:, h, :, :], wql[:, h, :, :], u // HPG, f"wq{h}", part)

                def turn_values(half):
                    bank = acc_bank(f"U{half}")
                    w("acc_out", acc_at[f"V{half}"] + 1)
                    for t in range(QT):
                        ins = nc.tensor.transpose(bank[:, t * P:(t + 1) * P], vT[:, t * P:(t + 1) * P], k.ident[:, :])
                    ins.then_inc(s["acc_mm"].sem, 1)

                def scores(u, n):
                    i, m, b = ORDER[n], 4 * u + n, u // HPG
                    w("exp_ok", m - 2 if m >= 3 else 0)
                    w("qk_lo", qk_at[f"Q{u}"] + 1)
                    keys = (i + 1) * P
                    out = sbank[m % 3][:, 0:keys]
                    rows = slice(i * P, (i + 1) * P)
                    matmul3(nc, out, qh[:, u % 3, rows], ql[:, u % 3, rows], kh[:, b, 0:keys], kl[:, b, 0:keys], True, False)
                    nc.tensor.matmul(sbank[m % 3][:, i * P:keys], k.identb[:, :], k.maskb[:, :],
                                     start=False, stop=True).then_inc(s["s_mm"].sem, 1)

                def turn_probs(u, j):
                    n = 4 * u + j
                    w("pt_lo", n - 1)
                    if j == 0:
                        w("norm_ok", 3 * u + 3)
                        w("norm_dve", u + 1)
                    for i in range(j, QT):
                        ins = nc.tensor.transpose(tbank[n % 2][:, i * P:(i + 1) * P],
                                                  probs[:, u % 2, row_off[i] + j * P:row_off[i] + (j + 1) * P], k.ident[:, :])
                    ins.then_inc(s["t_mm"].sem, 1)

                def values(u, j):
                    n, vt = 4 * u + j, (u // HPG) * QT + j
                    if j == 0:
                        w("o_lo", u)
                        w("acc_out", acc_at[f"U{u // HPG}"] + 1)
                    w("pt_lo", n + 1)
                    cols = slice(j * P, SEQ)
                    matmul3(nc, obank[:, cols], vh[:, vt, :], vl[:, vt, :], pth[:, n % 2, cols], ptl[:, n % 2, cols],
                            j == 0, j == QT - 1).then_inc(s["pv_mm"].sem, 1)

                def project_out(t, part=ALL):
                    bank, b = acc_bank(f"W{t}", part), t // QT
                    rows = slice((t % QT) * P, (t % QT + 1) * P)
                    for h in part:
                        u = b * HPG + h
                        w("o_lo", u + 1)
                        w("w_lo", w_at[f"wo{h}"] + 1)
                        ins = matmul3(nc, bank[:, :], oth[:, u, rows], otl[:, u, rows], woh[:, h, :], wol[:, h, :],
                                      h == 0, h == HPG - 1)
                    if part[-1] == HPG - 1:
                        ins.then_inc(s["acc_mm"].sem, 1)

                def project(a, part=ALL):
                    n = int(a[1])
                    if a[0] == "K":
                        project_qk(a, wkh, wkl, n, "wk", part)
                    elif a[0] == "Q":
                        project_q(n, part)
                    elif a[0] == "V":
                        project_qk(a, wvh, wvl, n, "wv", part)
                    elif a[0] == "U":
                        turn_values(n)
                    else:
                        project_out(n, part)

                for a in beside[-1]:
                    project(a)
                for u in range(UNITS + 1):
                    if u < UNITS:
                        scores(u, 0)
                        scores(u, 1)
                        scores(u, 2)
                    for a in beside[u][:1] if u == 0 else beside[u][:-1]:
                        project(a)
                    if u >= 1:
                        turn_probs(u - 1, 0)
                        turn_probs(u - 1, 1)
                    if u >= 1:
                        project(beside[u][-1], FIRST)
                    if u < UNITS:
                        scores(u, 3)
                    if u == 0:
                        for a in beside[u][1:]:
                            project(a)
                    else:
                        values(u - 1, 0)
                        turn_probs(u - 1, 2)
                        values(u - 1, 1)
                        turn_probs(u - 1, 3)
                        project(beside[u][-1], SECOND)
                        values(u - 1, 2)
                        values(u - 1, 3)
                    if u == 5:
                        project_out(0)
                for t in range(QT, TT):
                    project_out(t)

        @block.vector
        def _(dve):
            credit(dve, "acc_out", "maxed", "rinv_ok", "norm_dve", "pt_lo", "o_lo")
            dve.wait_ge(d_in["tab"].sem, d_base["tab"] + (32 if tile0_scale else 16))
            with dve.Fori(0, GROUPS) as g:
                w = waits(dve, g)

                def rope(a):
                    bank, c = acc[acc_at[a] % 2], 2 if a[0] == "K" else 0
                    w("acc_mm", acc_at[a] + 1)
                    w("qk_sum", qk_at[a])
                    H = HD // 2
                    nc.vector.tensor_tensor(rope_a[:, :], bank[:, :], tables[:, c, :], ALU.mult)
                    nc.vector.tensor_tensor(rope_b[0:H, :], bank[H:HD, :], tables[H:HD, c + 1, :], ALU.mult)
                    nc.vector.tensor_tensor(rope_b[H:HD, :], bank[0:H, :], tables[0:H, c + 1, :],
                                            ALU.mult).then_inc(s["acc_out"].sem, 1)

                def v_turned(half):
                    w("acc_mm", acc_at[f"V{half}"] + 1)
                    nc.vector.tensor_copy(vT[:, :], acc[acc_at[f"V{half}"] % 2][:, :]).then_inc(s["acc_out"].sem, 1)

                def v_low(half):
                    bank = acc[acc_at[f"U{half}"] % 2]
                    w("v_hi", half + 1)
                    tiles = slice(half * QT, (half + 1) * QT)
                    nc.vector.tensor_tensor(vl[:, tiles, :], bank[:, :].rearrange("p (t n) -> p t n", t=QT),
                                            vh[:, tiles, :].bitcast(F32), ALU.subtract).then_inc(s["acc_out"].sem, 1)

                def row_max(u, n):
                    i, m = ORDER[n], 4 * u + n
                    w("s_mm", m + 1)
                    sc = sbank[m % 3][:, 0:(i + 1) * P]
                    if i == 0 and tile0_scale:
                        nc.vector.tensor_tensor(sc, sc, t0s[:, :], ALU.mult).then_inc(swaps.sem, 1)
                        dve.wait_ge(swaps.sem, swaps.base + g * UNITS + u + 1)
                    nc.vector.tensor_reduce(negmax[:, u, i:i + 1], sc, AX, ALU.max, negate=True).then_inc(s["maxed"].sem, 1)

                def probs_low(u, j):
                    n = 4 * u + j
                    w("pt_hi", n + 1)
                    cols = slice(j * P, SEQ)
                    nc.vector.tensor_tensor(ptl[:, n % 2, cols], tbank[n % 2][:, cols], pth[:, n % 2, cols].bitcast(F32),
                                            ALU.subtract).then_inc(s["pt_lo"].sem, 1)

                def out_low(u):
                    w("o_hi", u + 1)
                    nc.vector.tensor_tensor(otl[:, u, :], obank[:, :], oth[:, u, :].bitcast(F32),
                                            ALU.subtract).then_inc(s["o_lo"].sem, 1)

                def add_out(t):
                    w("acc_mm", acc_at[f"W{t}"] + 1)
                    nc.vector.tensor_tensor(k.x[:, t, :], acc[acc_at[f"W{t}"] % 2][:, :], k.x[:, t, :],
                                            ALU.add).then_inc(s["acc_out"].sem, 1)

                def projected(names):
                    for a in names:
                        if a[0] == "U":
                            v_low(int(a[1]))
                        elif a[0] == "V":
                            v_turned(int(a[1]))
                        elif a[0] == "W":
                            add_out(int(a[1]))
                        else:
                            rope(a)

                projected(beside[-1])
                for u in range(UNITS + 1):
                    if u < UNITS:
                        row_max(u, 0)
                        row_max(u, 1)
                        row_max(u, 2)
                    if u == 0:
                        projected(["Q1"])
                    if u >= 2:
                        out_low(u - 2)
                    if u >= 1:
                        probs_low(u - 1, 0)
                        probs_low(u - 1, 1)
                    if u < UNITS:
                        row_max(u, 3)
                    if u >= 1:
                        probs_low(u - 1, 2)
                    if u < UNITS:
                        w("exp_ok", 4 * u + 4)
                        nc.vector.reciprocal(rinv[:, u, :], rowsum[:, u, :]).then_inc(s["rinv_ok"].sem, 1)
                        i = ORDER[0]
                        longest = probs[:, u % 2, row_off[i]:row_off[i + 1]]
                        w("rinv_ok", u + 1)
                        nc.vector.tensor_scalar(longest, longest, rinv[:, u, i:i + 1], None, ALU.mult).then_inc(s["norm_dve"].sem, 1)
                    if u >= 1:
                        probs_low(u - 1, 3)
                    projected(a for a in beside[u] if a != "Q1")
                    if u == 5:
                        add_out(0)
                out_low(UNITS - 1)
                for t in range(QT, TT):
                    add_out(t)

        @block.scalar
        def _(act):
            credit(act, "exp_ok", "pt_hi", "o_hi", "qk_hi", "v_hi", "w_hi")
            with act.Fori(0, GROUPS) as g:
                w = waits(act, g)

                def weight_high(wname):
                    src, hi, _, sem, per, at = weight_parts(wname)
                    act.wait_ge(d_in[sem].sem, d_base[sem] + g * 16 * per + 16 * at)
                    if wname == "wk":
                        w("acc_mm", acc_at["K1"] + 1 - ACC)
                    elif wname == "wv":
                        w("acc_mm", acc_at["V1"] + 1 - ACC)
                    elif wname[1] == "q":
                        w("acc_mm", acc_at[f"Q{int(wname[2]) + HPG}"] + 1 - ACC)
                    else:
                        w("acc_mm", 0)
                    w("w_lo", w_at[wname] - 10 + 1)
                    nc.scalar.activation(hi, src, ACT.Copy).then_inc(s["w_hi"].sem, 1)

                def qk_high(a):
                    w("qk_sum", qk_at[a] + 1)
                    w("s_mm", 4 * (int(a[1:]) - 2) if a[0] == "Q" and int(a[1:]) >= 3 else 0)
                    nc.scalar.activation(qk_parts(a)[0], rope_s[:, :], ACT.Copy).then_inc(s["qk_hi"].sem, 1)

                def v_high(half):
                    w("acc_mm", acc_at[f"U{half}"] + 1)
                    w("pv_mm", 0)
                    tiles = slice(half * QT, (half + 1) * QT)
                    nc.scalar.activation(vh[:, tiles, :], acc[acc_at[f"U{half}"] % 2][:, :].rearrange("p (t n) -> p t n", t=QT),
                                         ACT.Copy).then_inc(s["v_hi"].sem, 1)

                def exps(u, n):
                    i, m = ORDER[n], 4 * u + n
                    w("maxed", m + 1)
                    if n == 0:
                        w("t_mm", 4 * (u - 1))
                        w("rinv_ok", u - 1)
                    nc.scalar.activation(probs[:, u % 2, row_off[i]:row_off[i + 1]], sbank[m % 3][:, 0:(i + 1) * P], ACT.Exp,
                                         bias=negmax[:, u, i:i + 1], accum_out=rowsum[:, u, i:i + 1]).then_inc(s["exp_ok"].sem, 1)

                def probs_high(u, j):
                    n = 4 * u + j
                    w("t_mm", n + 1)
                    w("pv_mm", n - 1)
                    cols = slice(j * P, SEQ)
                    nc.scalar.activation(pth[:, n % 2, cols], tbank[n % 2][:, cols], ACT.Copy).then_inc(s["pt_hi"].sem, 1)

                def out_high(u):
                    w("pv_mm", 4 * u + 4)
                    w("acc_mm", -QT if u < HPG else 0)
                    nc.scalar.activation(oth[:, u, :], obank[:, :], ACT.Copy).then_inc(s["o_hi"].sem, 1)

                for wname in W_SEQ[:5]:
                    weight_high(wname)

                for a in beside[-1]:
                    if a[0] == "U":
                        v_high(int(a[1]))
                    elif a in ("K0", "Q0"):
                        qk_high(a)
                for u in range(UNITS + 1):
                    for n in range(3):
                        if u < UNITS:
                            exps(u, n)
                        if u >= 1 and n < 2:
                            probs_high(u - 1, n)
                    for a in ["K1", "Q1"] if u == 0 else beside[u - 1]:
                        if a[0] == "Q" and a != "Q1" or u == 0:
                            qk_high(a)
                    for a in beside[u]:
                        if a[0] == "U":
                            v_high(int(a[1]))
                    if u < UNITS:
                        exps(u, 3)
                    if u == 0:
                        weight_high("wq3")
                    if u >= 1:
                        probs_high(u - 1, 2)
                        probs_high(u - 1, 3)
                        out_high(u - 1)
                    if u < HPG:
                        weight_high(f"wo{u}")

        @block.gpsimd
        def _(pool):
            credit(pool, "qk_sum", "qk_lo", "norm_ok", "w_lo")
            with pool.Fori(0, GROUPS) as g:
                w = waits(pool, g)

                def weight_low(wname):
                    src, hi, lo, _, _, _ = weight_parts(wname)
                    w("w_hi", w_at[wname] + 1)
                    nc.gpsimd.tensor_tensor(lo, src, hi.bitcast(F32), ALU.subtract).then_inc(s["w_lo"].sem, 1)

                def rope_sum(a):
                    n = qk_at[a]
                    w("acc_out", acc_at[a] + 1)
                    w("qk_lo", n)
                    nc.gpsimd.tensor_tensor(rope_s[:, :], rope_a[:, :], rope_b[:, :], ALU.add).then_inc(s["qk_sum"].sem, 1)

                def qk_low(a):
                    n = qk_at[a]
                    w("qk_hi", n + 1)
                    w("qk_sum", n + 1)
                    hi, lo = qk_parts(a)
                    nc.gpsimd.tensor_tensor(lo, rope_s[:, :], hi.bitcast(F32), ALU.subtract).then_inc(s["qk_lo"].sem, 1)

                def normalise(u, n):
                    i = ORDER[n]
                    w("rinv_ok", u + 1)
                    tile = probs[:, u % 2, row_off[i]:row_off[i + 1]]
                    nc.gpsimd.tensor_tensor(tile, tile, rinv[:, u, i:i + 1].broadcast_to([P, (i + 1) * P]), ALU.mult).then_inc(s["norm_ok"].sem, 1)

                for wname in W_SEQ[:5]:
                    weight_low(wname)

                def projected(names):
                    for a in names:
                        if a[0] in "KQ":
                            rope_sum(a)
                            qk_low(a)

                projected(beside[-1] + ["Q1"])
                for u in range(UNITS):
                    for n in range(1, QT):
                        normalise(u, n)
                    if u == 0:
                        weight_low("wq3")
                    projected(a for a in beside[u] if a != "Q1")
                    if u < HPG:
                        weight_low(f"wo{u}")

        for n in pers:
            s[n].base += pers[n] * GROUPS
        for n, loads in (("wq0", 2), ("wq1", 2), ("wo0", 2), ("wo1", 2), ("wk", 1), ("wv", 1)):
            d_in[n].base += 16 * loads * GROUPS
        d_in["tab"].base += 32 if tile0_scale else 16
        if tile0_scale:
            swaps.base += GROUPS * UNITS


def experts(k, d):
    nc = k.nc
    E, G, EG = EXPERTS, MGROUPS, EXPERTS // MGROUPS
    with ExitStack() as st:
        def sb(nm, shape, dt=F32):
            return k.sb("mo_" + nm, shape, dt, st)

        rw, rwh, rwl = sb("rw", [P, KT, P]), sb("rwh", [P, KT, P], F32R), sb("rwl", [P, KT, P], F32R)
        logT = sb("logT", [E, TOK])
        rows = sb("rows", [P, 2, E])
        tri_g, tri_e = sb("tri_g", [P, G, G]), sb("tri_e", [P, E, E])
        z = sb("z", [P, TT, E])
        sc = sb("sc", [P, TT, E])
        mx, sm, ri = sb("mx", [P, TT]), sb("sm", [P, TT]), sb("ri", [P, TT])
        gm = sb("gm", [P, TT, G])
        cg, cg2 = sb("cg", [P, TT * G, G]), sb("cg2", [P, TT * G, G])
        rg, keep, pen = sb("rg", [P, TT, G]), sb("keep", [P, TT, G]), sb("pen", [P, TT, G])
        ce, ce2 = sb("ce", [P, TT * E, E]), sb("ce2", [P, TT * E, E])
        re_ = sb("re", [P, TT, E])
        gates = sb("gates", [P, TT, SLABS])
        gates_e = sb("gates_e", [P, SLABS, TT])
        gate = sb("gate", [P, TT])
        gT = sb("gT", [E + 1, TT, P])
        b3 = sb("b3", [E + 1, D])
        w1s, w2s, w3s = sb("w1s", [P, KT, INTER]), sb("w2s", [P, KT, INTER]), sb("w3s", [P, D])
        w1h, w1l = sb("w1h", [P, KT, INTER], F32R), sb("w1l", [P, KT, INTER], F32R)
        w2h, w2l = sb("w2h", [P, KT, INTER], F32R), sb("w2l", [P, KT, INTER], F32R)
        w3h, w3l = sb("w3h", [P, D], F32R), sb("w3l", [P, D], F32R)
        b12s, b12 = sb("b12s", [P, 2]), sb("b12", [P, 2, 2])
        act1 = sb("act1", [P, 2, SEQ])
        hf = sb("hf", [P, 2, SEQ])
        hh, hl = sb("hh", [P, 2, SEQ], F32R), sb("hl", [P, 2, SEQ], F32R)

        chain, r_in, r_split, r_mm, r_cp, r_turned, r_exp, g_mm, g_cp, b_mm, b_add = (
            k.sem("mo_" + n) for n in "chain r_in r_split r_mm r_cp r_turned r_exp g_mm g_cp b_mm b_add".split())
        pers = dict(up_mm=4, out_mm=TT, silu=2, h=2, x_add=TT, gate=1, h_hi=2, h_lo=2, w_hi=3, w_lo=3, b_cp=1)
        s = {n: k.sem("mo_" + n) for n in pers}
        for n in pers:
            s[n].start(pers[n])
        w_in = {n: k.sem("mo_in_" + n) for n in ("w1", "w2", "w3")}
        up = k.bank[0:4]
        ob = k.bank[4:8]
        block = st.enter_context(nc.Block())

        def waits(eng, e):
            def w(n, count):
                eng.wait_ge(s[n].sem, pers[n] * (e + 1) + count)
            return w

        @block.sync
        def _(sp):
            sp.dma_start(rw[:, :, :], d["router_w"]).then_inc(r_in.sem, 16)
            sp.dma_start(rows[:, :, :], d["router_rows"].partition_broadcast(P)).then_inc(r_in.sem, 16)
            sp.dma_start(tri_g[:, :, :], d["tri_g"].partition_broadcast(P)).then_inc(r_in.sem, 16)
            sp.dma_start(tri_e[:, :, :], d["tri_e"].partition_broadcast(P)).then_inc(r_in.sem, 16)
            sp.dma_start(b3[:, :], d["b3"]).then_inc(r_in.sem, 16)
            with sp.Fori(0, SLABS) as e:
                w = waits(sp, e)
                w("w_lo", -2)
                w("b_cp", 0)
                sp.dma_start(w1s[:, :, :], d["ew1"][bass.ds(e, 1)].rearrange("a p k n -> p (a k) n")).then_inc(w_in["w1"].sem, 16)
                sp.dma_start(b12s[:, :], d["eb12"][bass.ds(e, 1)].rearrange("a p n -> p (a n)")).then_inc(w_in["w1"].sem, 16)
                w("w_lo", -1)
                sp.dma_start(w2s[:, :, :], d["ew2"][bass.ds(e, 1)].rearrange("a p k n -> p (a k) n")).then_inc(w_in["w2"].sem, 16)
                w("w_lo", 0)
                sp.dma_start(w3s[:, :], d["ew3"][bass.ds(e, 1)].rearrange("a p n -> p (a n)")).then_inc(w_in["w3"].sem, 16)

        @block.tensor
        def _(pe):
            pe.wait_ge(r_split.sem, 2)
            for b in range(BATCH):
                for a in range(KT):
                    ins = matmul3(nc, up[b][:, :], rwh[:, a, :], rwl[:, a, :], k.xTh[:, a, b * SEQ:(b + 1) * SEQ],
                                  k.xTl[:, a, b * SEQ:(b + 1) * SEQ], a == 0, a == KT - 1)
                ins.then_inc(r_mm.sem, 1)
            pe.wait_ge(r_cp.sem, 2)
            for t in range(TT):
                ins = nc.tensor.transpose(ob[0][:, t * E:(t + 1) * E], logT[:, t * P:(t + 1) * P], k.ident[0:E, 0:E])
            ins.then_inc(r_turned.sem, 1)
            pe.sem_inc(s["up_mm"].sem, 4)
            pe.sem_inc(s["out_mm"].sem, TT)
            with pe.Fori(0, SLABS) as e:
                w = waits(pe, e)
                for half in range(BATCH):
                    tok = slice(half * SEQ, (half + 1) * SEQ)
                    for n, (wh, wl) in enumerate(((w1h, w1l), (w2h, w2l))):
                        w("h", half - 1)
                        w("w_lo", n + 1)
                        for a in range(KT):
                            ins = matmul3(nc, up[2 * half + n][:, :], wh[:, a, :], wl[:, a, :], k.xTh[:, a, tok],
                                          k.xTl[:, a, tok], a == 0, a == KT - 1)
                        ins.then_inc(s["up_mm"].sem, 1)
                w("w_lo", 3)
                for t in range(TT):
                    w("h_lo", t // QT + 1)
                    w("x_add", t - 3)
                    tok = slice((t % QT) * P, (t % QT + 1) * P)
                    matmul3(nc, ob[t % 4][:, :], hh[:, t // QT, tok], hl[:, t // QT, tok], w3h[:, :], w3l[:, :],
                            True, True).then_inc(s["out_mm"].sem, 1)
            for t in range(TT):
                pe.wait_ge(g_cp.sem, t)
                if t == 0:
                    pe.wait_ge(s["h"].sem, 2 * (SLABS + 1))
                    pe.wait_ge(chain.sem, 1)
                nc.tensor.transpose(up[0][0:E + 1, 0:P], gates[:, t, 0:E + 1], k.ident[:, :]).then_inc(g_mm.sem, 1)
            pe.wait_ge(s["x_add"].sem, TT * (SLABS + 1))
            pe.wait_ge(g_cp.sem, TT)
            for t in range(TT):
                if t >= 4:
                    pe.wait_ge(b_add.sem, t - 3)
                nc.tensor.matmul(ob[t % 4][:, :], gT[:, t, :], b3[:, :], start=True, stop=True).then_inc(b_mm.sem, 1)

        steps = [0]

        @block.vector
        def _(dve):
            def link(ins):
                steps[0] += 1
                ins.then_inc(chain.sem, 1)
                dve.wait_ge(chain.sem, steps[0])

            def over(ap, n):
                return ap.unsqueeze(2).broadcast_to([P, ap.shape[1], n])

            flat = lambda t: t[:, :, :].rearrange("p a b -> p (a b)")
            for n in ("h", "x_add", "gate"):
                dve.sem_inc(s[n].sem, pers[n])
            dve.wait_ge(r_in.sem, 80)
            nc.vector.tensor_copy(rwh[:, :, :], rw[:, :, :]).then_inc(r_split.sem, 1)
            dve.wait_ge(r_split.sem, 1)
            nc.vector.tensor_tensor(rwl[:, :, :], rw[:, :, :], rwh[:, :, :].bitcast(F32), ALU.subtract).then_inc(r_split.sem, 1)
            dve.wait_ge(r_turned.sem, 1)
            link(nc.vector.tensor_tensor(z[:, :, :], ob[0][:, 0:TT * E].rearrange("p (t e) -> p t e", t=TT),
                                         rows[:, 0:1, :].broadcast_to([P, TT, E]), ALU.add))
            link(nc.vector.tensor_reduce(mx[:, :], z[:, :, :], AX, ALU.max))
            link(nc.vector.tensor_tensor(z[:, :, :], z[:, :, :], over(mx[:, :], E), ALU.subtract))
            dve.wait_ge(r_exp.sem, 1)
            link(nc.vector.tensor_reduce(sm[:, :], sc[:, :, :], AX, ALU.add))
            link(nc.vector.reciprocal(ri[:, :], sm[:, :]))
            link(nc.vector.tensor_tensor(sc[:, :, :], sc[:, :, :], over(ri[:, :], E), ALU.mult))
            link(nc.vector.tensor_tensor(sc[:, :, :], sc[:, :, :], rows[:, 1:2, :].broadcast_to([P, TT, E]), ALU.add))
            link(nc.vector.tensor_reduce(gm[:, :, :], sc[:, :, :].rearrange("p t (g n) -> p t g n", g=G), AX, ALU.max))

            def choose(vals, n, cmp, cmp2, tri, rank, chosen, limit):
                mine = vals[:, :, :].rearrange("p t n -> p (t n)").unsqueeze(2).broadcast_to([P, TT * n, n])
                for t in range(TT):
                    theirs = vals[:, t:t + 1, :].broadcast_to([P, n, n])
                    own = mine[:, t * n:(t + 1) * n, :]
                    nc.vector.tensor_tensor(cmp[:, t * n:(t + 1) * n, :], theirs, own, ALU.is_gt)
                    ins = nc.vector.tensor_tensor(cmp2[:, t * n:(t + 1) * n, :], theirs, own, ALU.is_equal)
                link(ins)
                for t in range(TT):
                    ins = nc.vector.tensor_tensor(cmp2[:, t * n:(t + 1) * n, :], cmp2[:, t * n:(t + 1) * n, :], tri[:, :, :], ALU.mult)
                link(ins)
                link(nc.vector.tensor_tensor(cmp[:, :, :], cmp[:, :, :], cmp2[:, :, :], ALU.add))
                link(nc.vector.tensor_reduce(rank[:, :, :].rearrange("p t n -> p (t n)"), cmp[:, :, :], AX, ALU.add))
                link(nc.vector.tensor_scalar(chosen[:, :, :], rank[:, :, :], float(limit), None, ALU.is_lt))

            choose(gm, G, cg, cg2, tri_g, rg, keep, 2)
            link(nc.vector.tensor_scalar(pen[:, :, :], keep[:, :, :], -MASKED, MASKED, ALU.mult, ALU.add))
            link(nc.vector.tensor_tensor(z[:, :, :].rearrange("p t (g n) -> p (t g) n", g=G),
                                         sc[:, :, :].rearrange("p t (g n) -> p (t g) n", g=G), over(flat(keep), EG), ALU.mult))
            link(nc.vector.tensor_tensor(z[:, :, :].rearrange("p t (g n) -> p (t g) n", g=G),
                                         z[:, :, :].rearrange("p t (g n) -> p (t g) n", g=G), over(flat(pen), EG), ALU.add))
            choose(z, E, ce, ce2, tri_e, re_, re_, 2)
            nc.vector.memset(gates[:, :, E:SLABS], 1.0)
            link(nc.vector.tensor_tensor(gates[:, :, 0:E], sc[:, :, :], re_[:, :, :], ALU.mult))
            link(nc.vector.tensor_copy(gates_e[:, :, :], gates[:, :, :].rearrange("p t e -> p e t")))

            with dve.Fori(0, SLABS) as e:
                w = waits(dve, e)
                w("x_add", 0)
                nc.vector.tensor_copy(gate[:, :], gates_e[:, bass.ds(e, 1), :].rearrange("p a t -> p (a t)")).then_inc(s["gate"].sem, 1)
                for half in range(BATCH):
                    w("silu", half + 1)
                    w("up_mm", 2 * half + 2)
                    w("h_lo", half - 1)
                    nc.vector.scalar_tensor_tensor(out=hf[:, half, :], in0=up[2 * half + 1][:, :], scalar=b12[:, 1, 0:1],
                                                   in1=act1[:, half, :], op0=ALU.add, op1=ALU.mult).then_inc(s["h"].sem, 1)
                w("gate", 1)
                for t in range(TT):
                    w("out_mm", t + 1)
                    nc.vector.scalar_tensor_tensor(out=k.x[:, t, :], in0=ob[t % 4][:, :], scalar=gate[:, t:t + 1],
                                                   in1=k.x[:, t, :], op0=ALU.mult, op1=ALU.add).then_inc(s["x_add"].sem, 1)
            for t in range(TT):
                dve.wait_ge(g_mm.sem, t + 1)
                nc.vector.tensor_copy(gT[:, t, :], up[0][0:E + 1, 0:P]).then_inc(g_cp.sem, 1)
            for t in range(TT):
                dve.wait_ge(b_mm.sem, t + 1)
                nc.vector.tensor_tensor(k.x[:, t, :], ob[t % 4][:, :], k.x[:, t, :], ALU.add).then_inc(b_add.sem, 1)

        @block.scalar
        def _(act):
            for b in range(BATCH):
                act.wait_ge(r_mm.sem, b + 1)
                nc.scalar.activation(logT[:, b * SEQ:(b + 1) * SEQ], up[b][0:E, :], ACT.Copy).then_inc(r_cp.sem, 1)
            act.wait_ge(chain.sem, 3)
            nc.scalar.activation(sc[:, :, :], z[:, :, :], ACT.Exp).then_inc(r_exp.sem, 1)
            for n in ("silu", "h_hi", "w_hi", "b_cp"):
                act.sem_inc(s[n].sem, pers[n])
            with act.Fori(0, SLABS) as e:
                w = waits(act, e)

                def weight_high(n, src, hi):
                    act.wait_ge(w_in[f"w{n + 1}"].sem, (32 if n == 0 else 16) * (e + 1))
                    w("up_mm", (-1, 0)[n]) if n < 2 else w("out_mm", 0)
                    w("w_lo", n + 1 - 3)
                    nc.scalar.activation(hi, src, ACT.Copy).then_inc(s["w_hi"].sem, 1)

                weight_high(0, w1s[:, :, :], w1h[:, :, :])
                w("h", 0)
                nc.scalar.activation(b12[:, :, 0], b12s[:, :], ACT.Copy).then_inc(s["b_cp"].sem, 1)
                weight_high(1, w2s[:, :, :], w2h[:, :, :])
                w("b_cp", 1)
                for half in range(BATCH):
                    w("up_mm", 2 * half + 1)
                    w("h", half - 1)
                    nc.scalar.activation(act1[:, half, :], up[2 * half][:, :], ACT.Silu, bias=b12[:, 0, 0:1]).then_inc(s["silu"].sem, 1)
                    if half == 0:
                        weight_high(2, w3s[:, :], w3h[:, :])
                for half in range(BATCH):
                    w("h", half + 1)
                    w("out_mm", -4 if half == 0 else 0)
                    nc.scalar.activation(hh[:, half, :], hf[:, half, :], ACT.Copy).then_inc(s["h_hi"].sem, 1)

        @block.gpsimd
        def _(pool):
            for n in ("h_lo", "w_lo"):
                pool.sem_inc(s[n].sem, pers[n])
            with pool.Fori(0, SLABS) as e:
                w = waits(pool, e)

                def weight_low(n, src, hi, lo):
                    w("w_hi", n + 1)
                    nc.gpsimd.tensor_tensor(lo, src, hi.bitcast(F32), ALU.subtract).then_inc(s["w_lo"].sem, 1)

                weight_low(0, w1s[:, :, :], w1h[:, :, :], w1l[:, :, :])
                weight_low(1, w2s[:, :, :], w2h[:, :, :], w2l[:, :, :])
                weight_low(2, w3s[:, :], w3h[:, :], w3l[:, :])
                for half in range(BATCH):
                    w("h_hi", half + 1)
                    nc.gpsimd.tensor_tensor(hl[:, half, :], hf[:, half, :], hh[:, half, :].bitcast(F32), ALU.subtract).then_inc(s["h_lo"].sem, 1)


SLOTS = 6
Q_H, Q_M, Q_L = slice(0, 3), slice(3, 6, 2), slice(4, 5)
K_H, K_M, K_L = slice(2, 5), slice(1, 6, 4), slice(0, 1)


def by_slot(stack, slots, dh):
    return stack.rearrange("p h (s e) -> p h s e", e=dh)[:, :, slots, :]


def into_slots(part, copies):
    return part.unsqueeze(2).broadcast_to([part.shape[0], part.shape[1], copies, part.shape[2]])


def narrow_attention(k, name, turns, dh, causal, staging, q_tile, k_tile, v_tile, v_st, outs, shared_kv, divisor):
    nc = k.nc
    UNITS = 8
    ROWS = SLOTS * dh
    KV = UNITS // 4 if shared_kv else UNITS
    PER_KV = UNITS // KV
    SM = 4 * UNITS
    keys = [(i + 1) * P if causal else SEQ for i in range(QT)]
    first = [j if causal else 0 for j in range(QT)]
    row_off = [sum(keys[:i]) for i in range(QT + 1)]
    col_off = [sum((QT - first[m]) * P for m in range(j)) for j in range(QT + 1)]
    ORDER = [3, 2, 1, 0]

    def ahead(u):
        n = u + 1
        if n >= UNITS:
            return []
        return ([f"K{n // PER_KV}"] if n % PER_KV == 0 else []) + [f"Q{n}"]

    t_seq = ahead(-1)
    for u in range(UNITS + 1):
        if u >= 1:
            t_seq += [f"P{u - 1}.{j}" for j in range(QT)]
        t_seq += ahead(u)
    t_at = {a: n for n, a in enumerate(t_seq)}
    TR = len(t_seq)
    assert TR % 3 == 0
    act_seq, dve_seq = t_seq[3::2], t_seq[0:2] + t_seq[2::2]
    STAGED = len(staging(0))
    with ExitStack() as st:
        def sb(nm, shape, dt=F32):
            return k.sb(name + nm, shape, dt, st)

        qT, kT = sb("qT", [ROWS, UNITS, SEQ], BF16), sb("kT", [ROWS, KV, SEQ], BF16)
        probs, pt = sb("probs", [P, 2, row_off[QT]]), sb("pt", [P, 2, col_off[QT]])
        negmax = sb("negmax", [P, QT, UNITS])
        rowsum, rinv = sb("rowsum", [P, QT, UNITS]), sb("rinv", [P, QT, UNITS])
        oT = sb("out_t", [P, SEQ])
        sbank, tbank, obank, fbank = k.bank[0:3], k.bank[3:6], k.bank[6], k.bank[7]
        pers = dict(s_mm=SM, t_mm=TR, pv_mm=UNITS, turned=2, maxed=SM, t_dve=len(dve_seq), o_norm=2, rinv_ok=4,
                    exp_ok=SM, t_act=len(act_seq), o_copy=2, staged=STAGED)
        zeroed = k.sem(name + "_zeroed")
        s = {n: k.sem(name + "_" + n) for n in pers}
        due = {n: s[n].start(pers[n]) for n in pers}
        base = {n: s[n].base for n in pers}
        block = st.enter_context(nc.Block())

        def credit(eng, *names):
            for n in names:
                if due[n]:
                    eng.sem_inc(s[n].sem, pers[n])

        def waits(eng, g):
            def w(n, count):
                eng.wait_ge(s[n].sem, base[n] + pers[n] * (g + 1) + count)
            return w

        def copied(w, n):
            a, before = t_seq[n], n < 0
            if a in act_seq:
                w("t_act", act_seq.index(a) + 1 - before * len(act_seq))
            else:
                w("t_dve", dve_seq.index(a) + 1 - before * len(dve_seq))

        def copy_out(eng_copy, w, a):
            n = t_at[a]
            w("t_mm", n + 1)
            if a[0] == "P":
                u, j = int(a[1]), int(a[3])
                w("pv_mm", u - 1)
                return eng_copy(pt[:, u % 2, col_off[j]:col_off[j + 1]], tbank[n % 3][:, first[j] * P:SEQ])
            i = int(a[1])
            w("s_mm", 4 * (i + 1) * (PER_KV if a[0] == "K" else 1) - SM)
            return eng_copy((qT if a[0] == "Q" else kT)[:, i, :], tbank[n % 3][0:ROWS, :])

        @block.gpsimd
        def _(pool):
            nc.gpsimd.memset(v_st, 0.0).then_inc(zeroed.sem, 1)
            pool.wait_ge(zeroed.sem, 1)
            credit(pool, "staged")
            with pool.Fori(0, turns) as g:
                w = waits(pool, g)
                for n, (dst, src) in enumerate(staging(g)):
                    if n == 0:
                        w("t_mm", t_at[f"Q{UNITS - 1}"] + 1 - TR)
                    if n == STAGED - 1:
                        w("pv_mm", 0)
                    nc.gpsimd.tensor_copy(dst, src).then_inc(s["staged"].sem, 1)

        @block.tensor
        def _(pe):
            credit(pe, "s_mm", "t_mm", "pv_mm", "turned")
            with pe.Fori(0, turns) as g:
                w = waits(pe, g)

                def turn_stack(a):
                    n, i = t_at[a], int(a[1])
                    copied(w, n - 3)
                    for t in range(QT):
                        tile = q_tile(i, t) if a[0] == "Q" else k_tile(i, t)
                        ins = nc.tensor.matmul(tbank[n % 3][0:ROWS, t * P:(t + 1) * P], tile, k.identb[:, :], start=True, stop=True)
                    ins.then_inc(s["t_mm"].sem, 1)

                def scores(u, n):
                    i, m, kv = ORDER[n], 4 * u + n, u // PER_KV
                    w("exp_ok", m - 2 if m >= 3 else 0)
                    if n == 0:
                        copied(w, t_at[f"Q{u}"])
                        copied(w, t_at[f"K{kv}"])
                    ins = nc.tensor.matmul(sbank[m % 3][:, 0:keys[i]], qT[:, u, i * P:(i + 1) * P], kT[:, kv, 0:keys[i]],
                                           start=True, stop=not causal)
                    if causal:
                        ins = nc.tensor.matmul(sbank[m % 3][:, i * P:keys[i]], k.identb[:, :], k.maskb[:, :],
                                               start=False, stop=True)
                    ins.then_inc(s["s_mm"].sem, 1)

                def turn_probs(u, j):
                    n = t_at[f"P{u}.{j}"]
                    copied(w, n - 3)
                    if j == 0:
                        w("exp_ok", 4 * u + 4)
                    for i in range(first[j], QT):
                        ins = nc.tensor.transpose(tbank[n % 3][:, i * P:(i + 1) * P],
                                                  probs[:, u % 2, row_off[i] + j * P:row_off[i] + (j + 1) * P], k.ident[:, :])
                    ins.then_inc(s["t_mm"].sem, 1)

                def values(u):
                    copied(w, t_at[f"P{u}.2"])
                    copied(w, t_at[f"P{u}.3"])
                    if u == 0:
                        w("staged", STAGED)
                    if u % 4 == 0:
                        w("o_copy", u // 4)
                    rows = slice(32 * (u % 4), 32 * (u % 4) + 32)
                    for j in range(QT):
                        ins = nc.tensor.matmul(obank[rows, first[j] * P:SEQ], v_tile(u, j), pt[:, u % 2, col_off[j]:col_off[j + 1]],
                                               start=(j == 0), stop=(j == QT - 1))
                    ins.then_inc(s["pv_mm"].sem, 1)

                def turn_outputs(half):
                    w("o_copy", half + 1)
                    w("o_norm", half)
                    for i in range(QT):
                        ins = nc.tensor.transpose(fbank[:, i * P:(i + 1) * P], oT[:, i * P:(i + 1) * P], k.ident[:, :])
                    ins.then_inc(s["turned"].sem, 1)

                w("staged", STAGED - 1)
                for a in ahead(-1):
                    turn_stack(a)
                for u in range(UNITS + 2):
                    if u < UNITS:
                        scores(u, 0)
                        scores(u, 1)
                    if 1 <= u <= UNITS:
                        turn_probs(u - 1, 0)
                        turn_probs(u - 1, 1)
                    if u < UNITS:
                        scores(u, 2)
                    if 1 <= u <= UNITS:
                        turn_probs(u - 1, 2)
                        turn_probs(u - 1, 3)
                    if u < UNITS:
                        scores(u, 3)
                    for a in ahead(u):
                        turn_stack(a)
                    if u == 7:
                        turn_outputs(0)
                    if u >= 2:
                        values(u - 2)
                turn_outputs(1)

        @block.vector
        def _(dve):
            credit(dve, "maxed", "t_dve", "o_norm", "rinv_ok")
            with dve.Fori(0, turns) as g:
                w = waits(dve, g)

                def row_max(u, n):
                    i, m = ORDER[n], 4 * u + n
                    w("s_mm", m + 1)
                    nc.vector.tensor_reduce(negmax[:, i, u:u + 1], sbank[m % 3][:, 0:keys[i]], AX, ALU.max,
                                            negate=True).then_inc(s["maxed"].sem, 1)

                def copy(*stacks):
                    for a in stacks:
                        if a in dve_seq:
                            copy_out(nc.vector.tensor_copy, w, a).then_inc(s["t_dve"].sem, 1)

                def normalise(half):
                    units = slice(4 * half, 4 * half + 4)
                    w("exp_ok", SM // 2 * (half + 1))
                    nc.vector.tensor_scalar(rinv[:, :, units], rowsum[:, :, units], float(divisor), None, ALU.mult).then_inc(s["rinv_ok"].sem, 1)
                    w("rinv_ok", 2 * half + 1)
                    nc.vector.reciprocal(rinv[:, :, units], rinv[:, :, units]).then_inc(s["rinv_ok"].sem, 1)
                    w("turned", half + 1)
                    w("rinv_ok", 2 * half + 2)
                    nc.vector.tensor_tensor(outs(g, half), fbank[:, :].rearrange("p (i h e) -> p i h e", h=4, e=32)[:, :, :, 0:dh],
                                            rinv[:, :, units].unsqueeze(3).broadcast_to([P, QT, 4, dh]),
                                            ALU.mult).then_inc(s["o_norm"].sem, 1)

                copy(*ahead(-1))
                for u in range(UNITS + 1):
                    if u < UNITS:
                        row_max(u, 0)
                        row_max(u, 1)
                    if u >= 1:
                        copy(f"P{u - 1}.0", f"P{u - 1}.1")
                    if u < UNITS:
                        row_max(u, 2)
                    if u >= 1:
                        copy(f"P{u - 1}.2", f"P{u - 1}.3")
                    if u < UNITS:
                        row_max(u, 3)
                    copy(*ahead(u))
                    if u == UNITS - 1:
                        normalise(0)
                normalise(1)

        @block.scalar
        def _(act):
            credit(act, "exp_ok", "t_act", "o_copy")
            with act.Fori(0, turns) as g:
                w = waits(act, g)

                def exps(u, n):
                    i, m = ORDER[n], 4 * u + n
                    w("maxed", m + 1)
                    if n == 0:
                        w("t_mm", t_at[f"P{u - 2}.3"] + 1 if u >= 2 else t_at[f"P{u + UNITS - 2}.3"] + 1 - TR)
                        w("o_norm", -1 if u < 4 else 0)
                    nc.scalar.activation(probs[:, u % 2, row_off[i]:row_off[i + 1]], sbank[m % 3][:, 0:keys[i]], ACT.Exp,
                                         bias=negmax[:, i, u:u + 1], accum_out=rowsum[:, i, u:u + 1]).then_inc(s["exp_ok"].sem, 1)

                def copy(*stacks):
                    for a in stacks:
                        if a in act_seq:
                            copy_out(lambda o, i: nc.scalar.activation(o, i, ACT.Copy), w, a).then_inc(s["t_act"].sem, 1)

                def copy_outputs(half):
                    w("pv_mm", 4 * half + 4)
                    w("turned", half)
                    nc.scalar.activation(oT[:, :], obank[:, :], ACT.Copy).then_inc(s["o_copy"].sem, 1)

                for u in range(UNITS + 1):
                    if u < UNITS:
                        exps(u, 0)
                        exps(u, 1)
                    if u == 6:
                        copy_outputs(0)
                    if u >= 1:
                        copy(f"P{u - 1}.0", f"P{u - 1}.1")
                    if u < UNITS:
                        exps(u, 2)
                    if u >= 1:
                        copy(f"P{u - 1}.2", f"P{u - 1}.3")
                    if u < UNITS:
                        exps(u, 3)
                    copy(*ahead(u))
                copy_outputs(1)

        for n in pers:
            s[n].base += pers[n] * turns


def copy_parts(nc, part, q, kk, q_stack, k_stack, dh):
    q_slots, k_slots, copies = (Q_H, K_H, 3) if part == "high" else (Q_M, K_M, 2)
    nc.scalar.activation(by_slot(q_stack, q_slots, dh), into_slots(q, copies), ACT.Copy)
    return nc.scalar.activation(by_slot(k_stack, k_slots, dh), into_slots(kk, copies), ACT.Copy)


def subtract_parts(nc, part, q, kk, q_stack, k_stack, dh, rest=None):
    q_at, k_at = (Q_H, K_H) if part == "high" else (Q_M, K_M)
    q_rest, k_rest = rest or (by_slot(q_stack, Q_L, dh)[:, :, 0, :], by_slot(k_stack, K_L, dh)[:, :, 0, :])
    eng = nc.gpsimd if rest else nc.vector
    eng.tensor_tensor(q_rest, q, by_slot(q_stack, q_at, dh)[:, :, 0, :], ALU.subtract)
    return eng.tensor_tensor(k_rest, kk, by_slot(k_stack, k_at, dh)[:, :, 0, :], ALU.subtract)


def weights0(k, d, stack):
    wa, la, wf = (k.sb("n0" + nm, [P, KT, n], F32, stack) for nm, n in (("wa", 192), ("la", P), ("wf", D)))
    a_in, f_in = k.sem("n0_a_in"), k.sem("n0_f_in")

    def load(eng):
        eng.dma_start(wa[:, :, :], d["L0_wqkv"]).then_inc(a_in.sem, 16)
        eng.dma_start(la[:, :, :], d["L0_la"]).then_inc(f_in.sem, 16)
        eng.dma_start(wf[:, :, :], d["L0_wf"]).then_inc(f_in.sem, 16)

    return wa, la, wf, load


def narrow_layer0(k, d, wa, la, wf):
    nc = k.nc
    DH, H, NQKV, RANKS = 8, 8, 192, 48
    with ExitStack() as outer:
        def keep(nm, shape, dt=F32):
            return k.sb("n0" + nm, shape, dt, outer)

        qk = keep("qk", [P, 2, BATCH, QT * H, SLOTS * DH], BF16)
        vr = keep("vr", [P, BATCH, QT, H * DH])
        qk_st = keep("qk_st", [P, 2, QT, H, SLOTS * DH], BF16)
        v_st = keep("v_st", [P, QT * H, 32])
        outs = keep("outs", [P, BATCH, QT, H * DH])
        wo = keep("wo", [H * DH, D])
        with ExitStack() as st:
            def sb(nm, shape, dt=F32):
                return k.sb("n0" + nm, shape, dt, st)

            wah, wal = sb("wah", [P, KT, NQKV], F32R), sb("wal", [P, KT, NQKV], F32R)
            wfh, wfl = sb("wfh", [P, KT, D], F32R), sb("wfl", [P, KT, D], F32R)
            lah, lal = sb("lah", [P, KT, P], F32R), sb("lal", [P, KT, P], F32R)
            lb = sb("lb", [66, D])
            uT = sb("uT", [66, TOK])
            qkvb = sb("qkvb", [P, NQKV])
            qk_sum, qk_rest = sb("qk_sum", [P, 2, 2 * H, DH]), sb("qk_rest", [P, 2, 2 * H, DH])
            starts, startsf, cmp = sb("starts", [P, 4], I32), sb("startsf", [P, 4]), sb("cmp", [P, BATCH, 4])
            cnt, kcol, amask = sb("cnt", [P, BATCH]), sb("kcol", [P, 1]), sb("amask", [P, BATCH])
            a_in, f_in, c_in, hi, lo, chain, q_mm, q_out, u_mm, u_out, y_mm, y_out, ones = (
                k.sem("n0_" + n) for n in "a_in f_in c_in hi lo chain q_mm q_out u_mm u_out y_mm y_add ones".split())
            summed, high, rest, middle, low = (k.sem("n0_stack_" + n) for n in "sum high rest middle low".split())
            parts = ((wa, wah, wal), (la, lah, lal), (wf, wfh, wfl))

            def stacks(t):
                heads = slice((t % QT) * H, (t % QT + 1) * H)
                return qk[:, 0, t // QT, heads, :], qk[:, 1, t // QT, heads, :]

            block = st.enter_context(nc.Block())

            @block.sync
            def _(sp):
                sp.dma_start(lb[:, :], d["L0_lb"]).then_inc(c_in.sem, 16)
                sp.dma_start(qkvb[:, :], d["L0_qkvb"].partition_broadcast(P)).then_inc(c_in.sem, 16)
                sp.dma_start(starts[:, :], d["L0_starts"].partition_broadcast(P)).then_inc(c_in.sem, 16)
                sp.dma_start(kcol[:, :], d["L0_kcol"]).then_inc(c_in.sem, 16)
                sp.dma_start(wo[:, :], d["L0_wo"]).then_inc(c_in.sem, 16)

            @block.scalar
            def _(act):
                act.wait_ge(a_in.sem, 16)
                for n, (src, h, _) in enumerate(parts):
                    if n == 1:
                        act.wait_ge(f_in.sem, 32)
                    nc.scalar.activation(h[:, :, :], src[:, :, :], ACT.Copy).then_inc(hi.sem, 1)

                def high_part(t):
                    act.wait_ge(summed.sem, t + 1)
                    copy_parts(nc, "high", qk_sum[:, t % 2, 0:H, :], qk_sum[:, t % 2, H:, :], *stacks(t), DH).then_inc(high.sem, 1)

                high_part(0)
                for t in range(TT):
                    if t + 1 < TT:
                        high_part(t + 1)
                    act.wait_ge(rest.sem, t + 1)
                    copy_parts(nc, "middle", qk_rest[:, t % 2, 0:H, :], qk_rest[:, t % 2, H:, :], *stacks(t), DH).then_inc(middle.sem, 1)

            @block.gpsimd
            def _(pool):
                for n, (src, h, l) in enumerate(parts):
                    pool.wait_ge(hi.sem, n + 1)
                    nc.gpsimd.tensor_tensor(l[:, :, :], src[:, :, :], h[:, :, :].bitcast(F32), ALU.subtract).then_inc(lo.sem, 1)
                for t in range(TT):
                    pool.wait_ge(high.sem, t + 1)
                    if t >= 2:
                        pool.wait_ge(low.sem, t - 1)
                    subtract_parts(nc, "high", qk_sum[:, t % 2, 0:H, :], qk_sum[:, t % 2, H:, :], *stacks(t), DH,
                                   (qk_rest[:, t % 2, 0:H, :], qk_rest[:, t % 2, H:, :])).then_inc(rest.sem, 1)

            @block.tensor
            def _(pe):
                pe.wait_ge(lo.sem, 1)
                for t in range(TT):
                    if t >= 2:
                        pe.wait_ge(q_out.sem, t - 1)
                    tok = slice(t * P, (t + 1) * P)
                    for a in range(KT):
                        ins = matmul3(nc, k.bank[t % 2][:, 0:NQKV], k.xTh[:, a, tok], k.xTl[:, a, tok],
                                      wah[:, a, :], wal[:, a, :], a == 0, a == KT - 1)
                    ins.then_inc(q_mm.sem, 1)
                pe.wait_ge(lo.sem, 2)
                for b in range(BATCH):
                    tok = slice(b * SEQ, (b + 1) * SEQ)
                    for a in range(KT):
                        ins = matmul3(nc, k.bank[2 + b][:, :], lah[:, a, :], lal[:, a, :], k.xTh[:, a, tok],
                                      k.xTl[:, a, tok], a == 0, a == KT - 1)
                    ins.then_inc(u_mm.sem, 1)
                pe.wait_ge(lo.sem, 3)
                pe.wait_ge(ones.sem, 1)
                pe.wait_ge(c_in.sem, 80)
                for t in range(TT):
                    if t >= 4:
                        pe.wait_ge(y_out.sem, t - 3)
                    tok, bank = slice(t * P, (t + 1) * P), k.bank[4 + t % 4]
                    for a in range(KT):
                        matmul3(nc, bank[:, :], k.xTh[:, a, tok], k.xTl[:, a, tok], wfh[:, a, :], wfl[:, a, :], a == 0, False)
                    pe.wait_ge(u_out.sem, t // QT + 1)
                    nc.tensor.matmul(bank[:, :], uT[:, tok], lb[:, :], start=False, stop=True).then_inc(y_mm.sem, 1)

            @block.vector
            def _(dve):
                steps = [0]

                def link(ins):
                    steps[0] += 1
                    ins.then_inc(chain.sem, 1)
                    dve.wait_ge(chain.sem, steps[0])

                nc.vector.memset(uT[64:66, :], 1.0).then_inc(ones.sem, 1)
                dve.wait_ge(c_in.sem, 80)
                link(nc.vector.tensor_copy(startsf[:, :], starts[:, :]))
                for b in range(BATCH):
                    ins = nc.vector.tensor_scalar(cmp[:, b, :], startsf[:, :], float(b), None, ALU.is_le)
                link(ins)
                link(nc.vector.tensor_reduce(cnt[:, :], cmp[:, :, :], AX, ALU.add))
                link(nc.vector.tensor_tensor(amask[:, :], cnt[:, :], kcol[:, :].broadcast_to([P, BATCH]), ALU.is_equal))

                def low_part(t):
                    dve.wait_ge(middle.sem, t + 1)
                    subtract_parts(nc, "middle", qk_rest[:, t % 2, 0:H, :], qk_rest[:, t % 2, H:, :], *stacks(t), DH).then_inc(low.sem, 1)

                for t in range(TT):
                    b, tt = t // QT, t % QT
                    dve.wait_ge(q_mm.sem, t + 1)
                    if t >= 2:
                        dve.wait_ge(rest.sem, t - 1)
                    both = k.bank[t % 2][:, 0:P].rearrange("p (h e z) -> p h e z", h=H, e=DH)
                    qb = qkvb[:, 0:P].rearrange("p (h e z) -> p h e z", h=H, e=DH)
                    for z in range(2):
                        ins = nc.vector.tensor_tensor(qk_sum[:, t % 2, z * H:(z + 1) * H, :], both[:, :, :, z], qb[:, :, :, z], ALU.add)
                    ins.then_inc(summed.sem, 1)
                    nc.vector.tensor_tensor(vr[:, b, tt, :], k.bank[t % 2][:, P:NQKV], qkvb[:, P:NQKV], ALU.add).then_inc(q_out.sem, 1)
                    if t >= 2:
                        low_part(t - 2)
                low_part(TT - 2)
                low_part(TT - 1)
                for b in range(BATCH):
                    dve.wait_ge(u_mm.sem, b + 1)
                    nc.vector.tensor_scalar(uT[0:64, b * SEQ:(b + 1) * SEQ], k.bank[2 + b][0:64, :], amask[0:64, b:b + 1], None,
                                            ALU.mult).then_inc(u_out.sem, 1)
                for t in range(TT):
                    dve.wait_ge(y_mm.sem, t + 1)
                    nc.vector.tensor_tensor(k.x[:, t, :], k.bank[4 + t % 4][:, :], k.x[:, t, :], ALU.add).then_inc(y_out.sem, 1)

        def turn_outs(g, half):
            return outs[:, bass.ds(g, 1), :, half * 4 * DH:(half + 1) * 4 * DH].rearrange("p g i (h e) -> p (g i) h e", h=4)

        def staging(g):
            return [(qk_st[:, z, :, :, :].rearrange("p t h r -> p (t h r)").bitcast(I32),
                     qk[:, z, bass.ds(g, 1), :, :].rearrange("p b h r -> p (b h r)").bitcast(I32)) for z in range(2)] + [
                    (v_st[:, :, 0:DH], vr[:, bass.ds(g, 1), :, :].rearrange("p b t (h e) -> p (b t h) e", e=DH))]

        narrow_attention(k, "n0", BATCH, DH, False, staging, lambda u, t: qk_st[:, 0, t, u, :], lambda u, t: qk_st[:, 1, t, u, :],
                         lambda u, t: v_st[:, t * H + u, :], v_st[:, :, :], turn_outs, False, float(H * DH) ** 0.5)
        project_narrow(k, "n0", wo, 1, H * DH, lambda t, a: outs[:, t // QT, t % QT, :])


def project_narrow(k, name, wo, chunks, rows, piece):
    nc = k.nc
    with ExitStack() as st:
        oT = k.sb(name + "oT", [rows, 2, chunks, P], F32, st)
        turned, copied, mm, added = (k.sem("pn_" + n) for n in "turned copied mm added".split())
        b = [s.base for s in (turned, copied, mm, added)]
        block = st.enter_context(nc.Block())

        @block.tensor
        def _(pe):
            def turn(t):
                if t >= 2:
                    pe.wait_ge(copied.sem, b[1] + t - 1)
                for a in range(chunks):
                    ins = nc.tensor.transpose(k.bank[t % 2][0:rows, a * P:(a + 1) * P], piece(t, a), k.ident[:, :])
                ins.then_inc(turned.sem, 1)

            turn(0)
            for t in range(TT):
                if t + 1 < TT:
                    turn(t + 1)
                pe.wait_ge(copied.sem, b[1] + t + 1)
                if t >= 4:
                    pe.wait_ge(added.sem, b[3] + t - 3)
                for a in range(chunks):
                    w = wo[:, :] if chunks == 1 else wo[:, a, :]
                    ins = nc.tensor.matmul(k.bank[4 + t % 4][:, :], oT[:, t % 2, a, :], w, start=(a == 0), stop=(a == chunks - 1))
                ins.then_inc(mm.sem, 1)

        @block.scalar
        def _(act):
            for t in range(TT):
                act.wait_ge(turned.sem, b[0] + t + 1)
                if t >= 2:
                    act.wait_ge(mm.sem, b[2] + t - 1)
                nc.scalar.activation(oT[:, t % 2, :, :], k.bank[t % 2][0:rows, 0:chunks * P].rearrange("p (a q) -> p a q", a=chunks),
                                     ACT.Copy).then_inc(copied.sem, 1)

        @block.vector
        def _(dve):
            for t in range(TT):
                dve.wait_ge(mm.sem, b[2] + t + 1)
                nc.vector.tensor_tensor(k.x[:, t, :], k.bank[4 + t % 4][:, :], k.x[:, t, :], ALU.add).then_inc(added.sem, 1)

        for s in (turned, copied, mm, added):
            s.base += TT


def weights2(k, d, stack):
    wa = k.sb("n2wa", [P, KT, 768], F32, stack)
    tab = k.sb("n2tab", [P, QT, 4, 16], F32, stack)
    wo = k.sb("n2wo", [P, KT, D], F32, stack)
    a_in, c_in = k.sem("n2_a_in"), k.sem("n2_c_in")

    def load(eng):
        eng.dma_start(wa[:, :, :], d["L2_wqkv"]).then_inc(a_in.sem, 16)
        eng.dma_start(tab[:, :, :, :], d["L2_tab"]).then_inc(c_in.sem, 16)
        eng.dma_start(wo[:, :, :], d["L2_wo"]).then_inc(c_in.sem, 16)

    return wa, tab, wo, load


def narrow_attention2(k, d, wa, tab, wo):
    nc = k.nc
    DH, H, G = 16, 32, 8
    NQ, NKV = H * DH, 2 * G * DH
    with ExitStack() as outer:
        def keep(nm, shape, dt=F32):
            return k.sb("n2" + nm, shape, dt, outer)

        qs, ks = keep("qs", [P, TT, H, SLOTS * DH], BF16), keep("ks", [P, TT, G, SLOTS * DH], BF16)
        vr = keep("vr", [P, TT, G, DH])
        q_st, k_st = keep("q_st", [P, TT, HPG, SLOTS * DH], BF16), keep("k_st", [P, TT, SLOTS * DH], BF16)
        v_st = keep("v_st", [P, TT, 32])
        outs = keep("outs", [P, TT, G, 4 * DH])
        with ExitStack() as st:
            def sb(nm, shape, dt=F32):
                return k.sb("n2" + nm, shape, dt, st)

            NW = NQ + NKV
            wah, wal = sb("wah", [P, KT, NW], F32R), sb("wal", [P, KT, NW], F32R)
            ra, rb = sb("ra", [P, 2, NQ + G * DH]), sb("rb", [P, 2, NQ + G * DH])
            qk_sum, qk_rest = sb("qk_sum", [P, 2, H + G, DH]), sb("qk_rest", [P, 2, H + G, DH])
            a_in, c_in, hi, lo, mm, rot, summed, high, rest, middle, low = (
                k.sem("n2_" + n) for n in "a_in c_in hi lo mm rot summed high rest middle low".split())
            block = st.enter_context(nc.Block())

            @block.scalar
            def _(act):
                act.wait_ge(a_in.sem, 16)
                for a in range(KT):
                    nc.scalar.activation(wah[:, a, :], wa[:, a, :], ACT.Copy).then_inc(hi.sem, 1)

                def high_part(t):
                    act.wait_ge(summed.sem, t + 1)
                    copy_parts(nc, "high", qk_sum[:, t % 2, 0:H, :], qk_sum[:, t % 2, H:, :], qs[:, t, :, :], ks[:, t, :, :],
                               DH).then_inc(high.sem, 1)

                high_part(0)
                for t in range(TT):
                    if t + 1 < TT:
                        high_part(t + 1)
                    act.wait_ge(rest.sem, t + 1)
                    copy_parts(nc, "middle", qk_rest[:, t % 2, 0:H, :], qk_rest[:, t % 2, H:, :], qs[:, t, :, :], ks[:, t, :, :],
                               DH).then_inc(middle.sem, 1)

            @block.tensor
            def _(pe):
                for t in range(TT):
                    if t >= 2:
                        pe.wait_ge(rot.sem, t - 1)
                    tok = slice(t * P, (t + 1) * P)
                    for a in range(KT):
                        if t == 0:
                            pe.wait_ge(lo.sem, a + 1)
                        q, kv = k.bank[2 * (t % 2)][:, :], k.bank[2 * (t % 2) + 1][:, 0:NKV]
                        matmul3(nc, q, k.xTh[:, a, tok], k.xTl[:, a, tok], wah[:, a, 0:NQ], wal[:, a, 0:NQ], a == 0, a == KT - 1)
                        ins = matmul3(nc, kv, k.xTh[:, a, tok], k.xTl[:, a, tok], wah[:, a, NQ:], wal[:, a, NQ:], a == 0, a == KT - 1)
                    ins.then_inc(mm.sem, 1)

            @block.vector
            def _(dve):
                for a in range(KT):
                    dve.wait_ge(hi.sem, a + 1)
                    nc.vector.tensor_tensor(wal[:, a, :], wa[:, a, :], wah[:, a, :].bitcast(F32), ALU.subtract).then_inc(lo.sem, 1)
                dve.wait_ge(c_in.sem, 32)

                def low_part(t):
                    dve.wait_ge(middle.sem, t + 1)
                    subtract_parts(nc, "middle", qk_rest[:, t % 2, 0:H, :], qk_rest[:, t % 2, H:, :], qs[:, t, :, :], ks[:, t, :, :],
                                   DH).then_inc(low.sem, 1)

                for t in range(TT):
                    dve.wait_ge(mm.sem, t + 1)
                    if t >= 2:
                        dve.wait_ge(summed.sem, t - 1)
                    nc.vector.tensor_copy(vr[:, t, :, :],
                                          k.bank[2 * (t % 2) + 1][:, G * DH:NKV].rearrange("p (g e) -> p g e", g=G))
                    HF = DH // 2
                    for bank, heads, c, at in ((k.bank[2 * (t % 2)], H, 0, 0), (k.bank[2 * (t % 2) + 1], G, 2, NQ)):
                        src = bank[:, 0:heads * DH].rearrange("p (h e) -> p h e", h=heads)
                        a_ = ra[:, t % 2, at:at + heads * DH].rearrange("p (h e) -> p h e", h=heads)
                        b_ = rb[:, t % 2, at:at + heads * DH].rearrange("p (h e) -> p h e", h=heads)
                        cos = tab[:, t % QT, c:c + 1, :].broadcast_to([P, heads, DH])
                        sin = tab[:, t % QT, c + 1:c + 2, :].broadcast_to([P, heads, DH])
                        nc.vector.tensor_tensor(a_, src, cos, ALU.mult)
                        nc.vector.tensor_tensor(b_[:, :, 0:HF], src[:, :, HF:DH], sin[:, :, 0:HF], ALU.mult)
                        ins = nc.vector.tensor_tensor(b_[:, :, HF:DH], src[:, :, 0:HF], sin[:, :, HF:DH], ALU.mult)
                    ins.then_inc(rot.sem, 1)
                    if t >= 2:
                        low_part(t - 2)
                low_part(TT - 2)
                low_part(TT - 1)

            @block.gpsimd
            def _(pool):

                def add(t):
                    pool.wait_ge(rot.sem, t + 1)
                    if t >= 2:
                        pool.wait_ge(rest.sem, t - 1)
                    nc.gpsimd.tensor_tensor(qk_sum[:, t % 2, :, :].rearrange("p h e -> p (h e)"), ra[:, t % 2, :], rb[:, t % 2, :],
                                            ALU.add).then_inc(summed.sem, 1)

                add(0)
                for t in range(TT):
                    if t + 1 < TT:
                        add(t + 1)
                    pool.wait_ge(high.sem, t + 1)
                    if t >= 2:
                        pool.wait_ge(low.sem, t - 1)
                    subtract_parts(nc, "high", qk_sum[:, t % 2, 0:H, :], qk_sum[:, t % 2, H:, :], qs[:, t, :, :], ks[:, t, :, :], DH,
                                   (qk_rest[:, t % 2, 0:H, :], qk_rest[:, t % 2, H:, :])).then_inc(rest.sem, 1)

        def turn_outs(g, half):
            return outs[:, half * QT:(half + 1) * QT, bass.ds(g, 1), :].rearrange("p i g (h e) -> p (i g) h e", h=4)

        def staging(g):
            heads = qs[:, :, :, :].rearrange("p t (g h) r -> p t g (h r)", h=HPG)[:, :, bass.ds(g, 1), :]
            return [(q_st[:, :, :, :].rearrange("p t h r -> p t (h r)").bitcast(I32), heads.rearrange("p t g r -> p (t g) r").bitcast(I32)),
                    (k_st[:, :, :].bitcast(I32), ks[:, :, bass.ds(g, 1), :].rearrange("p t g r -> p (t g) r").bitcast(I32)),
                    (v_st[:, :, 0:DH], vr[:, :, bass.ds(g, 1), :].rearrange("p t g e -> p (t g) e"))]

        narrow_attention(k, "n2", G, DH, True, staging, lambda u, t: q_st[:, (u // 4) * QT + t, u % 4, :],
                         lambda a, t: k_st[:, a * QT + t, :], lambda u, t: v_st[:, (u // 4) * QT + t, :], v_st[:, :, :],
                         turn_outs, True, 1.0)

        def piece(t, a):
            return outs[:, t, 2 * a:2 * a + 2, :].rearrange("p g e -> p (g e)")

        project_narrow(k, "n2", wo, KT, P, piece)


def memory_buffers(k, d, name, stack):
    def sb(nm, shape):
        return k.sb(name + "m_" + nm, shape, F32, stack)

    m = Shared()
    m.wq, m.wu = sb("wq", [P, KT, P]), sb("wu", [P, KT, P])
    m.wr = sb("wr", [BOT, BOT])
    m.keysT = sb("keysT", [BOT, NSLOT])
    m.rkT, m.keysA = sb("rkT", [BOT + 1, NSLOT]), sb("keysA", [BOT + 1, NSLOT])
    m.valsT, m.wvd, m.wvu = sb("valsT", [P, KT, NSLOT]), sb("wvd", [P, KT, VB]), sb("wvu", [VB, D])
    m.bu1, m.wu2 = sb("bu1", [P, 1]), sb("wu2", [P, 1])
    m.scal = sb("scal", [P, 3])
    w_in, c_in = k.sem("m_w_in"), k.sem("m_c_in")

    def load(eng):
        eng.dma_start(m.wq[:, :, :], d[name + "m_wq"]).then_inc(w_in.sem, 16)
        eng.dma_start(m.wu[:, :, :], d[name + "m_wu1"]).then_inc(w_in.sem, 16)
        for buf, n in ((m.wr[:, :], "wr"), (m.keysT[:, :], "keysT"), (m.valsT[:, :, :], "valsT"), (m.wvd[:, :, :], "wvd"),
                       (m.wvu[:, :], "wvu"), (m.bu1[:, :], "bu1"), (m.wu2[:, :], "wu2"), (m.rkT[BOT:BOT + 1, :], "log_rel"),
                       (m.keysA[BOT:BOT + 1, :], "log_rel")):
            eng.dma_start(buf, d[name + "m_" + n]).then_inc(c_in.sem, 16)
        eng.dma_start(m.scal[:, :], d[name + "m_scal"].partition_broadcast(P)).then_inc(c_in.sem, 16)

    return m, load


def memory_ffn(k, d, name, m, load_ahead=None):
    nc = k.nc
    with ExitStack() as st:
        def sb(nm, shape, dt=F32):
            return k.sb(name + "m_" + nm, shape, dt, st)

        wq, wu, wr, keysT, rkT, keysA, valsT, wvd, wvu, bu1, wu2, scal = (
            m.wq, m.wu, m.wr, m.keysT, m.rkT, m.keysA, m.valsT, m.wvd, m.wvu, m.bu1, m.wu2, m.scal)
        wqh, wql = sb("wqh", [P, KT, P], F32R), sb("wql", [P, KT, P], F32R)
        wuh, wul = sb("wuh", [P, KT, P], F32R), sb("wul", [P, KT, P], F32R)
        qA, rqA = sb("qA", [BOT + 1, TOK]), sb("rqA", [BOT + 1, TOK])
        vw, mix = sb("vw", [VB, NSLOT]), sb("mix", [NSLOT, D])
        ones = sb("ones", [P, P])
        gl = sb("gl", [P, TOK])
        lv, lsum, rl = sb("lv", [P, TT]), sb("lsum", [P, 1]), sb("rl", [P, 1])
        sg, u, gate, ge, fac = sb("sg", [P, TT]), sb("u", [P, TT]), sb("gate", [P, TT]), sb("ge", [P, TT]), sb("fac", [P, TT])
        top, rep = sb("top", [P, TT, TOPK]), sb("rep", [P, 3, NSLOT])
        att = sb("att", [P, 3, NSLOT])
        negmax, rowsum, rinv = sb("negmax", [P, TT]), sb("rowsum", [P, TT]), sb("rinv", [P, TT])
        wts, wT = sb("wts", [P, 2, NSLOT]), sb("wT", [P, 2, P])
        names = "w_in c_in hi lo pe_mm mid chain gelu q_out s_mm masked exp wt_mm wt_cp y_mm y_add lrn ln sig sig2 ones".split()
        s = {n: k.sem("m_" + n) for n in names}
        b0 = {n: s[n].base for n in names}
        counts = dict.fromkeys(names, 0)

        def inc(ins, n, by=1):
            counts[n] += by
            return ins.then_inc(s[n].sem, by)

        block = st.enter_context(nc.Block())
        B = k.bank
        score_bank = (B[0], B[1], B[6])

        counts["w_in"], counts["c_in"] = 32, 160

        @block.sync
        def _(sp):
            if load_ahead:
                load_ahead(sp)

        C_IN = b0["c_in"] + 160

        @block.gpsimd
        def _(pool):
            for n, (src, h, l) in enumerate(((wq, wqh, wql), (wu, wuh, wul))):
                pool.wait_ge(s["hi"].sem, b0["hi"] + n + 1)
                inc(nc.gpsimd.tensor_tensor(l[:, :, :], src[:, :, :], h[:, :, :].bitcast(F32), ALU.subtract), "lo")

        @block.tensor
        def _(pe):
            pe.wait_ge(s["c_in"].sem, C_IN)
            for a in range(KT):
                ins = nc.tensor.matmul(B[0][0:VB, 0:NSLOT], wvd[:, a, :], valsT[:, a, :], start=(a == 0), stop=(a == KT - 1))
            inc(ins, "pe_mm")
            inc(nc.tensor.matmul(B[1][0:BOT, 0:NSLOT], wr[:, :], keysT[:, :], start=True, stop=True), "pe_mm")
            pe.wait_ge(s["lo"].sem, b0["lo"] + 1)
            for b in range(BATCH):
                tok = slice(b * SEQ, (b + 1) * SEQ)
                for a in range(KT):
                    ins = matmul3(nc, B[2 + b][:, :], wqh[:, a, :], wql[:, a, :], k.xTh[:, a, tok], k.xTl[:, a, tok], a == 0, a == KT - 1)
                inc(ins, "pe_mm")
            pe.wait_ge(s["lo"].sem, b0["lo"] + 2)
            for b in range(BATCH):
                tok = slice(b * SEQ, (b + 1) * SEQ)
                for a in range(KT):
                    ins = matmul3(nc, B[4 + b][:, :], wuh[:, a, :], wul[:, a, :], k.xTh[:, a, tok], k.xTl[:, a, tok], a == 0, a == KT - 1)
                inc(ins, "pe_mm")
            pe.wait_ge(s["mid"].sem, b0["mid"] + 1)
            inc(nc.tensor.matmul(B[6][:, :], vw[:, :], wvu[:, :], start=True, stop=True), "pe_mm")
            for b in range(BATCH):
                pe.wait_ge(s["q_out"].sem, b0["q_out"] + b + 1)
                inc(nc.tensor.matmul(B[2 + b][0:BOT, :], wr[:, :], qA[0:BOT, b * SEQ:(b + 1) * SEQ], start=True, stop=True), "pe_mm")
            pe.wait_ge(s["gelu"].sem, b0["gelu"] + 2)
            pe.wait_ge(s["mid"].sem, b0["mid"] + 3)
            for t in range(TT):
                ins = nc.tensor.matmul(B[7][:, t:t + 1], gl[:, t * P:(t + 1) * P], wu2[:, :], start=True, stop=True)
            pe.wait_ge(s["ones"].sem, b0["ones"] + 1)
            pe.wait_ge(s["ln"].sem, b0["ln"] + 1)
            inc(nc.tensor.matmul(B[7][:, 16:16 + TT], ones[:, :], lv[:, :], start=True, stop=True), "lrn")
            pe.wait_ge(s["mid"].sem, b0["mid"] + 5)

            def slot_scores(t):
                if t >= 3:
                    pe.wait_ge(s["masked"].sem, b0["masked"] + t - 2)
                tok = slice(t * P, (t + 1) * P)
                nc.tensor.matmul(score_bank[t % 3][:, 0:NSLOT], rqA[:, tok], rkT[:, :], start=True, stop=True)
                inc(nc.tensor.matmul(score_bank[t % 3][:, NSLOT:2 * NSLOT], qA[:, tok], keysA[:, :], start=True, stop=True), "s_mm")

            def turn_weights(t):
                pe.wait_ge(s["exp"].sem, b0["exp"] + t + 1)
                if t >= 2:
                    pe.wait_ge(s["wt_cp"].sem, b0["wt_cp"] + t - 1)
                inc(nc.tensor.transpose(B[2 + t % 2][:, 0:P], wts[:, t % 2, :], k.ident[:, :]), "wt_mm")

            slot_scores(0)
            slot_scores(1)
            turn_weights(0)
            for t in range(TT):
                if t + 2 < TT:
                    slot_scores(t + 2)
                if t + 1 < TT:
                    turn_weights(t + 1)
                pe.wait_ge(s["wt_cp"].sem, b0["wt_cp"] + t + 1)
                if t >= 2:
                    pe.wait_ge(s["y_add"].sem, b0["y_add"] + t - 1)
                inc(nc.tensor.matmul(B[4 + t % 2][:, :], wT[:, t % 2, :], mix[:, :], start=True, stop=True), "y_mm")

        @block.scalar
        def _(act):
            act.wait_ge(s["w_in"].sem, b0["w_in"] + 32)
            for src, h in ((wq, wqh), (wu, wuh)):
                inc(nc.scalar.activation(h[:, :, :], src[:, :, :], ACT.Copy), "hi")
            act.wait_ge(s["c_in"].sem, C_IN)
            for b in range(BATCH):
                act.wait_ge(s["pe_mm"].sem, b0["pe_mm"] + 5 + b)
                inc(nc.scalar.activation(gl[:, b * SEQ:(b + 1) * SEQ], B[4 + b][:, :], ACT.Gelu_apprx_tanh, bias=bu1[:, :]), "gelu")
            inc(nc.scalar.activation(lv[:, :], k.xvar[:, :], ACT.Ln, bias=1.0), "ln")
            act.wait_ge(s["chain"].sem, b0["chain"] + 1)
            inc(nc.scalar.activation(sg[:, :], B[7][:, 0:TT], ACT.Sigmoid, bias=scal[:, 0:1]), "sig")
            act.wait_ge(s["chain"].sem, b0["chain"] + 8)
            inc(nc.scalar.activation(gate[:, :], u[:, :], ACT.Sigmoid, bias=scal[:, 2:3], scale=scal[:, 1:2]), "sig2")
            for t in range(TT):
                act.wait_ge(s["masked"].sem, b0["masked"] + t + 1)
                if t >= 2:
                    act.wait_ge(s["wt_mm"].sem, b0["wt_mm"] + t - 1)
                inc(nc.scalar.activation(wts[:, t % 2, :], att[:, t % 3, :], ACT.Exp, bias=negmax[:, t:t + 1],
                                         accum_out=rowsum[:, t:t + 1]), "exp")
                act.wait_ge(s["wt_mm"].sem, b0["wt_mm"] + t + 1)
                if t >= 2:
                    act.wait_ge(s["y_mm"].sem, b0["y_mm"] + t - 1)
                inc(nc.scalar.activation(wT[:, t % 2, :], B[2 + t % 2][:, 0:P], ACT.Copy), "wt_cp")

        @block.vector
        def _(dve):
            steps = [0]

            def link(ins):
                steps[0] += 1
                inc(ins, "chain")
                dve.wait_ge(s["chain"].sem, b0["chain"] + steps[0])

            nc.vector.memset(qA[BOT:BOT + 1, :], 1.0)
            nc.vector.memset(rqA[BOT:BOT + 1, :], 1.0)
            inc(nc.vector.memset(ones[:, :], 1.0), "ones")
            dve.wait_ge(s["c_in"].sem, C_IN)
            dve.wait_ge(s["pe_mm"].sem, b0["pe_mm"] + 1)
            inc(nc.vector.tensor_copy(vw[:, :], B[0][0:VB, 0:NSLOT]), "mid")
            dve.wait_ge(s["pe_mm"].sem, b0["pe_mm"] + 2)
            inc(nc.vector.tensor_scalar(rkT[0:BOT, :], B[1][0:BOT, 0:NSLOT], float(1.0 / np.sqrt(RDIM)), None, ALU.mult), "mid")
            inc(nc.vector.tensor_scalar(keysA[0:BOT, :], keysT[:, :], float(1.0 / np.sqrt(BOT)), None, ALU.mult), "mid")
            for b in range(BATCH):
                dve.wait_ge(s["pe_mm"].sem, b0["pe_mm"] + 3 + b)
                inc(nc.vector.tensor_copy(qA[0:BOT, b * SEQ:(b + 1) * SEQ], B[2 + b][0:BOT, :]), "q_out")
            dve.wait_ge(s["pe_mm"].sem, b0["pe_mm"] + 7)
            nc.vector.tensor_copy(mix[:, :], B[6][:, :])
            for b in range(BATCH):
                dve.wait_ge(s["pe_mm"].sem, b0["pe_mm"] + 8 + b)
                inc(nc.vector.tensor_copy(rqA[0:BOT, b * SEQ:(b + 1) * SEQ], B[2 + b][0:BOT, :]), "mid")
            dve.wait_ge(s["lrn"].sem, b0["lrn"] + 1)
            link(nc.vector.tensor_reduce(lsum[:, :], B[7][:, 16:16 + TT], AX, ALU.add))
            link(nc.vector.tensor_scalar(lsum[:, :], lsum[:, :], 1.0 / TOK, 1e-6, ALU.mult, ALU.add))
            link(nc.vector.reciprocal(rl[:, :], lsum[:, :]))
            dve.wait_ge(s["sig"].sem, b0["sig"] + 1)
            dve.wait_ge(s["ln"].sem, b0["ln"] + 1)
            nc.vector.tensor_scalar(u[:, :], lv[:, :], rl[:, 0:1], 0.5, ALU.mult, ALU.mult)
            link(nc.vector.tensor_scalar(ge[:, :], sg[:, :], 2.5, None, ALU.mult))
            link(nc.vector.tensor_tensor(u[:, :], u[:, :], ge[:, :], ALU.add))
            link(nc.vector.tensor_scalar(u[:, :], u[:, :], 0.0, 5.0, ALU.max, ALU.min))
            TAU_LOW, TAU_HIGH = 0.5, 2.0
            link(nc.vector.tensor_scalar(fac[:, :], u[:, :], -TAU_LOW, 1.0 / (TAU_HIGH - TAU_LOW), ALU.add, ALU.mult))
            link(nc.vector.tensor_scalar(u[:, :], fac[:, :], 0.0, 1.0, ALU.max, ALU.min))
            dve.wait_ge(s["sig2"].sem, b0["sig2"] + 1)
            link(nc.vector.tensor_scalar(ge[:, :], gate[:, :], 0.05, None, ALU.is_ge))
            link(nc.vector.tensor_tensor(gate[:, :], gate[:, :], ge[:, :], ALU.mult))

            def choose(t):
                dve.wait_ge(s["s_mm"].sem, b0["s_mm"] + t + 1)
                sc = score_bank[t % 3][:, 0:NSLOT]
                link(nc.vector.max(top[:, t, :], sc))
                link(nc.vector.match_replace(rep[:, t % 3, :], top[:, t, :], sc, -3e38))
                link(nc.vector.tensor_tensor(rep[:, t % 3, :], rep[:, t % 3, :], sc, ALU.is_equal))
                if t >= 3:
                    dve.wait_ge(s["exp"].sem, b0["exp"] + t - 2)
                link(nc.vector.scalar_tensor_tensor(out=att[:, t % 3, :], in0=rep[:, t % 3, :], scalar=MASKED,
                                                    in1=score_bank[t % 3][:, NSLOT:2 * NSLOT], op0=ALU.mult, op1=ALU.add))
                inc(nc.vector.tensor_reduce(negmax[:, t:t + 1], att[:, t % 3, :], AX, ALU.max, negate=True), "masked")

            def add(t):
                dve.wait_ge(s["exp"].sem, b0["exp"] + t + 1)
                link(nc.vector.reciprocal(rinv[:, t:t + 1], rowsum[:, t:t + 1]))
                link(nc.vector.tensor_tensor(fac[:, t:t + 1], rinv[:, t:t + 1], gate[:, t:t + 1], ALU.mult))
                dve.wait_ge(s["y_mm"].sem, b0["y_mm"] + t + 1)
                inc(nc.vector.scalar_tensor_tensor(out=k.x[:, t, :], in0=B[4 + t % 2][:, :], scalar=fac[:, t:t + 1],
                                                   in1=k.x[:, t, :], op0=ALU.mult, op1=ALU.add), "y_add")

            choose(0)
            choose(1)
            for t in range(TT):
                if t + 2 < TT:
                    choose(t + 2)
                add(t)

        for n in names:
            s[n].base += counts[n]


def rotary(inv, dim, length):
    freqs = np.arange(length, dtype=np.float32)[:, None] * inv.astype(np.float32)[None, :]
    emb = np.concatenate([freqs, freqs], axis=-1)
    return np.cos(emb).T.astype(np.float32), np.sin(emb).T.astype(np.float32)


def llama_inv_freq(theta, factor, high, low, ctx, dim):
    inv = 1.0 / theta ** (np.arange(0, dim, 2, dtype=np.float64) / dim)
    wavelen = 2.0 * np.pi / inv
    smooth = (ctx / wavelen - low) / (high - low)
    scaled = np.where(wavelen > ctx / low, inv / factor, inv)
    mid = (wavelen <= ctx / low) & (wavelen >= ctx / high)
    return np.where(mid, (1 - smooth) * inv / factor + smooth * inv, scaled).astype(np.float32)


def wide_tables(inv, key_scale):
    cos, sin = rotary(inv, HD, SEQ)
    sign = np.where(np.arange(HD) < HD // 2, 1.0, -1.0).astype(np.float32)[:, None]
    ks = (key_scale / np.sqrt(np.float32(HD))).astype(np.float32)[None, :]
    return np.ascontiguousarray(np.stack([cos, sin * sign, cos * ks, sin * sign * ks], axis=1).astype(np.float32))


def constant_arrays():
    pos = np.arange(SEQ)
    key_scale = np.where(pos < SYS_LEN, SUP, np.where(pos < SYS_LEN + IMG_LEN, ENH, 1.0)).astype(np.float32)
    inv1 = 1.0 / np.float32(10000.0) ** (np.arange(0, HD, 2, dtype=np.float32) / np.float32(HD))
    back = 1.0 / key_scale[:P]
    t0s = np.where(np.arange(P)[:, None] >= SYS_LEN + IMG_LEN, 1.0, back[None, :]).astype(np.float32)
    mask = np.where(np.arange(P)[None, :] > np.arange(P)[:, None], MASKED, 0.0).astype(np.float32)
    consts = np.stack([np.eye(P, dtype=np.float32), mask], axis=1)
    a = {
        "consts": consts,
        "L1_tables": wide_tables(inv1, key_scale),
        "L1_t0s": t0s,
        "tri_g": np.tril(np.ones((MGROUPS, MGROUPS), np.float32), -1),
        "tri_e": np.tril(np.ones((EXPERTS, EXPERTS), np.float32), -1),
        "L3_tables": wide_tables(llama_inv_freq(500000.0, 8.0, 4.0, 1.0, 1024, HD), np.ones(SEQ, np.float32)),
    }
    a["L0_kcol"] = (np.arange(P) // 16 + 2).astype(np.float32).reshape(P, 1)
    dh = 16
    inv2 = 1.0 / np.float32(500000.0) ** (np.arange(0, dh, 2, dtype=np.float32) / np.float32(dh))
    inv2 = np.where(2.0 * np.pi / inv2 > 1024.0, inv2 / np.float32(32.0), inv2).astype(np.float32)
    cos, sin = (m.T for m in rotary(inv2, dh, SEQ))
    sin = sin * np.where(np.arange(dh) < dh // 2, -1.0, 1.0).astype(np.float32)
    sc = np.float32(1.0 / np.sqrt(dh))
    tab = np.stack([cos * sc, sin * sc, cos, sin], axis=1).astype(np.float32)
    a["L2_tab"] = tab.reshape(QT, P, 4, dh).transpose(1, 0, 2, 3)
    return a


def by_feature(w):
    return w.reshape(KT, P, -1).transpose(1, 0, 2)


def input_arrays(i):
    a = {"x": i["L0_attn_x"].reshape(TOK, D)}

    def padded(w, rows, cols):
        out = np.zeros((rows, cols), w.dtype)
        out[:w.shape[0], :w.shape[1]] = w
        return out

    def heads(w):
        return w.reshape(KT, P, -1, HD).transpose(2, 1, 0, 3)

    for name, t in (("L1_", True), ("L3_", False)):
        w = {n: (i[f"{name}attn_w{n}"].T if t else i[f"{name}attn_w{n}"]) for n in "qkvo"}
        for n in "qkv":
            a[f"{name}w{n}"] = heads(w[n])
        a[f"{name}wo"] = w["o"].reshape(HEADS, HD, D)

    def slabs(routed, shared):
        return np.concatenate([routed, shared])

    f = {n: i["L1_ffn_" + n] for n in ("router_w", "router_b", "router_bias", "ew1", "eb1", "ew2", "eb2", "ew3", "eb3",
                                       "sw1", "sb1", "sw2", "sb2", "sw3", "sb3")}
    a["router_w"] = by_feature(padded(f["router_w"], D, P))
    a["router_rows"] = np.stack([f["router_b"], f["router_bias"]])
    for n in "12":
        w = slabs(f["ew" + n], f["sw" + n].reshape(D, 2, INTER).transpose(1, 0, 2))
        a["ew" + n] = w.reshape(SLABS, KT, P, INTER).transpose(0, 2, 1, 3)
    a["ew3"] = slabs(f["ew3"], f["sw3"].reshape(2, INTER, D))
    a["eb12"] = np.stack([slabs(f["eb" + n], f["sb" + n].reshape(2, INTER)) for n in "12"], axis=2)
    a["b3"] = np.concatenate([f["eb3"], f["sb3"].reshape(1, D)])

    g = lambda n: i["L0_attn_" + n]
    a["L0_wqkv"] = by_feature(np.concatenate([g("Wqk_w"), g("Wv_w")]).T)
    a["L0_qkvb"] = np.concatenate([g("Wqk_b"), g("Wv_b")])
    a["L0_wo"] = g("Wo_w").T
    a["L0_wf"] = by_feature(i["L0_ffn_weight"].T)
    a["L0_la"] = by_feature(padded(i["L0_ffn_lora_A"].reshape(-1, D).T, D, P))
    lb = i["L0_ffn_lora_B"].transpose(0, 2, 1).reshape(-1, D)
    a["L0_lb"] = np.concatenate([lb, np.zeros((64 - lb.shape[0], D), lb.dtype), i["L0_ffn_bias"].reshape(1, D), g("Wo_b").reshape(1, D)])
    a["L0_starts"] = i["L0_ffn_lora_start_indices"]
    g = lambda n: i["L2_attn_" + n]
    a["L2_wqkv"] = by_feature(np.concatenate([g("Wq"), g("Wk"), g("Wv")]).T)
    a["L2_wo"] = by_feature(g("Wo").T)
    for name in ("L2_", "L3_"):
        g = lambda n: i[name + "ffn_" + n]
        a[name + "m_wq"] = by_feature(padded(g("Wq").T, D, P))
        a[name + "m_wu1"] = by_feature(g("Wu1").T)
        a[name + "m_wr"] = padded(g("Wr").T, BOT, BOT)
        a[name + "m_keysT"] = g("aux_keys").T
        a[name + "m_valsT"] = by_feature(g("aux_values").T)
        a[name + "m_wvd"] = by_feature(g("Wvd").T)
        a[name + "m_wvu"] = g("Wvu").T
        a[name + "m_bu1"] = g("bu1").reshape(P, 1)
        a[name + "m_wu2"] = g("Wu2").reshape(P, 1)
        a[name + "m_log_rel"] = g("log_rel").reshape(1, NSLOT)
        a[name + "m_scal"] = np.concatenate([g("bu2").reshape(1), g("gate_w1").reshape(1), g("gate_bias").reshape(1)])
    return a


def store(k, out):
    nc = k.nc
    with ExitStack() as st:
        y_out = k.sem("y_out")
        block = st.enter_context(nc.Block())

        @block.sync
        def _(sp):
            sp.dma_start(out.rearrange("(t p) n -> p t n", p=P), k.x[:, :, :]).then_inc(y_out.sem, 16)
            sp.wait_ge(y_out.sem, 16)


def program(nc, d, out):
    with ExitStack() as ctx:
        k = make_shared(nc, ctx)
        load_constants(k, d)
        with ExitStack() as st:
            *weights, load = weights0(k, d, st)
            layer_norm(k, 0, False, load)
            narrow_layer0(k, d, *weights)
        with ExitStack() as st:
            tables, t0s, load = rotary_buffers(k, d, "L1_", True, st)
            layer_norm(k, 1, False, load)
            wide_attention(k, d, "L1_", tables, t0s)
        experts(k, d)
        with ExitStack() as st:
            *weights, load = weights2(k, d, st)
            with ExitStack() as st_m:
                memory, load_m = memory_buffers(k, d, "L2_", st_m)
                layer_norm(k, 2, True, load_m)
                memory_ffn(k, d, "L2_", memory, load)
            narrow_attention2(k, d, *weights)
        with ExitStack() as st:
            tables, t0s, load = rotary_buffers(k, d, "L3_", False, st)
            with ExitStack() as st_m:
                memory, load_m = memory_buffers(k, d, "L3_", st_m)
                layer_norm(k, 3, True, load_m)
                memory_ffn(k, d, "L3_", memory, load)
            wide_attention(k, d, "L3_", tables, t0s)
        store(k, out)


def kernel(**inputs):
    import concourse.bacc as bacc
    from concourse.bass_utils import run_bass_kernel_spmd as run

    arrays = {n: np.ascontiguousarray(a) for n, a in {**input_arrays(inputs), **constant_arrays()}.items()}
    nc = bacc.Bacc("TRN2", target_bir_lowering=False, num_devices=1)
    d = {n: nc.dram_tensor("in_" + n, a.shape, mybir.dt.from_np(a.dtype), kind="ExternalInput").ap() for n, a in arrays.items()}
    out = nc.dram_tensor("out_y", (TOK, D), F32, kind="ExternalOutput").ap()
    program(nc, d, out)
    r = run(nc, [{"in_" + n: a for n, a in arrays.items()}], core_ids=[0])
    return r.results[0]["out_y"].reshape(BATCH, SEQ, D)
```
